# Optimizing a Trainium2 kernel written in Bass

```python
import numpy as np
import jax
import jax.numpy as jnp

def _softmax(x, axis=-1):
    return jax.nn.softmax(x, axis=axis)

def _gelu(x):
    return jax.nn.gelu(x, approximate=True)

def _silu(x):
    return jax.nn.silu(x)

def _sigmoid(x):
    return jax.nn.sigmoid(x)

def _layernorm(x, axis=-1, eps=1e-05):
    m = jnp.mean(x, axis=axis, keepdims=True)
    v = jnp.var(x, axis=axis, keepdims=True)
    return (x - m) / jnp.sqrt(v + eps)

def _scatter_add(tgt, idx, src, axis=0):
    return tgt.at[idx].add(src)

def _segment_sum(src, seg, n):
    return jax.ops.segment_sum(src, seg, n)
kernel_name = 'mk_gnn_resnorm_d4_gnn_r32_8f9b25'

def setup_inputs(seed: int=0):
    np.random.seed(seed)
    _w = jnp.asarray

    def _rec_inputs():
        import jax
        import jax.numpy as jnp
        _gk = jax.random.key(seed)
        x = -0.0003713 + 1 * jax.random.normal(jax.random.fold_in(_gk, 1), (50000, 128), jnp.float32)
        src = jax.random.randint(jax.random.fold_in(_gk, 2), (25000,), 0, 50000, jnp.int32)
        dst = jax.random.randint(jax.random.fold_in(_gk, 3), (25000,), 0, 50000, jnp.int32)
        _o = jnp.argsort(dst, stable=True)
        src = src[_o]
        dst = dst[_o]
        edge_attr_16 = 0.000398945 + 1.00003 * jax.random.normal(jax.random.fold_in(_gk, 12), (25000, 16), jnp.float32)
        return (x, src, dst, edge_attr_16)
    x, src, dst, edge_attr_16 = _rec_inputs()

    def _L0_gnn_setup():
        import jax, jax.numpy as jnp
        import numpy as np
        N_NODES = 3125
        N_EDGES = 18750
        IN_FEATS = 128
        OUT_FEATS = 128
        key = jax.random.key(seed)
        k1, k2, k3, k4 = jax.random.split(key, 4)
        feat = jax.random.normal(k1, (N_NODES, IN_FEATS), dtype=jnp.float32)
        W_neigh = jax.random.normal(k2, (2 * IN_FEATS, OUT_FEATS), dtype=jnp.float32) / np.sqrt(2 * IN_FEATS)
        b_neigh = jnp.zeros((OUT_FEATS,), dtype=jnp.float32)
        src = jax.random.randint(k3, (N_EDGES,), 0, N_NODES, dtype=jnp.int32)
        dst = jax.random.randint(k4, (N_EDGES,), 0, N_NODES, dtype=jnp.int32)
        return {'feat': feat, 'W_neigh': W_neigh, 'b_neigh': b_neigh, 'src': src, 'dst': dst}
    _L0_gnn_all = _L0_gnn_setup()
    _L0_gnn_in = {k: v for k, v in _L0_gnn_all.items() if k in ('W_neigh', 'b_neigh')}
    del _L0_gnn_all

    def _L1_gnn_setup():
        import jax, jax.numpy as jnp
        import numpy as np
        ALPHA = 0.1
        THETA = 0.5

        def _gcn_norm(edge_index, num_nodes):
            loop = jnp.arange(num_nodes, dtype=edge_index.dtype)
            row = jnp.concatenate([edge_index[0], loop])
            col = jnp.concatenate([edge_index[1], loop])
            ones = jnp.ones(row.shape[0], dtype=jnp.float32)
            deg = jax.ops.segment_sum(ones, col, num_segments=num_nodes)
            dis = jnp.where(deg > 0, jax.lax.rsqrt(deg), 0.0)
            norm = dis[row] * dis[col]
            return (row, col, norm)

        def _gcn2_layer(x, W, beta, row, col, norm, num_nodes):
            h = jax.ops.segment_sum(norm[:, None] * x[col], row, num_segments=num_nodes)
            xp = (1.0 - ALPHA) * h + ALPHA * x
            return (1.0 - beta) * xp + beta * (xp @ W)
        key = jax.random.key(seed)
        k1, k2, k3, k4 = jax.random.split(key, 4)
        N, E, C = (1250, 20000, 128)
        x = jax.random.normal(k1, (N, C), dtype=jnp.float32)
        edge_index = jax.random.randint(k2, (2, E), 0, N, dtype=jnp.int64)
        s = 1.0 / np.sqrt(C)
        W1 = jax.random.normal(k3, (C, C), dtype=jnp.float32) * s
        W2 = jax.random.normal(k4, (C, C), dtype=jnp.float32) * s
        return {'x': x, 'edge_index': edge_index, 'W1': W1, 'W2': W2}
    _L1_gnn_all = _L1_gnn_setup()
    _L1_gnn_in = {k: v for k, v in _L1_gnn_all.items() if k in ('W1', 'W2')}
    del _L1_gnn_all

    def _L2_gnn_setup():
        import jax, jax.numpy as jnp
        import numpy as np
        N, E, D, H, ED = (50000, 12500, 128, 4, 16)
        NEG_SLOPE = 0.2
        LN_EPS = 1e-05

        def _layernorm(x, g, b):
            mu = jnp.mean(x, axis=-1, keepdims=True)
            var = jnp.mean((x - mu) ** 2, axis=-1, keepdims=True)
            return (x - mu) * jax.lax.rsqrt(var + LN_EPS) * g + b

        def _gatv2(x, edge_index, edge_attr, Wl, bl, Wr, br, We, att, conv_bias):
            n = x.shape[0]
            src, dst = (edge_index[0], edge_index[1])
            xl = (x @ Wl.T + bl).reshape(n, H, D)
            xr = (x @ Wr.T + br).reshape(n, H, D)
            e = (edge_attr @ We.T).reshape(-1, H, D)
            z = jax.nn.leaky_relu(xl[src] + xr[dst] + e, NEG_SLOPE)
            logit = jnp.einsum('ehd,hd->eh', z, att)
            m = jax.ops.segment_max(logit, dst, num_segments=n)
            ex = jnp.exp(logit - m[dst])
            den = jax.ops.segment_sum(ex, dst, num_segments=n)
            alpha = ex / (den[dst] + 1e-16)
            agg = jax.ops.segment_sum(xl[src] * alpha[:, :, None], dst, num_segments=n)
            return agg.mean(axis=1) + conv_bias
        key = jax.random.key(seed)
        ks = jax.random.split(key, 12)
        s = 0.05
        f32 = jnp.float32
        return {'x': jax.random.normal(ks[0], (N, D), f32), 'edge_index': jax.random.randint(ks[1], (2, E), 0, N, jnp.int32), 'edge_attr': jax.random.normal(ks[2], (E, ED), f32), 'Wl': jax.random.normal(ks[3], (H * D, D), f32) * s, 'bl': jnp.zeros((H * D,), f32), 'Wr': jax.random.normal(ks[4], (H * D, D), f32) * s, 'br': jnp.zeros((H * D,), f32), 'We': jax.random.normal(ks[5], (H * D, ED), f32) * s, 'att': jax.random.normal(ks[6], (H, D), f32) * s, 'conv_bias': jnp.zeros((D,), f32), 'g1': jnp.ones((D,), f32), 'beta1': jnp.zeros((D,), f32), 'W1': jax.random.normal(ks[7], (2 * D, D), f32) * s, 'b1': jnp.zeros((2 * D,), f32), 'W2': jax.random.normal(ks[8], (D, 2 * D), f32) * s, 'b2': jnp.zeros((D,), f32), 'g2': jnp.ones((D,), f32), 'beta2': jnp.zeros((D,), f32)}
    _L2_gnn_all = _L2_gnn_setup()
    _L2_gnn_in = {k: v for k, v in _L2_gnn_all.items() if k in ('Wl', 'bl', 'Wr', 'br', 'We', 'att', 'conv_bias', 'g1', 'beta1', 'W1', 'b1', 'W2', 'b2', 'g2', 'beta2')}
    del _L2_gnn_all

    def _L3_gnn_setup():
        import jax, jax.numpy as jnp
        import numpy as np
        N, E, F_IN, H, C = (50000, 25000, 128, 2, 64)
        NEG_SLOPE = 0.2

        def gat_conv(x, W, att_src, att_dst, b, src, dst):
            n = x.shape[0]
            h = (x @ W).reshape(n, H, C)
            loops = jnp.arange(n, dtype=src.dtype)
            s = jnp.concatenate([src, loops])
            d = jnp.concatenate([dst, loops])
            a_s = jnp.einsum('nhc,hc->nh', h, att_src)
            a_d = jnp.einsum('nhc,hc->nh', h, att_dst)
            e = jax.nn.leaky_relu(a_s[s] + a_d[d], NEG_SLOPE)
            m = jax.ops.segment_max(e, d, num_segments=n)
            p = jnp.exp(e - m[d])
            denom = jax.ops.segment_sum(p, d, num_segments=n)
            alpha = p / (denom[d] + 1e-16)
            out = jax.ops.segment_sum(h[s] * alpha[:, :, None], d, num_segments=n)
            return out.reshape(n, H * C) + b
        key = jax.random.key(seed)
        ks = jax.random.split(key, 16)
        rn = lambda k, shape, s=0.1: jax.random.normal(k, shape, jnp.float32) * s
        return {'x': jax.random.normal(ks[0], (N, F_IN), jnp.float32), 'src': jax.random.randint(ks[1], (E,), 0, N, jnp.int32), 'dst': jax.random.randint(ks[2], (E,), 0, N, jnp.int32), 'W1': rn(ks[3], (F_IN, H * C)), 'att_src1': rn(ks[4], (H, C)), 'att_dst1': rn(ks[5], (H, C)), 'b1': rn(ks[6], (H * C,)), 'Wsk1': rn(ks[7], (F_IN, H * C)), 'bsk1': rn(ks[8], (H * C,)), 'W2': rn(ks[9], (H * C, H * C)), 'att_src2': rn(ks[10], (H, C)), 'att_dst2': rn(ks[11], (H, C)), 'b2': rn(ks[12], (H * C,)), 'Wsk2': rn(ks[13], (H * C, H * C)), 'bsk2': rn(ks[14], (H * C,))}
    _L3_gnn_all = _L3_gnn_setup()
    _L3_gnn_in = {k: v for k, v in _L3_gnn_all.items() if k in ('W1', 'att_src1', 'att_dst1', 'b1', 'Wsk1', 'bsk1', 'W2', 'att_src2', 'att_dst2', 'b2', 'Wsk2', 'bsk2')}
    del _L3_gnn_all
    return {'x': x, 'src': src, 'dst': dst, 'edge_attr_16': edge_attr_16, 'L0_gnn_W_neigh': _L0_gnn_in['W_neigh'], 'L0_gnn_b_neigh': _L0_gnn_in['b_neigh'], 'L1_gnn_W1': _L1_gnn_in['W1'], 'L1_gnn_W2': _L1_gnn_in['W2'], 'L2_gnn_Wl': _L2_gnn_in['Wl'], 'L2_gnn_bl': _L2_gnn_in['bl'], 'L2_gnn_Wr': _L2_gnn_in['Wr'], 'L2_gnn_br': _L2_gnn_in['br'], 'L2_gnn_We': _L2_gnn_in['We'], 'L2_gnn_att': _L2_gnn_in['att'], 'L2_gnn_conv_bias': _L2_gnn_in['conv_bias'], 'L2_gnn_g1': _L2_gnn_in['g1'], 'L2_gnn_beta1': _L2_gnn_in['beta1'], 'L2_gnn_W1': _L2_gnn_in['W1'], 'L2_gnn_b1': _L2_gnn_in['b1'], 'L2_gnn_W2': _L2_gnn_in['W2'], 'L2_gnn_b2': _L2_gnn_in['b2'], 'L2_gnn_g2': _L2_gnn_in['g2'], 'L2_gnn_beta2': _L2_gnn_in['beta2'], 'L3_gnn_W1': _L3_gnn_in['W1'], 'L3_gnn_att_src1': _L3_gnn_in['att_src1'], 'L3_gnn_att_dst1': _L3_gnn_in['att_dst1'], 'L3_gnn_b1': _L3_gnn_in['b1'], 'L3_gnn_Wsk1': _L3_gnn_in['Wsk1'], 'L3_gnn_bsk1': _L3_gnn_in['bsk1'], 'L3_gnn_W2': _L3_gnn_in['W2'], 'L3_gnn_att_src2': _L3_gnn_in['att_src2'], 'L3_gnn_att_dst2': _L3_gnn_in['att_dst2'], 'L3_gnn_b2': _L3_gnn_in['b2'], 'L3_gnn_Wsk2': _L3_gnn_in['Wsk2'], 'L3_gnn_bsk2': _L3_gnn_in['bsk2']}

def reference(x, src, dst, edge_attr_16, L0_gnn_W_neigh, L0_gnn_b_neigh, L1_gnn_W1, L1_gnn_W2, L2_gnn_Wl, L2_gnn_bl, L2_gnn_Wr, L2_gnn_br, L2_gnn_We, L2_gnn_att, L2_gnn_conv_bias, L2_gnn_g1, L2_gnn_beta1, L2_gnn_W1, L2_gnn_b1, L2_gnn_W2, L2_gnn_b2, L2_gnn_g2, L2_gnn_beta2, L3_gnn_W1, L3_gnn_att_src1, L3_gnn_att_dst1, L3_gnn_b1, L3_gnn_Wsk1, L3_gnn_bsk1, L3_gnn_W2, L3_gnn_att_src2, L3_gnn_att_dst2, L3_gnn_b2, L3_gnn_Wsk2, L3_gnn_bsk2):
    import jax
    import jax.numpy as jnp

    def _L0_gnn_ref(feat, W_neigh, b_neigh, src, dst):
        import jax, jax.numpy as jnp
        import numpy as np
        N_NODES = 3125
        N_EDGES = 18750
        IN_FEATS = 128
        OUT_FEATS = 128
        N = feat.shape[0]
        msgs = feat[src]
        neigh_sum = jax.ops.segment_sum(msgs, dst, num_segments=N)
        deg = jax.ops.segment_sum(jnp.ones(src.shape[0], feat.dtype), dst, num_segments=N)
        h_neigh = neigh_sum / jnp.maximum(deg, 1.0)[:, None]
        h = jnp.concatenate([feat, h_neigh], axis=1)
        return h @ W_neigh + b_neigh

    def _L1_gnn_ref(x, edge_index, W1, W2):
        import jax, jax.numpy as jnp
        import numpy as np
        ALPHA = 0.1
        THETA = 0.5

        def _gcn_norm(edge_index, num_nodes):
            loop = jnp.arange(num_nodes, dtype=edge_index.dtype)
            row = jnp.concatenate([edge_index[0], loop])
            col = jnp.concatenate([edge_index[1], loop])
            ones = jnp.ones(row.shape[0], dtype=jnp.float32)
            deg = jax.ops.segment_sum(ones, col, num_segments=num_nodes)
            dis = jnp.where(deg > 0, jax.lax.rsqrt(deg), 0.0)
            norm = dis[row] * dis[col]
            return (row, col, norm)

        def _gcn2_layer(x, W, beta, row, col, norm, num_nodes):
            h = jax.ops.segment_sum(norm[:, None] * x[col], row, num_segments=num_nodes)
            xp = (1.0 - ALPHA) * h + ALPHA * x
            return (1.0 - beta) * xp + beta * (xp @ W)
        N = x.shape[0]
        row, col, norm = _gcn_norm(edge_index, N)
        beta1 = jnp.log(THETA / 1.0 + 1.0).astype(x.dtype)
        beta2 = jnp.log(THETA / 2.0 + 1.0).astype(x.dtype)
        x = _gcn2_layer(x, W1, beta1, row, col, norm, N)
        x = _gcn2_layer(x, W2, beta2, row, col, norm, N)
        return x

    def _L2_gnn_ref(x, edge_index, edge_attr, Wl, bl, Wr, br, We, att, conv_bias, g1, beta1, W1, b1, W2, b2, g2, beta2):
        import jax, jax.numpy as jnp
        import numpy as np
        N, E, D, H, ED = (50000, 12500, 128, 4, 16)
        NEG_SLOPE = 0.2
        LN_EPS = 1e-05

        def _layernorm(x, g, b):
            mu = jnp.mean(x, axis=-1, keepdims=True)
            var = jnp.mean((x - mu) ** 2, axis=-1, keepdims=True)
            return (x - mu) * jax.lax.rsqrt(var + LN_EPS) * g + b

        def _gatv2(x, edge_index, edge_attr, Wl, bl, Wr, br, We, att, conv_bias):
            n = x.shape[0]
            src, dst = (edge_index[0], edge_index[1])
            xl = (x @ Wl.T + bl).reshape(n, H, D)
            xr = (x @ Wr.T + br).reshape(n, H, D)
            e = (edge_attr @ We.T).reshape(-1, H, D)
            z = jax.nn.leaky_relu(xl[src] + xr[dst] + e, NEG_SLOPE)
            logit = jnp.einsum('ehd,hd->eh', z, att)
            m = jax.ops.segment_max(logit, dst, num_segments=n)
            ex = jnp.exp(logit - m[dst])
            den = jax.ops.segment_sum(ex, dst, num_segments=n)
            alpha = ex / (den[dst] + 1e-16)
            agg = jax.ops.segment_sum(xl[src] * alpha[:, :, None], dst, num_segments=n)
            return agg.mean(axis=1) + conv_bias
        h = _gatv2(x, edge_index, edge_attr, Wl, bl, Wr, br, We, att, conv_bias)
        x1 = _layernorm(x + h, g1, beta1)
        f = jax.nn.gelu(x1 @ W1.T + b1, approximate=False) @ W2.T + b2
        return _layernorm(x1 + f, g2, beta2)

    def _L3_gnn_ref(x, W1, att_src1, att_dst1, b1, Wsk1, bsk1, W2, att_src2, att_dst2, b2, Wsk2, bsk2, src, dst):
        import jax, jax.numpy as jnp
        import numpy as np
        N, E, F_IN, H, C = (50000, 25000, 128, 2, 64)
        NEG_SLOPE = 0.2

        def gat_conv(x, W, att_src, att_dst, b, src, dst):
            n = x.shape[0]
            h = (x @ W).reshape(n, H, C)
            loops = jnp.arange(n, dtype=src.dtype)
            s = jnp.concatenate([src, loops])
            d = jnp.concatenate([dst, loops])
            a_s = jnp.einsum('nhc,hc->nh', h, att_src)
            a_d = jnp.einsum('nhc,hc->nh', h, att_dst)
            e = jax.nn.leaky_relu(a_s[s] + a_d[d], NEG_SLOPE)
            m = jax.ops.segment_max(e, d, num_segments=n)
            p = jnp.exp(e - m[d])
            denom = jax.ops.segment_sum(p, d, num_segments=n)
            alpha = p / (denom[d] + 1e-16)
            out = jax.ops.segment_sum(h[s] * alpha[:, :, None], d, num_segments=n)
            return out.reshape(n, H * C) + b
        h = gat_conv(x, W1, att_src1, att_dst1, b1, src, dst) + x @ Wsk1 + bsk1
        h = jax.nn.relu(h)
        out = gat_conv(h, W2, att_src2, att_dst2, b2, src, dst) + h @ Wsk2 + bsk2
        return out
    edge_index = jnp.stack([src, dst])
    x = _layernorm(x + _L0_gnn_ref(x, L0_gnn_W_neigh, L0_gnn_b_neigh, src, dst), axis=-1)
    x = _layernorm(x + _L1_gnn_ref(x, edge_index, L1_gnn_W1, L1_gnn_W2), axis=-1)
    x = _layernorm(x + _L2_gnn_ref(x, edge_index, edge_attr_16, L2_gnn_Wl, L2_gnn_bl, L2_gnn_Wr, L2_gnn_br, L2_gnn_We, L2_gnn_att, L2_gnn_conv_bias, L2_gnn_g1, L2_gnn_beta1, L2_gnn_W1, L2_gnn_b1, L2_gnn_W2, L2_gnn_b2, L2_gnn_g2, L2_gnn_beta2), axis=-1)
    x = _layernorm(x + _L3_gnn_ref(x, L3_gnn_W1, L3_gnn_att_src1, L3_gnn_att_dst1, L3_gnn_b1, L3_gnn_Wsk1, L3_gnn_bsk1, L3_gnn_W2, L3_gnn_att_src2, L3_gnn_att_dst2, L3_gnn_b2, L3_gnn_Wsk2, L3_gnn_bsk2, src, dst), axis=-1)
    return x

_drawn_inputs = setup_inputs


def setup_inputs(seed=0):
    import zlib

    import numpy as np

    out = dict(_drawn_inputs(seed))
    spreads = {'L0_gnn_b_neigh': (0.0, 0.1),
     'L2_gnn_bl': (0.0, 0.523),
     'L2_gnn_br': (0.0, 0.8),
     'L2_gnn_conv_bias': (0.0, 0.1),
     'L2_gnn_g1': (1.0, 0.2),
     'L2_gnn_beta1': (0.0, 0.1),
     'L2_gnn_b1': (0.0, 0.31),
     'L2_gnn_b2': (0.0, 0.1),
     'L2_gnn_g2': (1.0, 0.2),
     'L2_gnn_beta2': (0.0, 0.1)}
    factors = {'edge_attr_16': 8.0,
     'L2_gnn_Wr': 8.0,
     'L2_gnn_We': 8.0,
     'L2_gnn_att': 8.0,
     'L3_gnn_att_dst2': 2.909}
    for name, (base, spread) in spreads.items():
        noise = np.random.default_rng([zlib.crc32(name.encode()), seed]).standard_normal(out[name].shape)
        drawn = base * np.exp(spread * noise) if base else spread * noise
        out[name] = jnp.asarray(drawn.astype(out[name].dtype))
    for name, factor in factors.items():
        out[name] = (out[name] * factor).astype(out[name].dtype)
    return out
```

```python
from contextlib import ExitStack
import numpy as np
import concourse.bass as bass
from concourse import mybir

F32, I32, F16, BF16 = mybir.dt.float32, mybir.dt.int32, mybir.dt.float16, mybir.dt.bfloat16
ALU, ACT, AX = mybir.AluOpType, mybir.ActivationFunctionType, mybir.AxisListType

P = 128
D = 128
NODES, EDGES = 50000, 25000
GB = 4
BLOCK = P * GB
SLOT = 4
NB = SLOT * -(-NODES // (SLOT * BLOCK))
NPAD = NB * BLOCK
GC, SLOTS = 7, 4
TURN = GC * SLOTS
J = TURN * -(-EDGES // (P * TURN))
EPAD = P * J
TURNS = J // TURN
ROW = D + 4
HEADS, HD = 4, 4 * D
ATT_IN = 16
WD = 3 + ATT_IN
WS = 2
LOW = 256
HIGH = NPAD // LOW
BIG = 1.0e30
GCN_BETA = (float(np.log(np.float32(1.5))), float(np.log(np.float32(1.25))))
FAR = 65536.0
assert NPAD % LOW == 0 and HIGH <= LOW and J % TURN == 0


class Phase:

    def __init__(self, nc, name):
        self.nc, self.name, self.stack, self.sems = nc, name, ExitStack(), []

    def sb(self, name, shape, dt=F32):
        return self.stack.enter_context(self.nc.sbuf_tensor(f"{self.name}_{name}", shape, dt))

    def ps(self, name, shape, dt=F32):
        return self.stack.enter_context(self.nc.psum_tensor(f"{self.name}_{name}", shape, dt))

    def sem(self, name):
        s = self.nc.alloc_semaphore(f"{self.name}_{name}")
        self.sems.append(s)
        return s

    def __enter__(self):
        return self

    def __exit__(self, *e):
        if e[0] is None:
            self.nc.clear_and_free_semaphores(self.sems)
            self.nc.all_engine_barrier()
        self.stack.close()


class Keep:
    pass


def constants(nc, keep, stack):
    def sb(name, shape, dt=F32):
        return stack.enter_context(nc.sbuf_tensor(name, shape, dt))

    keep.ident, keep.ones = sb("ident", [P, P]), sb("ones", [P, P])
    keep.ident_h, keep.ones_h = sb("ident_h", [P, P], F16), sb("ones_h", [P, P], F16)
    keep.tri_h, keep.iota_h = sb("tri_h", [P, P], F16), sb("iota_h", [P, LOW], F16)
    keep.ones_b = sb("ones_b", [P, P], BF16)
    keep.eps, keep.minus_half = sb("eps", [P, GB]), sb("minus_half", [P, GB])
    with Phase(nc, "const") as ph:
        iota_i, filled, iota_done = ph.sb("iota_i", [P, LOW], I32), ph.sem("filled"), ph.sem("iota_done")
        shaped = ph.sem("shaped")
        with nc.Block() as block:
            @block.gpsimd
            def _(pool):
                pool.memset(keep.ident[:, :], 0.0).then_inc(filled, 1)
                pool.memset(keep.ones[:, :], 1.0).then_inc(filled, 1)
                pool.memset(keep.ones_h[:, :], 1.0).then_inc(filled, 1)
                pool.iota(iota_i[:, :], [[1, LOW]], base=0, channel_multiplier=0).then_inc(iota_done, 1)
                pool.wait_ge(filled, 3)
                pool.affine_select(out=keep.ident[:, :], in_=keep.ident[:, :], compare_op=ALU.not_equal, fill=1.0,
                                   base=0, pattern=[[-1, P]], channel_multiplier=1).then_inc(shaped, 1)
                pool.affine_select(out=keep.tri_h[:, :], in_=keep.ones_h[:, :], compare_op=ALU.is_gt, fill=0.0,
                                   base=0, pattern=[[1, P]], channel_multiplier=-1).then_inc(shaped, 1)

            @block.vector
            def _(dve):
                dve.memset(keep.eps[:, :], LN_EPS)
                dve.memset(keep.minus_half[:, :], -0.5)
                dve.memset(keep.ones_b[:, :], 1.0)
                dve.wait_ge(iota_done, 1)
                dve.tensor_copy(keep.iota_h[:, :], iota_i[:, :])
                dve.wait_ge(shaped, 1)
                dve.tensor_copy(keep.ident_h[:, :], keep.ident[:, :])


def sort_pass(nc, keep, name, words, digits, high, load, target, zero_fill=None):
    with Phase(nc, name) as ph:
        pay = ph.sb("pay", [P, J, words])
        dig = ph.sb("dig", [P, J])
        key_i = ph.sb("key_i", [P, J], I32)
        onehot = ph.sb("onehot", [P, SLOTS, GC, digits], F16)
        digs = ph.sb("digs", [P, SLOTS, GC])
        place = ph.sb("place", [P, SLOTS, GC])
        place_i = ph.sb("place_i", [P, SLOTS, GC], I32)
        pay_s = ph.sb("pay_s", [P, SLOTS, GC, words])
        junk = ph.sb("junk", [P, 4, digits])
        hist = ph.sb("hist", [P, digits], F16)
        zero_h = ph.sb("zero_h", [P, P], F16)
        one_row = ph.sb("one_row", [P, digits])
        upto = ph.sb("upto", [P, digits])
        base = ph.sb("base", [P, digits])
        hist_ps = ph.ps("hist_ps", [P, 512])
        total_ps = ph.ps("total_ps", [P, 512])
        before_ps = ph.ps("before_ps", [P, 512])
        run_ps = [ph.ps(f"run_ps{q}", [P, 512]) for q in range(4)]
        loaded, digit_ready = ph.sem("loaded"), ph.sem("digit_ready")
        prepared, chain = ph.sem("prepared"), ph.sem("chain")
        digs_ready, hot_ready, hot_used = ph.sem("digs_ready"), ph.sem("hot_ready"), ph.sem("hot_used")
        hist_done, hist_read = ph.sem("hist_done"), ph.sem("hist_read")
        sums_done, base_ready = ph.sem("sums_done"), ph.sem("base_ready")
        digs2_ready, hot2_ready = ph.sem("digs2_ready"), ph.sem("hot2_ready")
        run_ready, ranked = ph.sem("run_ready"), ph.sem("ranked")
        placed, go = ph.sem("placed"), ph.sem("go")
        scattered = [ph.sem(f"scattered{s}") for s in range(SLOTS)]
        zeroed, zero_ready = ph.sem("zeroed"), ph.sem("zero_ready")
        n_zero = 0
        if zero_fill:
            zeros = ph.sb("zeros", [P, 8 * ROW])
        with nc.Block() as block:
            n_loads = load(block, ph, pay, loaded, prepared)

            @block.scalar
            def _(act):
                n = 0
                if zero_fill:
                    act.wait_ge(zero_ready, 1)
                    for a in zero_fill:
                        flat = a.rearrange("(p n) d -> p (n d)", p=P)
                        step = 8 * a.shape[1]
                        for k in range(0, flat.shape[1], step):
                            act.dma_start(flat[:, k:k + step], zeros[:, 0:step]).then_inc(zeroed, 16)
                            n += 16
                    act.wait_ge(zeroed, n)

            @block.vector
            def _(dve):
                if zero_fill:
                    dve.memset(zeros[:, :], 0.0).then_inc(zero_ready, 1)
                dve.memset(zero_h[:, :], 0.0)
                dve.memset(one_row[:, :], 1.0)
                dve.sem_inc(hot_used, SLOTS)
                dve.sem_inc(ranked, 4)
                dve.memset(onehot[:, :], 0.0).then_inc(digit_ready, 1)
                dve.wait_ge(loaded, n_loads)
                dve.wait_ge(digit_ready, 1)
                dve.tensor_copy(key_i[:, :], pay[:, :, 0]).then_inc(chain, 1)
                dve.wait_ge(chain, 1)
                op, by = (ALU.logical_shift_right, LOW.bit_length() - 1) if high else (ALU.bitwise_and, LOW - 1)
                dve.tensor_scalar(key_i[:, :], key_i[:, :], by, None, op).then_inc(chain, 1)
                dve.wait_ge(chain, 2)
                dve.tensor_copy(dig[:, :], key_i[:, :]).then_inc(chain, 1)
                dve.wait_ge(chain, 3)

                def hot(turn, s, copied, made):
                    dve.tensor_copy(digs[:, s, :], dig[:, bass.ds(turn * TURN + s * GC, GC)]).then_inc(copied, 1)
                    dve.wait_ge(copied, turn * SLOTS + s + 1)
                    for k in range(GC):
                        ins = dve.tensor_scalar(onehot[:, s, k, :], keep.iota_h[:, 0:digits], digs[:, s, k:k + 1],
                                                None, ALU.is_equal)
                    ins.then_inc(made, 1)

                with dve.Fori(0, TURNS) as turn:
                    for s in range(SLOTS):
                        dve.wait_ge(hot_used, turn * SLOTS + s + 1)
                        hot(turn, s, digs_ready, hot_ready)
                dve.wait_ge(hist_done, 1)
                dve.tensor_copy(hist[:, :], hist_ps[:, 0:digits]).then_inc(hist_read, 1)
                dve.memset(onehot[:, SLOTS - 1, :, :], 0.0).then_inc(chain, 1)
                dve.wait_ge(sums_done, 1)
                dve.tensor_tensor_scan(upto[:, :], one_row[:, :], total_ps[:, 0:digits], 0.0, ALU.mult, ALU.add).then_inc(chain, 1)
                dve.wait_ge(chain, 5)
                dve.tensor_tensor(base[:, :], upto[:, :], total_ps[:, 0:digits], ALU.subtract).then_inc(chain, 1)
                dve.wait_ge(chain, 6)
                dve.tensor_tensor(base[:, :], base[:, :], before_ps[:, 0:digits], ALU.add).then_inc(base_ready, 1)
                with dve.Fori(0, TURNS) as turn:
                    for s in range(SLOTS):
                        hot(turn, s, digs2_ready, hot2_ready)
                        dve.wait_ge(hot2_ready, turn * SLOTS + s + 1)
                        for k in range(GC):
                            c = s * GC + k
                            dve.wait_ge(run_ready, turn * TURN + c + 1)
                            dve.tensor_tensor_reduce(junk[:, c % 4, :], onehot[:, s, k, :], run_ps[c % 4][:, 0:digits],
                                                     1.0, 0.0, ALU.mult, ALU.add, place[:, s, k:k + 1]).then_inc(ranked, 1)
                        dve.wait_ge(scattered[s], turn * (16 * GC))
                        dve.wait_ge(ranked, turn * TURN + (s + 1) * GC + 4)
                        dve.tensor_copy(place_i[:, s, :], place[:, s, :]).then_inc(placed, 1)
                        dve.tensor_copy(pay_s[:, s, :, :], pay[:, bass.ds(turn * TURN + s * GC, GC), :]).then_inc(placed, 1)

            @block.tensor
            def _(pe):
                pe.wait_ge(digit_ready, 1)
                pe.matmul(hist_ps[:, 0:digits], zero_h[:, :], keep.iota_h[:, 0:digits], start=True, stop=False,
                          skip_group_check=True)
                with pe.Fori(0, TURNS) as turn:
                    for s in range(SLOTS):
                        pe.wait_ge(hot_ready, turn * SLOTS + s + 1)
                        for k in range(GC):
                            ins = pe.matmul(hist_ps[:, 0:digits], keep.ident_h[:, :], onehot[:, s, k, :],
                                            start=False, stop=False, skip_group_check=True)
                        ins.then_inc(hot_used, 1)
                pe.matmul(hist_ps[:, 0:digits], zero_h[:, :], keep.iota_h[:, 0:digits], start=False, stop=True,
                          skip_group_check=True).then_inc(hist_done, 1)
                pe.wait_ge(hist_read, 1)
                pe.matmul(total_ps[:, 0:digits], keep.ones_h[:, :], hist[:, :], start=True, stop=True)
                pe.matmul(before_ps[:, 0:digits], keep.tri_h[:, :], hist[:, :], start=True, stop=True).then_inc(sums_done, 1)
                pe.wait_ge(base_ready, 1)
                for q in range(4):
                    pe.matmul(run_ps[q][:, 0:digits], keep.ident[:, :], base[:, :], start=True, stop=False,
                              skip_group_check=True)
                with pe.Fori(0, TURNS) as turn:
                    for c in range(TURN):
                        if c % GC == 1:
                            pe.wait_ge(hot2_ready, turn * SLOTS + c // GC + 1)
                        pe.wait_ge(ranked, turn * TURN + c + 1)
                        for b in range(c - 4, c):
                            b = b % TURN
                            ins = pe.matmul(run_ps[c % 4][:, 0:digits], keep.ident_h[:, :], onehot[:, b // GC, b % GC, :],
                                            start=False, stop=False, skip_group_check=True)
                        ins.then_inc(run_ready, 1)

            @block.gpsimd
            def _(pool):
                with pool.Fori(0, TURNS) as turn:
                    for s in range(SLOTS):
                        pool.wait_ge(placed, turn * (2 * SLOTS) + 2 * s + 2)
                        pool.sem_inc(go, 1)
                        for k in range(GC):
                            pool.indirect_dma_start(
                                out=target, out_offset=bass.IndirectOffsetOnAxis(ap=place_i[:, s, k:k + 1], axis=0),
                                in_=pay_s[:, s, k, :], in_offset=None).then_inc(scattered[s], 16)
                for s in range(SLOTS):
                    pool.wait_ge(scattered[s], TURNS * 16 * GC)


def load_edges(nc, src, dst, attr):
    def load(block, ph, pay, loaded, prepared):
        ends = ph.sb("ends", [P, 2, J], I32)
        ends_in = ph.sem("ends_in")
        n = 16 if attr is not None else 0

        @block.sync
        def _(sp):
            keys = (dst, src) if attr is not None else (src, dst)
            for i, a in enumerate(keys):
                sp.dma_start(ends[:, i, :], a.rearrange("(p j) -> p j", p=P)).then_inc(ends_in, 16)
            if attr is not None:
                sp.wait_ge(prepared, 1)
                sp.dma_start(pay[:, :, 2:2 + ATT_IN], attr.rearrange("(p j) a -> p j a", p=P)).then_inc(loaded, 16)

        @block.gpsimd
        def _(pool):
            if attr is not None:
                pool.memset(pay[:, :, :], 1.0).then_inc(prepared, 1)
                pool.wait_ge(prepared, 1)
            pool.wait_ge(ends_in, 32)
            pool.tensor_copy(pay[:, :, 0], ends[:, 0, :]).then_inc(loaded, 1)
            pool.tensor_copy(pay[:, :, 1], ends[:, 1, :]).then_inc(loaded, 1)
        return n + 2
    return load


def load_sorted(rows):
    def load(block, ph, pay, loaded, prepared):
        @block.sync
        def _(sp):
            sp.dma_start(pay[:, :, :], rows.rearrange("(p j) w -> p j w", p=P)).then_inc(loaded, 16)
        return 16
    return load


def linked(engine, sem):
    n = [0]

    def link(ins):
        n[0] += 1
        ins.then_inc(sem, 1)
        engine.wait_ge(sem, n[0])
    return link


class Edges:
    pass


def edge_tables(nc, keep, name, rows, words, stack, full):
    e = Edges()

    def sb(n, shape, dt=F32):
        return stack.enter_context(nc.sbuf_tensor(f"{name}_{n}", shape, dt))

    e.other_i = sb("other_i", [P, J], I32)
    e.put_i = sb("put_i", [P, J], I32)
    e.fix_i = sb("fix_i", [P, 1], I32)
    e.cont = sb("cont", [P, J])
    e.carry = sb("carry", [P, P])
    if full:
        e.key_i = sb("key_i", [P, J], I32)
        e.att = sb("att", [P, J, ATT_IN + 1])
        e.cont_h = sb("cont_h", [P, HEADS, J])
        e.reset_h = sb("reset_h", [P, HEADS, J])
        e.end_h = sb("end_h", [P, HEADS, J])
        e.next_h = sb("next_h", [P, HEADS, J])
        e.same = [sb(f"same{t}", [P, 2, P]) for t in range(2)]
        e.same_add = [sb(f"same_add{t}", [P, 2, P]) for t in range(2)]
        e.in_add = [sb(f"in_add{t}", [P, J]) for t in range(2)]
        e.split = sb("split", [P, 1])
        e.deg, e.rdeg = sb("deg", [P, J]), sb("rdeg", [P, J])
    with Phase(nc, name + "t") as ph:
        key, other = ph.sb("key", [P, J]), ph.sb("other", [P, J])
        after, before = ph.sb("after", [P, 1]), ph.sb("before", [P, 1])
        tmp, end = ph.sb("tmp", [P, J]), ph.sb("end", [P, J])
        diag, off = ph.sb("diag", [P, 2, P]), ph.sb("off", [P, P])
        goes_on, whole, owns = ph.sb("goes_on", [P, 1]), ph.sb("whole", [P, 1]), ph.sb("owns", [P, 1])
        fix = ph.sb("fix", [P, 1])
        spread = ph.ps("spread", [P, 2, P])
        loaded, chain, preset = ph.sem("loaded"), ph.sem("chain"), ph.sem("preset")
        diag_ready, spread_done = ph.sem("diag_ready"), ph.sem("spread_done")
        view = rows.rearrange("(p j) w -> p j w", p=P)
        with nc.Block() as block, nc.allow_non_contiguous_dma(reason="one word of an edge's payload"):
            @block.sync
            def _(sp):
                sp.dma_start(key[:, :], view[:, :, 0]).then_inc(loaded, 16)
                sp.dma_start(other[:, :], view[:, :, 1]).then_inc(loaded, 16)
                sp.wait_ge(preset, 2)
                sp.dma_start(after[0:P - 1, :], view[1:P, 0, 0:1]).then_inc(loaded, 16)
                sp.dma_start(before[1:P, :], view[0:P - 1, J - 1, 0:1]).then_inc(loaded, 16)
                if full:
                    sp.dma_start(e.att[:, :, :], view[:, :, 2:WD]).then_inc(loaded, 16)

            @block.vector
            def _(dve):
                link = linked(dve, chain)
                dve.memset(after[:, :], -1.0).then_inc(preset, 1)
                dve.memset(before[:, :], -1.0).then_inc(preset, 1)
                link(dve.memset(e.cont[:, :], 0.0))
                link(dve.memset(end[:, :], 1.0))
                link(dve.tensor_scalar(off[:, :], keep.ident[:, :], -1.0, 1.0, ALU.mult, ALU.add))
                dve.wait_ge(loaded, 80 if full else 64)
                first, last = key[:, 0:1], key[:, J - 1:J]
                link(dve.tensor_copy(e.other_i[:, :], other[:, :]))
                link(dve.tensor_tensor(e.cont[:, 1:J], key[:, 1:J], key[:, 0:J - 1], ALU.is_equal))
                link(dve.tensor_scalar(end[:, 0:J - 1], e.cont[:, 1:J], -1.0, 1.0, ALU.mult, ALU.add))
                if full:
                    link(dve.tensor_copy(e.key_i[:, :], key[:, :]))
                    for h in range(HEADS):
                        dve.tensor_copy(e.cont_h[:, h, :], e.cont[:, :])
                        dve.tensor_copy(e.end_h[:, h, :], end[:, :])
                        dve.tensor_scalar(e.next_h[:, h, :], end[:, :], -1.0, 1.0, ALU.mult, ALU.add)
                        link(dve.tensor_scalar(e.reset_h[:, h, :], e.cont[:, :], -1.0, BIG, ALU.add, ALU.mult))
                link(dve.tensor_tensor(goes_on[:, :], last, after[:, :], ALU.is_equal))
                link(dve.tensor_scalar(end[:, J - 1:J], goes_on[:, :], -1.0, 1.0, ALU.mult, ALU.add))
                link(dve.tensor_scalar(tmp[:, :], end[:, :], -FAR, FAR, ALU.mult, ALU.add))
                link(dve.tensor_tensor(tmp[:, :], tmp[:, :], key[:, :], ALU.add))
                link(dve.tensor_copy(e.put_i[:, :], tmp[:, :]))
                link(dve.tensor_tensor(whole[:, :], first, last, ALU.is_equal))
                link(dve.tensor_tensor(owns[:, :], whole[:, :], goes_on[:, :], ALU.mult))
                link(dve.tensor_scalar(owns[:, :], owns[:, :], -1.0, 1.0, ALU.mult, ALU.add))
                link(dve.tensor_tensor(fix[:, :], first, before[:, :], ALU.is_equal))
                link(dve.tensor_tensor(fix[:, :], fix[:, :], owns[:, :], ALU.mult))
                link(dve.tensor_scalar(fix[:, :], fix[:, :], -FAR, FAR, ALU.mult, ALU.add))
                link(dve.tensor_tensor(fix[:, :], fix[:, :], first, ALU.add))
                link(dve.tensor_copy(e.fix_i[:, :], fix[:, :]))
                dve.tensor_scalar(diag[:, 0, :], keep.ident[:, :], last, None, ALU.mult).then_inc(diag_ready, 1)
                dve.tensor_scalar(diag[:, 1, :], keep.ident[:, :], first, None, ALU.mult).then_inc(diag_ready, 1)
                dve.wait_ge(spread_done, 1)
                link(dve.tensor_scalar(e.carry[:, :], spread[:, 1, :], last, None, ALU.is_equal))
                link(dve.tensor_tensor(e.carry[:, :], e.carry[:, :], off[:, :], ALU.mult))
                if full:
                    for t, mine in enumerate((first, last)):
                        link(dve.tensor_scalar(e.same[t][:, :, :], spread[:, :, :], mine, None, ALU.is_equal))
                        link(dve.tensor_scalar(e.same_add[t][:, :, :], e.same[t][:, :, :], -1.0, BIG, ALU.add, ALU.mult))
                        link(dve.tensor_scalar(e.in_add[t][:, :], key[:, :], mine, None, ALU.is_equal))
                        link(dve.tensor_scalar(e.in_add[t][:, :], e.in_add[t][:, :], -1.0, BIG, ALU.add, ALU.mult))
                    link(dve.tensor_scalar(e.split[:, :], whole[:, :], -1.0, 1.0, ALU.mult, ALU.add))

            @block.tensor
            def _(pe):
                pe.wait_ge(diag_ready, 2)
                pe.matmul(spread[:, :, :], keep.ones[:, :], diag[:, :, :], start=True, stop=True).then_inc(spread_done, 1)
    return e


def spread_ends(pe, keep, heads, diag, spread_ps, diag_ready, spread_done, n):
    pe.wait_ge(diag_ready, n)
    pe.matmul(spread_ps[0][:, 0:heads * P], keep.ones[:, :], diag[:, 0, 0:heads, :], start=True, stop=True)
    pe.matmul(spread_ps[1][:, 0:heads * P], keep.ones[:, :], diag[:, 1, 0:heads, :], start=True, stop=True)\
        .then_inc(spread_done, 1)


def key_reduce(dve, link, keep, e, kind, heads, values, out, run, diag, cand, whole, ends, spread_ps, diag_ready,
               spread_done, n):
    def flat(a):
        return a[:, 0:heads, :].rearrange("p h j -> p (h j)")

    if kind == "max":
        link(dve.tensor_tensor_scan(flat(run), flat(e.reset_h), flat(values), -BIG, ALU.add, ALU.max))
    else:
        link(dve.tensor_tensor_scan(flat(run), flat(e.cont_h), flat(values), 0.0, ALU.mult, ALU.add))
    link(dve.tensor_tensor(flat(run), flat(run), flat(e.end_h), ALU.mult))
    link(dve.tensor_tensor_scan(flat(out)[:, ::-1], flat(e.next_h)[:, ::-1], flat(run)[:, ::-1], 0.0, ALU.mult, ALU.add))
    link(dve.tensor_copy(ends[:, 0, 0:heads], out[:, 0:heads, J - 1]))
    if kind == "max":
        link(dve.tensor_copy(ends[:, 1, 0:heads], out[:, 0:heads, 0]))
    else:
        link(dve.tensor_scalar(ends[:, 1, 0:heads], out[:, 0:heads, 0], e.split[:, 0:1], None, ALU.mult))
    for t in range(2):
        for h in range(heads):
            dve.tensor_scalar(diag[:, t, h, :], keep.ident[:, :], ends[:, t, h:h + 1], None, ALU.mult)\
                .then_inc(diag_ready, 1)
    dve.wait_ge(spread_done, n)
    for t in range(2):
        for u in range(2):
            mask = (e.same_add if kind == "max" else e.same)[t][:, u, :].unsqueeze(1).broadcast_to([P, heads, P])
            link(dve.tensor_tensor(cand[:, 0:heads, u, :], spread_ps[u][:, 0:heads * P].rearrange("p (h q) -> p h q", h=heads),
                                   mask, ALU.add if kind == "max" else ALU.mult))
        link(dve.tensor_reduce(whole[:, 0:heads], cand[:, 0:heads, :, :], AX.XY, ALU.max if kind == "max" else ALU.add))
        for h in range(heads):
            link(dve.scalar_tensor_tensor(out[:, h, :], e.in_add[t][:, :], whole[:, h:h + 1], out[:, h, :], ALU.add, ALU.max))


def reduce_memory(ph, heads):
    run, diag = ph.sb("run", [P, heads, J]), ph.sb("diag", [P, 2, heads, P])
    cand, whole, ends = ph.sb("cand", [P, heads, 2, P]), ph.sb("whole", [P, heads]), ph.sb("ends", [P, 2, heads])
    spread_ps = [ph.ps(f"spread_ps{t}", [P, 512]) for t in range(2)]
    return run, diag, cand, whole, ends, spread_ps, ph.sem("diag_ready"), ph.sem("spread_done")


def degrees(nc, keep, e):
    with Phase(nc, "deg") as ph:
        mem = reduce_memory(ph, 1)
        ones = ph.sb("ones", [P, 1, J])
        chain = ph.sem("chain")
        with nc.Block() as block:
            @block.vector
            def _(dve):
                link = linked(dve, chain)
                link(dve.memset(ones[:, :, :], 1.0))
                key_reduce(dve, link, keep, e, "sum", 1, ones, e.deg[:, :].unsqueeze(1), *mem, 1)
                link(dve.tensor_scalar(e.rdeg[:, :], e.deg[:, :], 1.0, None, ALU.max))
                link(dve.reciprocal(e.rdeg[:, :], e.rdeg[:, :]))

            @block.tensor
            def _(pe):
                spread_ends(pe, keep, 1, mem[1], mem[5], mem[6], mem[7], 2)


def edge_sum(nc, keep, name, e, agg, prepare, table=None, fetched=0):
    out_width = agg.shape[1]
    with Phase(nc, name) as ph:
        msg = ph.sb("msg", [P, SLOTS, GC, ROW])
        get_s = ph.sb("get_s", [P, SLOTS, GC], I32)
        put_s = ph.sb("put_s", [P, SLOTS, GC], I32)
        fixed = ph.sb("fixed", [P, ROW])
        carry_ps = ph.ps("carry_ps", [P, 512])
        cleared, staged, go = ph.sem("cleared"), ph.sem("staged"), ph.sem("go")
        gathered = [ph.sem(f"gathered{s}") for s in range(SLOTS)]
        scattered = [ph.sem(f"scattered{s}") for s in range(SLOTS)]
        step, summed = ph.sem("step"), ph.sem("summed")
        carried, fix_in, fix_done, fix_out = ph.sem("carried"), ph.sem("fix_in"), ph.sem("fix_done"), ph.sem("fix_out")
        with nc.Block() as block:
            prepare.start(block, ph)

            @block.gpsimd
            def _(pool):
                bound = pool.to_reg(NPAD - 1)
                pool.wait_ge(cleared, 2)

                def stage(turn, s, of, to, n):
                    pool.tensor_copy(to[:, s, :], of[:, bass.ds(turn * TURN + s * GC, GC)]).then_inc(staged, 1)
                    pool.wait_ge(staged, n)

                def gather(turn, s, n):
                    pool.wait_ge(scattered[s], turn * (16 * GC))
                    stage(turn, s, e.other_i, get_s, n)
                    pool.sem_inc(go, 1)
                    for k in range(GC):
                        pool.indirect_dma_start(out=msg[:, s, k, 0:fetched], out_offset=None, in_=table,
                                                in_offset=bass.IndirectOffsetOnAxis(ap=get_s[:, s, k:k + 1], axis=0))\
                            .then_inc(gathered[s], 16)

                def scatter(turn, s, n):
                    pool.wait_ge(summed, turn * SLOTS + s + 1)
                    stage(turn, s, e.put_i, put_s, n)
                    pool.sem_inc(go, 1)
                    for k in range(GC):
                        pool.indirect_dma_start(out=agg, out_offset=bass.IndirectOffsetOnAxis(ap=put_s[:, s, k:k + 1], axis=0),
                                                in_=msg[:, s, k, 0:out_width], in_offset=None, bounds_check=bound,
                                                oob_is_err=False).then_inc(scattered[s], 16)

                if table is None:
                    with pool.Fori(0, TURNS) as turn:
                        for s in range(SLOTS):
                            scatter(turn, s, turn * SLOTS + s + 1)
                else:
                    gather(0, 0, 1)
                    gather(0, 1, 2)

                    def groups(turn, last):
                        for s in range(SLOTS):
                            n = turn * (2 * SLOTS) + 2 * s + 2
                            ahead = (s + 2) // SLOTS
                            more = not (last and ahead)
                            if more:
                                gather(turn + ahead, (s + 2) % SLOTS, n + 1)
                            scatter(turn, s, n + 2 if more else turn * (2 * SLOTS) + 6 + s - 1)

                    with pool.Fori(0, TURNS - 1) as turn:
                        groups(turn, False)
                    groups(TURNS - 1, True)
                for s in range(SLOTS):
                    pool.wait_ge(scattered[s], TURNS * 16 * GC)
                pool.indirect_dma_start(out=fixed[:, 0:out_width], out_offset=None, in_=agg,
                                        in_offset=bass.IndirectOffsetOnAxis(ap=e.fix_i[:, 0:1], axis=0),
                                        bounds_check=bound, oob_is_err=False).then_inc(fix_in, 16)
                pool.wait_ge(fix_done, 1)
                pool.indirect_dma_start(out=agg, out_offset=bass.IndirectOffsetOnAxis(ap=e.fix_i[:, 0:1], axis=0),
                                        in_=fixed[:, 0:out_width], in_offset=None, bounds_check=bound,
                                        oob_is_err=False).then_inc(fix_out, 16)
                pool.wait_ge(fix_out, 16)

            @block.vector
            def _(dve):
                dve.memset(msg[:, :, :, :], 0.0).then_inc(cleared, 1)
                dve.memset(fixed[:, :], 0.0).then_inc(cleared, 1)
                dve.wait_ge(cleared, 1)
                per_turn = SLOTS * (GC + prepare.steps)
                with dve.Fori(0, TURNS) as turn:
                    n = 0
                    for s in range(SLOTS):
                        if table is None:
                            dve.wait_ge(scattered[s], turn * (16 * GC))
                        else:
                            dve.wait_ge(gathered[s], turn * (16 * GC) + 16 * GC)
                        for ins in prepare(dve, turn, s, msg, lambda: dve.wait_ge(step, turn * per_turn + n)):
                            ins.then_inc(step, 1)
                            n += 1
                        for k in range(GC):
                            before = msg[:, s, k - 1, 0:D] if k else msg[:, (s - 1) % SLOTS, GC - 1, 0:D]
                            dve.wait_ge(step, turn * per_turn + n)
                            ins = dve.scalar_tensor_tensor(msg[:, s, k, 0:D], before,
                                                           e.cont[:, bass.ds(turn * TURN + s * GC + k, 1)],
                                                           msg[:, s, k, 0:D], ALU.mult, ALU.add)
                            ins.then_inc(step, 1)
                            n += 1
                        dve.wait_ge(step, turn * per_turn + n)
                        dve.sem_inc(summed, 1)
                    assert n == per_turn
                dve.wait_ge(carried, 1)
                dve.wait_ge(fix_in, 16)
                dve.tensor_tensor(fixed[:, 0:D], fixed[:, 0:D], carry_ps[:, 0:D], ALU.add).then_inc(fix_done, 1)

            @block.tensor
            def _(pe):
                pe.wait_ge(summed, TURNS * SLOTS)
                pe.matmul(carry_ps[:, 0:D], e.carry[:, :], msg[:, SLOTS - 1, GC - 1, 0:D], start=True, stop=True)\
                    .then_inc(carried, 1)


class PrepareMean:
    steps = 2

    def __init__(self, e):
        self.e = e

    def start(self, block, ph):
        pass

    def __call__(self, dve, turn, s, msg, settle):
        cols = bass.ds(turn * TURN + s * GC, GC)
        yield dve.tensor_tensor(msg[:, s, :, 0:D], msg[:, s, :, 0:D],
                                self.e.rdeg[:, cols].unsqueeze(2).broadcast_to([P, GC, D]), ALU.mult)
        yield dve.tensor_copy(msg[:, s, :, D], self.e.deg[:, cols])


class PrepareNorm:
    steps = 1

    def start(self, block, ph):
        pass

    def __call__(self, dve, turn, s, msg, settle):
        yield dve.tensor_tensor(msg[:, s, :, 0:D], msg[:, s, :, 0:D],
                                msg[:, s, :, D:D + 1].broadcast_to([P, GC, D]), ALU.mult)


class PrepareAttention:
    steps = 2

    def __init__(self, rows, weight, tail):
        self.rows, self.weight, self.tail = rows, weight, tail

    def start(self, block, ph):
        pass

    def __call__(self, dve, turn, s, msg, settle):
        cols = bass.ds(turn * TURN + s * GC, GC)
        yield dve.tensor_tensor(
            msg[:, s, :, 0:D].rearrange("p k (h d) -> p k h d", h=GAT_HEADS),
            self.rows[:, cols, 0:D].rearrange("p k (h d) -> p k h d", h=GAT_HEADS),
            self.weight[:, :, cols].rearrange("p h k -> p k h").unsqueeze(3).broadcast_to([P, GC, GAT_HEADS, GAT_D]), ALU.mult)
        yield dve.tensor_copy(msg[:, s, :, D:ROW], self.tail[:, :, cols].rearrange("p w k -> p k w"))


class PrepareGatv2:
    steps = HEADS * GC

    def __init__(self, keep, xt, wl, bl_parts, alpha):
        self.keep, self.xt, self.wl, self.bl_parts, self.alpha = keep, xt, wl, bl_parts, alpha

    def start(self, block, ph):
        xg = ph.sb("xg", [P, 2, GC, P])
        self.xl_ps = [ph.ps(f"xl_ps{q}", [P, HD]) for q in range(XL_BANKS)]
        copied = ph.sem("copied")
        self.xl_ready, self.used = ph.sem("xl_ready"), ph.sem("used")

        @block.scalar
        def _(act):
            def copy(turn, s):
                after(act, self.xl_ready, turn, s * GC, GC + 1, TURN)
                act.activation(xg[:, s % 2].rearrange("p k n -> p (k n)"),
                               self.xt[:, bass.ds((turn * TURN + s * GC) * P, GC * P)], ACT.Copy).then_inc(copied, 1)
            pipeline(act, (0, copy), per_turn=SLOTS, total=TURNS * SLOTS)

        @block.tensor
        def _(pe):
            def product(turn, c):
                s, k = c // GC, c % GC
                if k == 0:
                    pe.wait_ge(copied, turn * SLOTS + s + 1)
                after(pe, self.used, turn, c, XL_BANKS, TURN)
                pe.matmul(self.xl_ps[c % XL_BANKS][:, :], xg[:, s % 2, k, :], self.wl[:, :], start=True, stop=False)
                pe.matmul(self.xl_ps[c % XL_BANKS][:, :], self.keep.ones_b[0:3, :], self.bl_parts[0:3, :],
                          start=False, stop=True).then_inc(self.xl_ready, 1)
            pipeline(pe, (0, product), per_turn=TURN, total=J)

    def __call__(self, dve, turn, s, msg, settle):
        for k in range(GC):
            c = s * GC + k
            col = bass.ds(turn * TURN + c, 1)
            dve.wait_ge(self.xl_ready, turn * TURN + c + 1)
            for h in range(HEADS):
                part, weight = self.xl_ps[c % XL_BANKS][:, h * D:(h + 1) * D], self.alpha[:, h, col]
                if h == 0:
                    yield dve.tensor_scalar(msg[:, s, k, 0:D], part, weight, None, ALU.mult)
                else:
                    settle()
                    yield dve.scalar_tensor_tensor(msg[:, s, k, 0:D], part, weight, msg[:, s, k, 0:D], ALU.mult, ALU.add)
            settle()
            dve.sem_inc(self.used, 1)


XL_BANKS = 4
GAT_HEADS, GAT_D = 2, D // 2


def after(engine, sem, turn, place, lag, per_turn):
    n = turn * per_turn + place + 1 - lag
    if not isinstance(n, int) or n > 0:
        engine.wait_ge(sem, n)


class Steps:

    def __init__(self, engine, sem, turn, per_turn):
        self.engine, self.sem, self.first, self.per_turn, self.n = engine, sem, turn * per_turn, per_turn, 0

    def __call__(self, ins):
        ins.then_inc(self.sem, 1)
        self.n += 1

    def wait(self):
        self.engine.wait_ge(self.sem, self.first + self.n)


def slot_sems(ph, name):
    return [ph.sem(f"{name}{s}") for s in range(SLOT)]


LN_EPS = 1e-05
BANKS = 2
NTURN = NB // SLOT


def wait_bank(engine, sems, turn, s, per_block=1):
    engine.wait_ge(sems[(s - BANKS) % SLOT], (turn + (s - BANKS) // SLOT + 1) * per_block)


def norm_sums(dve, aside, r, stats, mv, done):
    for g in range(GB):
        ins = dve.bn_stats(stats[:, g, :], r[:, g, :])
    aside(ins)
    aside.wait()
    dve.sem_inc(aside.sem, 1)
    aside.n += 1
    for g in range(GB):
        ins = dve.bn_aggr(mv[:, g, :], stats[:, g, :])
    ins.then_inc(done, 1)


NORM_STEPS = 2


def norm_scale(pool, keep, st, mv, rstd, done):
    st(pool.tensor_tensor(rstd, mv[:, :, 1], keep.eps[:, :], ALU.add))
    st.wait()
    pool.tensor_tensor(rstd, rstd, keep.minus_half[:, :], ALU.pow).then_inc(done, 1)


def norm_apply(dve, r, mv, rstd, out):
    for g in range(GB):
        ins = dve.tensor_scalar(out[:, g, 0:D], r[:, g, :], mv[:, g, 0:1], rstd[:, g:g + 1], ALU.subtract, ALU.mult)
    return ins


def block_rows(a, turn, s):
    return a.rearrange("(t s p g) d -> t s p g d", s=SLOT, p=P, g=GB)[turn, s] if isinstance(turn, int) else \
        a.rearrange("(t s p g) d -> t s p g d", s=SLOT, p=P, g=GB)[bass.ds(turn, 1), s].squeeze(0)


def pipeline(engine, *stages, per_turn=SLOT, total=NB):
    first = max(1, -(-max(lag for lag, _ in stages) // per_turn))

    def steps(turn, peeled):
        for s in range(per_turn):
            for lag, fn in stages:
                if not peeled or 0 <= turn * per_turn + s - lag < total:
                    fn(turn + (s - lag) // per_turn, (s - lag) % per_turn)

    for turn in range(first):
        steps(turn, True)
    with engine.Fori(first, total // per_turn) as turn:
        steps(turn, False)
    for turn in range(total // per_turn, total // per_turn + first):
        steps(turn, True)


def node_sage(nc, keep, x, agg, w, bias, x1):
    with Phase(nc, "n0") as ph:
        wa, wb, b = ph.sb("wa", [P, D]), ph.sb("wb", [P, D]), ph.sb("b", [P, D])
        xs, ag = ph.sb("xs", [P, SLOT, GB, D]), ph.sb("ag", [P, SLOT, GB, ROW])
        xb, r = ph.sb("xb", [P, SLOT, GB, D]), ph.sb("r", [P, SLOT, GB, D])
        o = ph.sb("o", [P, SLOT, GB, ROW])
        xt, at = ph.sb("xt", [P, SLOT, GB, P]), ph.sb("at", [P, SLOT, GB, P])
        stats, mv, rstd = ph.sb("stats", [P, SLOT, GB, 6]), ph.sb("mv", [P, SLOT, GB, 2]), ph.sb("rstd", [P, SLOT, GB])
        xt_ps = [ph.ps(f"xt_ps{q}", [P, GB, P]) for q in range(BANKS)]
        at_ps = [ph.ps(f"at_ps{q}", [P, GB, P]) for q in range(BANKS)]
        y_ps = [ph.ps(f"y_ps{q}", [P, GB, D]) for q in range(BANKS)]
        weights = ph.sem("weights")
        x_in, ag_in = [ph.sem(f"x_in{s}") for s in range(SLOT)], [ph.sem(f"ag_in{s}") for s in range(SLOT)]
        stored = [ph.sem(f"stored{s}") for s in range(SLOT)]
        turned, moved, xb_ready, y_ready, x1_ready, steps = (
            slot_sems(ph, "turned"), slot_sems(ph, "moved"), slot_sems(ph, "xb_ready"), slot_sems(ph, "y_ready"), slot_sems(ph, "x1_ready"), ph.sem("steps"))
        sums_ready, rstd_ready, cleared, pool_step, norm_step = (
            slot_sems(ph, "sums_ready"), slot_sems(ph, "rstd_ready"), ph.sem("cleared"), ph.sem("pool_step"), ph.sem("norm_step"))
        with nc.Block() as block:
            @block.sync
            def _(sp):
                sp.dma_start(wa[:, :], w[0:D, :]).then_inc(weights, 16)
                sp.dma_start(wb[:, :], w[D:2 * D, :]).then_inc(weights, 16)
                sp.dma_start(b[:, :], bias.partition_broadcast(P)).then_inc(weights, 16)
                with sp.Fori(0, NTURN) as turn:
                    for s in range(SLOT):
                        sp.wait_ge(xb_ready[s], turn * 2)
                        sp.wait_ge(turned[s], turn)
                        sp.dma_start(xs[:, s], block_rows(x, turn, s)).then_inc(x_in[s], 16)
                        sp.dma_start(ag[:, s], block_rows(agg, turn, s)).then_inc(ag_in[s], 16)

            @block.gpsimd
            def _(pool):
                pool.wait_ge(weights, 48)
                pool.wait_ge(cleared, 1)

                def add_bias(turn, s):
                    st = Steps(pool, pool_step, turn * SLOT + s, 1)
                    pool.wait_ge(x_in[s], turn * 16 + 16)
                    pool.tensor_tensor(xb[:, s], xs[:, s], b[:, :].unsqueeze(1).broadcast_to([P, GB, D]), ALU.add)\
                        .then_inc(xb_ready[s], 1)
                    pool.wait_ge(ag_in[s], turn * 16 + 16)
                    pool.wait_ge(stored[s], turn * 16)
                    st(pool.tensor_tensor(o[:, s, :, D], ag[:, s, :, D], keep.ones[:, 0:GB], ALU.add))
                    st.wait()
                    pool.tensor_tensor(o[:, s, :, D], o[:, s, :, D], keep.minus_half[:, :], ALU.pow).then_inc(xb_ready[s], 1)

                def scale(turn, s):
                    pool.wait_ge(sums_ready[s], turn + 1)
                    st = Steps(pool, norm_step, turn * SLOT + s, 1)
                    norm_scale(pool, keep, st, mv[:, s], rstd[:, s, :], rstd_ready[s])

                pipeline(pool, (3, scale), (0, add_bias))

            @block.tensor
            def _(pe):
                pe.wait_ge(weights, 48)

                def turn_over(turn, s):
                    pe.wait_ge(x_in[s], turn * 16 + 16)
                    pe.wait_ge(ag_in[s], turn * 16 + 16)
                    wait_bank(pe, moved, turn, s, 2)
                    for g in range(GB):
                        pe.transpose(xt_ps[s % BANKS][:, g, :], xs[:, s, g, :], keep.ident[:, :])
                    for g in range(GB):
                        ins = pe.transpose(at_ps[s % BANKS][:, g, :], ag[:, s, g, 0:D], keep.ident[:, :])
                    ins.then_inc(turned[s], 1)

                def product(turn, s):
                    pe.wait_ge(moved[s], turn * 2 + 2)
                    wait_bank(pe, sums_ready, turn, s)
                    for g in range(GB):
                        pe.matmul(y_ps[s % BANKS][:, g, :], xt[:, s, g, :], wa[:, :], start=True, stop=False)
                        ins = pe.matmul(y_ps[s % BANKS][:, g, :], at[:, s, g, :], wb[:, :], start=False, stop=True)
                    ins.then_inc(y_ready[s], 1)

                pipeline(pe, (2, product), (0, turn_over))

            @block.scalar
            def _(act):
                def store(turn, s):
                    act.wait_ge(x1_ready[s], turn + 1)
                    act.dma_start(block_rows(x1, turn, s), o[:, s]).then_inc(stored[s], 16)

                def move(turn, s):
                    act.wait_ge(turned[s], turn + 1)
                    act.wait_ge(y_ready[s], turn)
                    act.activation(xt[:, s], xt_ps[s % BANKS][:, :, :], ACT.Copy).then_inc(moved[s], 1)
                    act.activation(at[:, s], at_ps[s % BANKS][:, :, :], ACT.Copy).then_inc(moved[s], 1)

                pipeline(act, (5, store), (0, move))
                for s in range(SLOT):
                    act.wait_ge(stored[s], 16 * NTURN)

            @block.vector
            def _(dve):
                dve.memset(o[:, :, :, :], 0.0).then_inc(cleared, 1)

                def sums(turn, s):
                    st = Steps(dve, steps, turn * SLOT + s, NORM_STEPS + 1)
                    dve.wait_ge(y_ready[s], turn + 1)
                    dve.wait_ge(xb_ready[s], turn * 2 + 2)
                    st(dve.tensor_tensor(r[:, s], y_ps[s % BANKS][:, :, :], xb[:, s], ALU.add))
                    st.wait()
                    norm_sums(dve, st, r[:, s], stats[:, s], mv[:, s], sums_ready[s])

                def apply(turn, s):
                    dve.wait_ge(rstd_ready[s], turn + 1)
                    norm_apply(dve, r[:, s], mv[:, s], rstd[:, s], o[:, s]).then_inc(x1_ready[s], 1)

                pipeline(dve, (4, apply), (2, sums))


def node_gcn(nc, keep, name, z, agg, w, beta, out, x1=None):
    with Phase(nc, name) as ph:
        wm = ph.sb("wm", [P, D])
        zs, ag = ph.sb("zs", [P, SLOT, GB, ROW]), ph.sb("ag", [P, SLOT, GB, D])
        t, c1, c2 = ph.sb("t", [P, SLOT, GB, D]), ph.sb("c1", [P, SLOT, GB]), ph.sb("c2", [P, SLOT, GB])
        xp, xt = ph.sb("xp", [P, SLOT, GB, D]), ph.sb("xt", [P, SLOT, GB, P])
        width = out.shape[1]
        o = ph.sb("o", [P, SLOT, GB, width])
        xr = ph.sb("xr", [P, SLOT, GB, ROW]) if x1 is not None else None
        r = ph.sb("r", [P, SLOT, GB, D])
        stats, mv, rstd = ph.sb("stats", [P, SLOT, GB, 6]), ph.sb("mv", [P, SLOT, GB, 2]), ph.sb("rstd", [P, SLOT, GB])
        t_ps = [ph.ps(f"t_ps{q}", [P, GB, P]) for q in range(BANKS)]
        y_ps = [ph.ps(f"y_ps{q}", [P, GB, D]) for q in range(BANKS)]
        weights, mixed, w_ready = ph.sem("weights"), ph.sem("mixed"), ph.sem("w_ready")
        z_in = [ph.sem(f"z_in{s}") for s in range(SLOT)]
        ag_in = [ph.sem(f"ag_in{s}") for s in range(SLOT)]
        r_in = [ph.sem(f"r_in{s}") for s in range(SLOT)]
        stored = [ph.sem(f"stored{s}") for s in range(SLOT)]
        pstep, scaled, xp_ready, turned, moved, y_ready, out_ready, steps = (
            ph.sem("pstep"), slot_sems(ph, "scaled"), slot_sems(ph, "xp_ready"), slot_sems(ph, "turned"), slot_sems(ph, "moved"),
            slot_sems(ph, "y_ready"), slot_sems(ph, "out_ready"), ph.sem("steps"))
        sums_ready, rstd_ready, pool_step = slot_sems(ph, "sums_ready"), slot_sems(ph, "rstd_ready"), ph.sem("pool_step")
        last = x1 is not None
        with nc.Block() as block:
            @block.sync
            def _(sp):
                sp.dma_start(wm[:, :], w).then_inc(weights, 16)
                with sp.Fori(0, NTURN) as turn:
                    for s in range(SLOT):
                        sp.wait_ge(scaled[s], turn)
                        sp.wait_ge(xp_ready[s], turn)
                        sp.dma_start(zs[:, s], block_rows(z, turn, s)).then_inc(z_in[s], 16)
                        sp.dma_start(ag[:, s], block_rows(agg, turn, s)).then_inc(ag_in[s], 16)
                        if last:
                            sp.wait_ge(sums_ready[s], turn)
                            sp.dma_start(xr[:, s], block_rows(x1, turn, s)).then_inc(r_in[s], 16)

            @block.gpsimd
            def _(pool):
                def scale(turn, s):
                    st = Steps(pool, pstep, turn * SLOT + s, 5 if last else 6)
                    pool.wait_ge(z_in[s], turn * 16 + 16)
                    pool.wait_ge(xp_ready[s], turn)
                    pool.sem_inc(pstep, 1)
                    st.n += 1
                    if not last:
                        pool.wait_ge(stored[s], turn * 16)
                        st(pool.tensor_tensor(o[:, s, :, D:ROW], zs[:, s, :, D:ROW],
                                              keep.ones[:, 0:GB * (ROW - D)].rearrange("p (g w) -> p g w", g=GB), ALU.mult))
                    st(pool.tensor_scalar(c1[:, s, :], zs[:, s, :, D], 0.9, None, ALU.mult))
                    st.wait()
                    st(pool.tensor_tensor(c2[:, s, :], c1[:, s, :], zs[:, s, :, D], ALU.mult))
                    st.wait()
                    pool.sem_inc(pstep, 1)
                    st.n += 1
                    st(pool.tensor_scalar(c2[:, s, :], c2[:, s, :], 0.1, None, ALU.add))
                    st.wait()
                    pool.tensor_tensor(t[:, s], zs[:, s, :, 0:D], c2[:, s, :].unsqueeze(2).broadcast_to([P, GB, D]),
                                       ALU.mult).then_inc(scaled[s], 1)

                def deviation(turn, s):
                    pool.wait_ge(sums_ready[s], turn + 1)
                    norm_scale(pool, keep, Steps(pool, pool_step, turn * SLOT + s, 1), mv[:, s], rstd[:, s, :], rstd_ready[s])

                pipeline(pool, *([(3, deviation)] if last else []), (0, scale))

            @block.tensor
            def _(pe):
                pe.wait_ge(w_ready, 1)

                def turn_over(turn, s):
                    pe.wait_ge(xp_ready[s], turn + 1)
                    wait_bank(pe, moved, turn, s)
                    for g in range(GB):
                        ins = pe.transpose(t_ps[s % BANKS][:, g, :], xp[:, s, g, :], keep.ident[:, :])
                    ins.then_inc(turned[s], 1)

                def product(turn, s):
                    pe.wait_ge(moved[s], turn + 1)
                    wait_bank(pe, sums_ready if last else out_ready, turn, s)
                    for g in range(GB):
                        ins = pe.matmul(y_ps[s % BANKS][:, g, :], xt[:, s, g, :], wm[:, :], start=True, stop=True)
                    ins.then_inc(y_ready[s], 1)

                pipeline(pe, (2, product), (0, turn_over))

            @block.scalar
            def _(act):
                def move(turn, s):
                    act.wait_ge(turned[s], turn + 1)
                    act.wait_ge(y_ready[s], turn)
                    act.activation(xt[:, s], t_ps[s % BANKS][:, :, :], ACT.Copy).then_inc(moved[s], 1)

                def keep_z(turn, s):
                    act.wait_ge(y_ready[s], turn + 1)
                    act.wait_ge(stored[s], turn * 16)
                    act.activation(o[:, s, :, 0:D], y_ps[s % BANKS][:, :, :], ACT.Copy).then_inc(out_ready[s], 1)

                def store(turn, s):
                    act.wait_ge(out_ready[s], turn + 1)
                    act.dma_start(block_rows(out, turn, s), o[:, s]).then_inc(stored[s], 16)

                if last:
                    pipeline(act, (5, store), (0, move))
                else:
                    pipeline(act, (3, store), (2, keep_z), (0, move))
                for s in range(SLOT):
                    act.wait_ge(stored[s], 16 * NTURN)

            @block.vector
            def _(dve):
                dve.wait_ge(weights, 16)
                dve.tensor_scalar(r[:, 0, 0, :], keep.ident[:, :], 1.0 - beta, None, ALU.mult).then_inc(mixed, 1)
                dve.wait_ge(mixed, 1)
                dve.scalar_tensor_tensor(wm[:, :], wm[:, :], beta, r[:, 0, 0, :], ALU.mult, ALU.add).then_inc(w_ready, 1)
                dve.wait_ge(w_ready, 1)

                def mix(turn, s):
                    dve.wait_ge(scaled[s], turn + 1)
                    dve.wait_ge(ag_in[s], turn * 16 + 16)
                    dve.wait_ge(turned[s], turn)
                    for g in range(GB):
                        ins = dve.scalar_tensor_tensor(xp[:, s, g, :], ag[:, s, g, :], c1[:, s, g:g + 1], t[:, s, g, :],
                                                       ALU.mult, ALU.add)
                    ins.then_inc(xp_ready[s], 1)

                def sums(turn, s):
                    st = Steps(dve, steps, turn * SLOT + s, NORM_STEPS + 1)
                    dve.wait_ge(y_ready[s], turn + 1)
                    dve.wait_ge(r_in[s], turn * 16 + 16)
                    st(dve.tensor_tensor(r[:, s], y_ps[s % BANKS][:, :, :], xr[:, s, :, 0:D], ALU.add))
                    st.wait()
                    norm_sums(dve, st, r[:, s], stats[:, s], mv[:, s], sums_ready[s])

                def apply(turn, s):
                    dve.wait_ge(rstd_ready[s], turn + 1)
                    dve.wait_ge(stored[s], turn * 16)
                    norm_apply(dve, r[:, s], mv[:, s], rstd[:, s], o[:, s]).then_inc(out_ready[s], 1)

                pipeline(dve, *([(4, apply), (2, sums)] if last else []), (0, mix))


def split_bf16(engine, link, value, rest, parts):
    link(engine.tensor_copy(parts[0], value))
    link(engine.tensor_tensor(rest, value, parts[0], ALU.subtract))
    link(engine.tensor_copy(parts[1], rest))
    link(engine.tensor_tensor(rest, rest, parts[1], ALU.subtract))
    link(engine.tensor_copy(parts[2], rest))


def gatv2_weights(nc, keep, stack, w):
    g = Keep()

    def sb(name, shape, dt=F32):
        return stack.enter_context(nc.sbuf_tensor(f"gat2_{name}", shape, dt))

    g.wl, g.wr, g.att = sb("wl", [P, HD]), sb("wr", [P, HD]), sb("att", [P, HD])
    g.edge, g.bl_parts = sb("edge", [ATT_IN + 1, HD]), sb("bl_parts", [3, HD], BF16)
    with Phase(nc, "g2w") as ph:
        both = ph.sb("both", [1, 3, HD])
        part = [ph.sb(f"part{i}", [1, HD], BF16) for i in range(3)]
        loaded, chain, summed, edge_in, spread = (ph.sem("loaded"), ph.sem("chain"), ph.sem("summed"), ph.sem("edge_in"),
                                                 ph.sem("spread"))
        with nc.Block() as block:
            @block.sync
            def _(sp):
                sp.dma_start(both[0:1, 0, :], w["bl"].unsqueeze(0)).then_inc(loaded, 16)
                sp.dma_start(both[0:1, 1, :], w["br"].unsqueeze(0)).then_inc(loaded, 16)
                sp.dma_start(g.wl[:, :], w["Wl"]).then_inc(edge_in, 16)
                sp.dma_start(g.wr[:, :], w["Wr"]).then_inc(edge_in, 16)
                sp.dma_start(g.att[:, :], w["att"].rearrange("h d -> (h d)").partition_broadcast(P)).then_inc(edge_in, 16)
                sp.dma_start(g.edge[0:ATT_IN, :], w["We"]).then_inc(edge_in, 16)
                sp.wait_ge(summed, 1)
                sp.dma_start(g.edge[ATT_IN:ATT_IN + 1, :], both[0:1, 2, :]).then_inc(spread, 16)
                for i in range(3):
                    sp.dma_start(g.bl_parts[i:i + 1, :], part[i][0:1, :]).then_inc(spread, 16)
                sp.wait_ge(edge_in, 64)
                sp.wait_ge(spread, 64)

            @block.vector
            def _(dve):
                link = linked(dve, chain)
                dve.wait_ge(loaded, 32)
                link(dve.tensor_tensor(both[0:1, 2, :], both[0:1, 0, :], both[0:1, 1, :], ALU.add))
                split_bf16(dve, link, both[0:1, 0, :], both[0:1, 1, :], [p[0:1, :] for p in part])
                dve.sem_inc(summed, 1)
    return g


def gatv2_logits(nc, keep, e, g, x, xt, logits):
    with Phase(nc, "lg") as ph:
        rows = ph.sb("rows", [P, SLOTS, GC, 2, D])
        get_s = ph.sb("get_s", [P, SLOTS, 2, GC], I32)
        att_s = ph.sb("att_s", [P, SLOTS, GC, ATT_IN + 1])
        tr = ph.sb("tr", [P, 2, 2, P])
        at = ph.sb("at", [ATT_IN + 1, 2, P])
        z = ph.sb("z", [P, 2, HD])
        junk = ph.sb("junk", [P, 2, HD])
        sums = ph.sb("sums", [P, 2, HEADS, GC])
        tr_ps = [ph.ps(f"tr_ps{q}", [P, 4, P]) for q in range(2)]
        at_ps = [ph.ps(f"at_ps{q}", [P, 512]) for q in range(2)]
        z_ps = [ph.ps(f"z_ps{q}", [P, HD]) for q in range(2)]
        gathered = [ph.sem(f"gathered{s}") for s in range(SLOTS)]
        turned = [ph.sem(f"turned{s}") for s in range(SLOTS)]
        staged, go, moved, moved_att, kept = ph.sem("staged"), ph.sem("go"), ph.sem("moved"), ph.sem("moved_att"), ph.sem("kept")
        z_low = ph.sem("z_low")
        z_ready, z_out, scored, grouped, stage_go = (ph.sem("z_ready"), ph.sem("z_out"), ph.sem("scored"), ph.sem("grouped"), ph.sem("stage_go"))
        with nc.Block() as block:
            @block.gpsimd
            def _(pool):
                with pool.Fori(0, TURNS) as turn:
                    for s in range(SLOTS):
                        pool.wait_ge(turned[s], turn * GC)
                        cols = bass.ds(turn * TURN + s * GC, GC)
                        pool.sem_inc(stage_go, 1)
                        pool.tensor_copy(get_s[:, s, 0, :], e.other_i[:, cols]).then_inc(staged, 1)
                        pool.tensor_copy(get_s[:, s, 1, :], e.key_i[:, cols]).then_inc(staged, 1)
                        pool.tensor_copy(att_s[:, s], e.att[:, cols, :]).then_inc(staged, 1)
                        pool.wait_ge(staged, turn * (3 * SLOTS) + 3 * s + 3)
                        pool.sem_inc(go, 1)
                        for k in range(GC):
                            for i in range(2):
                                pool.indirect_dma_start(out=rows[:, s, k, i, :], out_offset=None, in_=x,
                                                        in_offset=bass.IndirectOffsetOnAxis(ap=get_s[:, s, i, k:k + 1], axis=0))\
                                    .then_inc(gathered[s], 16)

            @block.tensor
            def _(pe):
                def turn_over(turn, c):
                    s, k, q = c // GC, c % GC, c % 2
                    if k == 0:
                        pe.wait_ge(gathered[s], turn * (32 * GC) + 32 * GC)
                        pe.wait_ge(staged, turn * (3 * SLOTS) + 3 * s + 3)
                    after(pe, moved, turn, c, 2, TURN)
                    after(pe, moved_att, turn, c, 2, TURN)
                    for i in range(2):
                        pe.transpose(tr_ps[q][:, i, :], rows[:, s, k, i, :], keep.ident[:, :])
                    pe.transpose(at_ps[q][0:ATT_IN + 1, 0:P], att_s[:, s, k, :], keep.ident[:, :]).then_inc(turned[s], 1)

                def product(turn, c):
                    q = c % 2
                    pe.wait_ge(moved, turn * TURN + c + 1)
                    pe.wait_ge(moved_att, turn * TURN + c + 1)
                    after(pe, z_out, turn, c, 2, TURN)
                    pe.matmul(z_ps[q][:, :], tr[:, q, 0, :], g.wl[:, :], start=True, stop=False)
                    pe.matmul(z_ps[q][:, :], tr[:, q, 1, :], g.wr[:, :], start=False, stop=False)
                    pe.matmul(z_ps[q][:, :], at[:, q, :], g.edge[:, :], start=False, stop=True).then_inc(z_ready, 1)

                pipeline(pe, (0, turn_over), (1, product), per_turn=TURN, total=J)

            @block.scalar
            def _(act):
                def move(turn, c):
                    s, k, q = c // GC, c % GC, c % 2
                    act.wait_ge(turned[s], turn * GC + k + 1)
                    after(act, z_ready, turn, c, 2, TURN)
                    after(act, kept, turn, c, 2, TURN)
                    act.activation(tr[:, q, :, :], tr_ps[q][:, 0:2, :], ACT.Copy).then_inc(moved, 1)

                def low(turn, c):
                    act.wait_ge(z_ready, turn * TURN + c + 1)
                    after(act, scored, turn, c, 2, TURN)
                    act.activation(z[:, c % 2, :], z_ps[c % 2][:, :], ACT.Copy, scale=SLOPE).then_inc(z_low, 1)

                pipeline(act, (0, move), (1, low), per_turn=TURN, total=J)

            @block.vector
            def _(dve):
                def move(turn, c):
                    s, k, q = c // GC, c % GC, c % 2
                    dve.wait_ge(turned[s], turn * GC + k + 1)
                    after(dve, z_ready, turn, c, 2, TURN)
                    dve.tensor_copy(at[:, q, :], at_ps[q][0:ATT_IN + 1, 0:P]).then_inc(moved_att, 1)

                def score(turn, c):
                    s, k, q = c // GC, c % GC, c % 2
                    dve.wait_ge(moved, turn * TURN + c + 1)
                    dve.tensor_copy(xt[:, bass.ds((turn * TURN + c) * P, P)], tr[:, q, 0, :]).then_inc(kept, 1)
                    dve.wait_ge(z_low, turn * TURN + c + 1)
                    dve.tensor_tensor(z[:, q, :], z_ps[q][:, :], z[:, q, :], ALU.max).then_inc(z_out, 1)
                    dve.wait_ge(z_out, turn * TURN + c + 1)
                    if k == 0:
                        after(dve, grouped, turn, s, 2, SLOTS)
                    for h in range(HEADS):
                        part = slice(h * D, (h + 1) * D)
                        ins = dve.tensor_tensor_reduce(junk[:, q, part], z[:, q, part], g.att[:, part], 1.0, 0.0,
                                                       ALU.mult, ALU.add, sums[:, s % 2, h, k:k + 1])
                    ins.then_inc(scored, 1)
                    if k == GC - 1:
                        dve.wait_ge(scored, turn * TURN + c + 1)
                        dve.tensor_copy(logits[:, :, bass.ds(turn * TURN + s * GC, GC)], sums[:, s % 2]).then_inc(grouped, 1)

                pipeline(dve, (0, move), (1, score), per_turn=TURN, total=J)


SLOPE = 0.2


def softmax(nc, keep, e, heads, logits, out, name, make_logits=None, top=None, total=None):
    with Phase(nc, name) as ph:
        mem = reduce_memory(ph, heads)
        red = ph.sb("red", [P, heads, J])
        chain, ready, done = ph.sem("chain"), ph.sem("ready"), ph.sem("done")
        top = top if top is not None else red[:, :, :]
        with nc.Block() as block:
            @block.vector
            def _(dve):
                link = linked(dve, chain)
                if make_logits is not None:
                    make_logits(dve, link)
                key_reduce(dve, link, keep, e, "max", heads, logits, top, *mem, 1)
                link(dve.tensor_tensor(logits, logits, top, ALU.subtract))
                dve.sem_inc(ready, 1)
                dve.wait_ge(done, 1)
                sums = total if total is not None else red[:, :, :]
                key_reduce(dve, link, keep, e, "sum", heads, out, sums, *mem, 2)
                if total is None:
                    link(dve.tensor_scalar(sums, sums, 1e-16, float(heads), ALU.add, ALU.mult))
                    link(dve.reciprocal(sums, sums))
                    link(dve.tensor_tensor(out, out, sums, ALU.mult))

            @block.scalar
            def _(act):
                act.wait_ge(ready, 1)
                act.activation(out, logits, ACT.Exp).then_inc(done, 1)

            @block.tensor
            def _(pe):
                for n in range(2):
                    spread_ends(pe, keep, heads, mem[1], mem[5], mem[6], mem[7], 2 * heads * (n + 1))


def gatv2_edges(nc, keep, e, w, x, agg):
    with ExitStack() as stack:
        g = gatv2_weights(nc, keep, stack, w)
        xt = stack.enter_context(nc.sbuf_tensor("xt_kept", [P, J * P], F32))
        logits = stack.enter_context(nc.sbuf_tensor("logits", [P, HEADS, J], F32))
        alpha = stack.enter_context(nc.sbuf_tensor("alpha", [P, HEADS, J], F32))
        gatv2_logits(nc, keep, e, g, x, xt, logits)
        softmax(nc, keep, e, HEADS, logits[:, :, :], alpha[:, :, :], "sm2")
        edge_sum(nc, keep, "e2", e, agg, PrepareGatv2(keep, xt, g.wl, g.bl_parts, alpha))


def gat_edges(nc, keep, name, e, h, agg):
    with ExitStack() as stack:
        def sb(n, shape):
            return stack.enter_context(nc.sbuf_tensor(f"{name}_{n}", shape, F32))

        rows, a_dst = sb("rows", [P, J, ROW]), sb("a_dst", [P, J, GAT_HEADS])
        logits, weight = sb("logits", [P, GAT_HEADS, J]), sb("weight", [P, GAT_HEADS, J])
        tail = sb("tail", [P, 2 * GAT_HEADS, J])
        pairs = h.rearrange("n (a b) -> (n a) b", b=GAT_HEADS)
        with Phase(nc, name + "g") as ph:
            got, got_a = ph.sb("got", [P, SLOTS, GC, ROW]), ph.sb("got_a", [P, SLOTS, GC, GAT_HEADS])
            a_row = ph.sb("a_row", [P, J], I32)
            get_s = ph.sb("get_s", [P, SLOTS, 2, GC], I32)
            gathered, kept = [ph.sem(f"gathered{s}") for s in range(SLOTS)], [ph.sem(f"kept{s}") for s in range(SLOTS)]
            rows_known, staged, go = ph.sem("rows_known"), ph.sem("staged"), ph.sem("go")
            with nc.Block() as block:
                @block.vector
                def _(dve):
                    dve.tensor_scalar(a_row[:, :], e.key_i[:, :], ROW // GAT_HEADS, ROW // GAT_HEADS - 1, ALU.mult, ALU.add)\
                        .then_inc(rows_known, 1)
                    with dve.Fori(0, TURNS) as turn:
                        for s in range(SLOTS):
                            dve.wait_ge(gathered[s], turn * (32 * GC) + 32 * GC)
                            cols = bass.ds(turn * TURN + s * GC, GC)
                            dve.tensor_copy(rows[:, cols, :], got[:, s]).then_inc(kept[s], 1)
                            dve.tensor_copy(a_dst[:, cols, :], got_a[:, s]).then_inc(kept[s], 1)

                @block.gpsimd
                def _(pool):
                    pool.wait_ge(rows_known, 1)
                    with pool.Fori(0, TURNS) as turn:
                        for s in range(SLOTS):
                            pool.wait_ge(kept[s], turn * 2)
                            cols = bass.ds(turn * TURN + s * GC, GC)
                            pool.sem_inc(go, 1)
                            pool.tensor_copy(get_s[:, s, 0, :], e.other_i[:, cols]).then_inc(staged, 1)
                            pool.tensor_copy(get_s[:, s, 1, :], a_row[:, cols]).then_inc(staged, 1)
                            pool.wait_ge(staged, turn * (2 * SLOTS) + 2 * s + 2)
                            pool.sem_inc(go, 1)
                            for k in range(GC):
                                for table, to, i in ((h, got, 0), (pairs, got_a, 1)):
                                    pool.indirect_dma_start(out=to[:, s, k, :], out_offset=None, in_=table,
                                                            in_offset=bass.IndirectOffsetOnAxis(ap=get_s[:, s, i, k:k + 1], axis=0))\
                                        .then_inc(gathered[s], 16)

        def make_logits(dve, link):
            link(dve.tensor_tensor(logits[:, :, :], rows[:, :, D:D + GAT_HEADS].rearrange("p j h -> p h j"),
                                   a_dst[:, :, :].rearrange("p j h -> p h j"), ALU.add))
            link(dve.scalar_tensor_tensor(logits[:, :, :], logits[:, :, :], SLOPE, logits[:, :, :], ALU.mult, ALU.max))

        softmax(nc, keep, e, GAT_HEADS, logits[:, :, :], weight[:, :, :], name + "s", make_logits,
                tail[:, 0:GAT_HEADS, :], tail[:, GAT_HEADS:, :])
        edge_sum(nc, keep, name + "m", e, agg, PrepareAttention(rows, weight, tail))


def done(engine, sems, turn, s, per_turn=1):
    engine.wait_ge(sems[s], (turn + 1) * per_turn)


def free(engine, sems, turn, s, per_turn=1):
    engine.wait_ge(sems[s], turn * per_turn)


def bank_free(engine, sems, turn, s, per_turn=1):
    engine.wait_ge(sems[(s - 1) % SLOT], (turn + (s - 1) // SLOT + 1) * per_turn)


def wide(v):
    return v.unsqueeze(1).broadcast_to([P, GB, D])


def attention_weights(dve, link, out, w, att_src, att_dst, tmp):
    link(dve.tensor_copy(out[:, 0:D], w))
    for i, att in enumerate((att_src, att_dst)):
        link(dve.tensor_tensor(tmp, w, att, ALU.mult))
        link(dve.tensor_reduce(out[:, D + GAT_HEADS * i:D + GAT_HEADS * (i + 1)],
                               tmp.rearrange("p (h c) -> p h c", h=GAT_HEADS), AX.X, ALU.add))


def node_gatv2(nc, keep, x2, agg, w, gat, x3, h3):
    with Phase(nc, "n2") as ph:
        names = ("conv_bias", "g1", "beta1", "b2", "g2", "beta2")
        vec = {n: ph.sb(n, [P, D]) for n in names}
        w1, b1, w2 = ph.sb("w1", [P, 2, D]), ph.sb("b1", [P, 2]), ph.sb("w2", [P, 2, D])
        wh, att, waug, tmp = ph.sb("wh", [P, D]), ph.sb("att", [P, 2, D]), ph.sb("waug", [P, ROW]), ph.sb("tmp", [P, D])
        xs, ag = ph.sb("xs", [P, SLOT, GB, D]), ph.sb("ag", [P, SLOT, GB, D])
        r1, r2, x3s = ph.sb("r1", [P, SLOT, GB, D]), ph.sb("r2", [P, SLOT, GB, D]), ph.sb("x3s", [P, SLOT, GB, D])
        xt1, xt3, gt = ph.sb("xt1", [P, SLOT, GB, P]), ph.sb("xt3", [P, SLOT, GB, P]), ph.sb("gt", [P, SLOT, 2, GB, P])
        ho = ph.sb("ho", [P, SLOT, GB, ROW])
        stats = [ph.sb(f"stats{i}", [P, SLOT, GB, 6]) for i in range(3)]
        mv, rstd = [ph.sb(f"mv{i}", [P, SLOT, GB, 2]) for i in range(3)], [ph.sb(f"rstd{i}", [P, SLOT, GB]) for i in range(3)]
        t1_ps, t3_ps, y_ps = (ph.ps(n, [P, GB, P]) for n in ("t1_ps", "t3_ps", "y_ps"))
        f_ps, h_ps = [ph.ps(f"f_ps{j}", [P, GB, P]) for j in range(2)], [ph.ps(f"h_ps{j}", [P, 2, ROW]) for j in range(2)]
        weights, chain, w_ready = ph.sem("weights"), ph.sem("chain"), ph.sem("w_ready")
        x_in, ag_in, x3_out, h_out = (slot_sems(ph, n) for n in ("x_in", "ag_in", "x3_out", "h_out"))
        added, sums1, rstd1, normed1, scaled1 = (slot_sems(ph, n) for n in ("added", "sums1", "rstd1", "normed1", "scaled1"))
        turned1, moved1, f_ready, gelued, y_ready = (slot_sems(ph, n) for n in ("turned1", "moved1", "f_ready", "gelued", "y_ready"))
        sums2, rstd2, normed2, scaled2 = (slot_sems(ph, n) for n in ("sums2", "rstd2", "normed2", "scaled2"))
        sums3, rstd3, x3_ready = (slot_sems(ph, n) for n in ("sums3", "rstd3", "x3_ready"))
        turned3, moved3, h_ready, h_kept = (slot_sems(ph, n) for n in ("turned3", "moved3", "h_ready", "h_kept"))
        pool_steps = [ph.sem(f"pool_steps{i}") for i in range(5)]
        dve_steps = [ph.sem(f"dve_steps{i}") for i in range(3)]
        n_weights = 16 * (len(names) + 6)
        with nc.Block() as block, nc.allow_non_contiguous_dma(reason="the FFN's first bias, a column for each half"):
            @block.sync
            def _(sp):
                for n in names:
                    sp.dma_start(vec[n][:, :], w[n].partition_broadcast(P)).then_inc(weights, 16)
                sp.dma_start(w1[:, :, :], w["W1"].rearrange("d (j f) -> d j f", j=2)).then_inc(weights, 16)
                sp.dma_start(w2[:, :, :], w["W2"].rearrange("(j f) d -> f j d", j=2)).then_inc(weights, 16)
                sp.dma_start(b1[:, :], w["b1"].rearrange("(j f) -> f j", j=2)).then_inc(weights, 16)
                sp.dma_start(wh[:, :], gat["W"]).then_inc(weights, 16)
                for i, n in enumerate(("att_src", "att_dst")):
                    sp.dma_start(att[:, i, :], gat[n].rearrange("h c -> (h c)").partition_broadcast(P)).then_inc(weights, 16)
                with sp.Fori(0, NTURN) as turn:
                    for s in range(SLOT):
                        free(sp, scaled2, turn, s)
                        free(sp, sums1, turn, s)
                        sp.dma_start(xs[:, s], block_rows(x2, turn, s)).then_inc(x_in[s], 16)
                        sp.dma_start(ag[:, s], block_rows(agg, turn, s)[:, :, 0:D]).then_inc(ag_in[s], 16)

            @block.gpsimd
            def _(pool):
                pool.wait_ge(weights, n_weights)

                def add(turn, s):
                    done(pool, x_in, turn, s, 16)
                    free(pool, turned1, turn, s)
                    pool.tensor_tensor(r1[:, s], xs[:, s], wide(vec["conv_bias"][:, :]), ALU.add).then_inc(added[s], 1)

                def deviation(i, sums, out):
                    def fn(turn, s):
                        done(pool, sums, turn, s)
                        norm_scale(pool, keep, Steps(pool, pool_steps[i], turn * SLOT + s, 1), mv[i][:, s], rstd[i][:, s, :], out[s])
                    return fn

                def scale1(turn, s):
                    st = Steps(pool, pool_steps[3], turn * SLOT + s, 2)
                    done(pool, normed1, turn, s)
                    st(pool.tensor_tensor(r1[:, s], r1[:, s], wide(vec["g1"][:, :]), ALU.mult))
                    st.wait()
                    st(pool.tensor_tensor(r1[:, s], r1[:, s], wide(vec["beta1"][:, :]), ALU.add))
                    st.wait()
                    free(pool, x3_ready, turn, s)
                    pool.tensor_tensor(r2[:, s], r1[:, s], wide(vec["b2"][:, :]), ALU.add).then_inc(scaled1[s], 1)

                def scale2(turn, s):
                    st = Steps(pool, pool_steps[4], turn * SLOT + s, 2)
                    done(pool, normed2, turn, s)
                    st(pool.tensor_tensor(r2[:, s], r2[:, s], wide(vec["g2"][:, :]), ALU.mult))
                    st.wait()
                    st(pool.tensor_tensor(r2[:, s], r2[:, s], wide(vec["beta2"][:, :]), ALU.add))
                    st.wait()
                    pool.tensor_tensor(r2[:, s], r2[:, s], xs[:, s], ALU.add).then_inc(scaled2[s], 1)

                pipeline(pool, (3, deviation(2, sums3, rstd3)), (2, deviation(1, sums2, rstd2)), (0, add), (1, scale1),
                         (2, scale2), (0, deviation(0, sums1, rstd1)))

            @block.vector
            def _(dve):
                link = linked(dve, chain)
                dve.wait_ge(weights, n_weights)
                attention_weights(dve, link, waug[:, :], wh[:, :], att[:, 0, :], att[:, 1, :], tmp[:, :])
                dve.sem_inc(w_ready, 1)

                def sums(i, turn, s, r, out, other):
                    st = Steps(dve, dve_steps[i], turn * SLOT + s, 2 + (other is not None))
                    if other is not None:
                        st(dve.tensor_tensor(r, r, other, ALU.add))
                        st.wait()
                    norm_sums(dve, st, r, stats[i][:, s], mv[i][:, s], out[s])

                def first_sums(turn, s):
                    done(dve, added, turn, s)
                    done(dve, ag_in, turn, s, 16)
                    sums(0, turn, s, r1[:, s], sums1, ag[:, s])

                def second_sums(turn, s):
                    done(dve, y_ready, turn, s)
                    done(dve, scaled1, turn, s)
                    sums(1, turn, s, r2[:, s], sums2, y_ps[:, :, :])

                def third_sums(turn, s):
                    done(dve, scaled2, turn, s)
                    sums(2, turn, s, r2[:, s], sums3, None)

                def first_norm(turn, s):
                    done(dve, rstd1, turn, s)
                    norm_apply(dve, r1[:, s], mv[0][:, s], rstd[0][:, s], r1[:, s]).then_inc(normed1[s], 1)

                def second_norm(turn, s):
                    done(dve, rstd2, turn, s)
                    norm_apply(dve, r2[:, s], mv[1][:, s], rstd[1][:, s], r2[:, s]).then_inc(normed2[s], 1)

                def third_norm(turn, s):
                    done(dve, rstd3, turn, s)
                    free(dve, x3_out, turn, s, 16)
                    free(dve, turned3, turn, s)
                    norm_apply(dve, r2[:, s], mv[2][:, s], rstd[2][:, s], x3s[:, s]).then_inc(x3_ready[s], 1)

                pipeline(dve, (3, third_sums), (2, second_sums), (3, third_norm), (1, first_norm), (2, second_norm),
                         (0, first_sums))

            @block.tensor
            def _(pe):
                pe.wait_ge(weights, n_weights)
                pe.wait_ge(w_ready, 1)

                def ffn2(turn, s):
                    done(pe, gelued, turn, s, 2)
                    bank_free(pe, sums2, turn, s)
                    for g in range(GB):
                        for j in range(2):
                            ins = pe.matmul(y_ps[:, g, :], gt[:, s, j, g, :], w2[:, j, :], start=j == 0, stop=j == 1)
                    ins.then_inc(y_ready[s], 1)

                def turn3(turn, s):
                    done(pe, x3_ready, turn, s)
                    bank_free(pe, moved3, turn, s)
                    for g in range(GB):
                        ins = pe.transpose(t3_ps[:, g, :], x3s[:, s, g, :], keep.ident[:, :])
                    ins.then_inc(turned3[s], 1)

                def product3(turn, s):
                    done(pe, moved3, turn, s)
                    bank_free(pe, h_kept, turn, s, 2)
                    for g in range(GB):
                        ins = pe.matmul(h_ps[g // 2][:, g % 2, :], xt3[:, s, g, :], waug[:, :], start=True, stop=True)
                    ins.then_inc(h_ready[s], 1)

                def turn1(turn, s):
                    done(pe, scaled1, turn, s)
                    bank_free(pe, moved1, turn, s)
                    for g in range(GB):
                        ins = pe.transpose(t1_ps[:, g, :], r1[:, s, g, :], keep.ident[:, :])
                    ins.then_inc(turned1[s], 1)

                def ffn1(turn, s):
                    done(pe, moved1, turn, s)
                    bank_free(pe, gelued, turn, s, 2)
                    for j in range(2):
                        ins = pe.matmul(f_ps[j][:, :, :], w1[:, j, :], xt1[:, s], start=True, stop=True)
                    ins.then_inc(f_ready[s], 1)

                pipeline(pe, (2, ffn2), (3, turn3), (3, product3), (1, turn1), (1, ffn1))

            @block.scalar
            def _(act):
                def store_h(turn, s):
                    done(act, h_kept, turn, s, 2)
                    act.dma_start(block_rows(h3, turn, s), ho[:, s]).then_inc(h_out[s], 16)

                def store_x3(turn, s):
                    done(act, x3_ready, turn, s)
                    act.dma_start(block_rows(x3, turn, s), x3s[:, s]).then_inc(x3_out[s], 16)

                def move3(turn, s):
                    done(act, turned3, turn, s)
                    free(act, h_ready, turn, s)
                    act.activation(xt3[:, s], t3_ps[:, :, :], ACT.Copy).then_inc(moved3[s], 1)

                def keep_h(turn, s):
                    done(act, h_ready, turn, s)
                    free(act, h_out, turn, s, 16)
                    for j in range(2):
                        act.activation(ho[:, s, 2 * j:2 * j + 2, :], h_ps[j][:, :, :], ACT.Copy).then_inc(h_kept[s], 1)

                def move1(turn, s):
                    done(act, turned1, turn, s)
                    free(act, f_ready, turn, s)
                    act.activation(xt1[:, s], t1_ps[:, :, :], ACT.Copy).then_inc(moved1[s], 1)

                def gelu(turn, s):
                    done(act, f_ready, turn, s)
                    free(act, y_ready, turn, s)
                    for j in range(2):
                        act.activation(gt[:, s, j], f_ps[j][:, :, :], ACT.Gelu, bias=b1[:, j:j + 1]).then_inc(gelued[s], 1)

                pipeline(act, (4, store_h), (3, move3), (3, store_x3), (3, keep_h), (1, move1), (1, gelu))
                for s in range(SLOT):
                    act.wait_ge(x3_out[s], 16 * NTURN)
                    act.wait_ge(h_out[s], 16 * NTURN)


class Attend:
    FIRST_STEPS, LAST_STEPS = 6, 3

    def __init__(self, ph, hs, ag):
        self.hs, self.ag = hs, ag
        self.own, self.top = ph.sb("own", [P, SLOT, GB, GAT_HEADS]), ph.sb("top", [P, SLOT, GB, GAT_HEADS])
        self.most = ph.sb("most", [P, SLOT, GB, GAT_HEADS])
        self.less, self.exps = ph.sb("less", [P, SLOT, 2, GB, GAT_HEADS]), ph.sb("exps", [P, SLOT, 2, GB, GAT_HEADS])
        self.total, self.share = ph.sb("total", [P, SLOT, GB, GAT_HEADS]), ph.sb("share", [P, SLOT, 2, GB, GAT_HEADS])
        self.u = ph.sb("u", [P, SLOT, 2, GB, D])
        self.steps = [ph.sem(f"attend_steps{i}") for i in range(3)]
        self.h_in, self.ag_in = slot_sems(ph, "h_in"), slot_sems(ph, "ag_in")
        self.less_ready, self.exps_ready, self.share_ready = (slot_sems(ph, n) for n in ("less_ready", "exps_ready", "share_ready"))
        self.u_ready = slot_sems(ph, "u_ready")

    def load(self, sp, turn, s, h, agg):
        free(sp, self.u_ready, turn, s)
        sp.dma_start(self.hs[:, s], block_rows(h, turn, s)).then_inc(self.h_in[s], 16)
        sp.dma_start(self.ag[:, s], block_rows(agg, turn, s)).then_inc(self.ag_in[s], 16)

    def first(self, dve, turn, s):
        a, h = self, GAT_HEADS
        st = Steps(dve, a.steps[0], turn * SLOT + s, a.FIRST_STEPS)
        done(dve, a.h_in, turn, s, 16)
        done(dve, a.ag_in, turn, s, 16)
        free(dve, a.exps_ready, turn, s)
        st(dve.tensor_tensor(a.own[:, s], a.hs[:, s, :, D:D + h], a.hs[:, s, :, D + h:ROW], ALU.add))
        st(dve.tensor_scalar(a.top[:, s], a.ag[:, s, :, D + h:ROW], 0.0, -BIG, ALU.is_equal, ALU.mult))
        st.wait()
        st(dve.scalar_tensor_tensor(a.own[:, s], a.own[:, s], SLOPE, a.own[:, s], ALU.mult, ALU.max))
        st(dve.tensor_tensor(a.top[:, s], a.top[:, s], a.ag[:, s, :, D:D + h], ALU.add))
        st.wait()
        st(dve.tensor_tensor(a.most[:, s], a.top[:, s], a.own[:, s], ALU.max))
        st.wait()
        st(dve.tensor_tensor(a.less[:, s, 0], a.top[:, s], a.most[:, s], ALU.subtract))
        dve.tensor_tensor(a.less[:, s, 1], a.own[:, s], a.most[:, s], ALU.subtract).then_inc(a.less_ready[s], 1)

    def exp(self, act, turn, s):
        done(act, self.less_ready, turn, s)
        free(act, self.share_ready, turn, s)
        act.activation(self.exps[:, s], self.less[:, s], ACT.Exp).then_inc(self.exps_ready[s], 1)

    def last(self, dve, turn, s):
        a = self
        st = Steps(dve, a.steps[1], turn * SLOT + s, a.LAST_STEPS)
        done(dve, a.exps_ready, turn, s)
        st(dve.tensor_tensor(a.total[:, s], a.ag[:, s, :, D + GAT_HEADS:ROW], a.exps[:, s, 0], ALU.mult))
        st.wait()
        st(dve.scalar_tensor_tensor(a.total[:, s], a.total[:, s], 1e-16, a.exps[:, s, 1], ALU.add, ALU.add))
        st.wait()
        free(dve, a.u_ready, turn, s)
        st(dve.reciprocal(a.total[:, s], a.total[:, s]))
        st.wait()
        dve.tensor_tensor(a.share[:, s], a.exps[:, s], a.total[:, s].unsqueeze(1).broadcast_to([P, 2, GB, GAT_HEADS]),
                          ALU.mult).then_inc(a.share_ready[s], 1)

    def combine(self, pool, turn, s):
        a = self
        st = Steps(pool, a.steps[2], turn * SLOT + s, 2)
        done(pool, a.share_ready, turn, s)
        for i, rows in enumerate((a.ag, a.hs)):
            st(pool.tensor_tensor(a.u[:, s, i].rearrange("p g (h c) -> p g h c", h=GAT_HEADS),
                                  rows[:, s, :, 0:D].rearrange("p g (h c) -> p g h c", h=GAT_HEADS),
                                  a.share[:, s, i].unsqueeze(3).broadcast_to([P, GB, GAT_HEADS, GAT_D]), ALU.mult))
        st.wait()
        pool.tensor_tensor(a.u[:, s, 0], a.u[:, s, 0], a.u[:, s, 1], ALU.add).then_inc(a.u_ready[s], 1)


def node_gat(nc, keep, x3, h3, agg, one, two, s2, h2):
    with Phase(nc, "n3") as ph:
        wsk1, wsk2, wh, att = ph.sb("wsk1", [P, D]), ph.sb("wsk2", [P, D]), ph.sb("wh", [P, D]), ph.sb("att", [P, 2, D])
        waug, tmp, b1, b2 = ph.sb("waug", [P, ROW]), ph.sb("tmp", [P, D]), ph.sb("b1", [P, 2]), ph.sb("b2", [P, 2, D])
        bias1, bias2 = ph.sb("bias1", [P, 1]), ph.sb("bias2", [P, D])
        xs, xb, xt, ht = (ph.sb(n, [P, SLOT, GB, D]) for n in ("xs", "xb", "xt", "ht"))
        hs, ag, ho = (ph.sb(n, [P, SLOT, GB, ROW]) for n in ("hs", "ag", "ho"))
        a = Attend(ph, hs, ag)
        t_ps, r_ps, s_ps = (ph.ps(n, [P, GB, P]) for n in ("t_ps", "r_ps", "s_ps"))
        h_ps = [ph.ps(f"h_ps{j}", [P, 2, ROW]) for j in range(2)]
        weights, chain, w_ready = ph.sem("weights"), ph.sem("chain"), ph.sem("w_ready")
        x_in, added, turned, moved, r_ready, relued = (slot_sems(ph, n) for n in ("x_in", "added", "turned", "moved", "r_ready", "relued"))
        product_ready, s_ready, h_kept, s_out, h_out = (slot_sems(ph, n) for n in ("product_ready", "s_ready", "h_kept", "s_out", "h_out"))
        n_weights = 16 * 9
        with nc.Block() as block, nc.allow_non_contiguous_dma(reason="two biases, a float on each partition"):
            @block.sync
            def _(sp):
                for to, of in ((wsk1, one["Wsk"]), (wsk2, two["Wsk"]), (wh, two["W"])):
                    sp.dma_start(to[:, :], of).then_inc(weights, 16)
                for i, n in enumerate(("att_src", "att_dst")):
                    sp.dma_start(att[:, i, :], two[n].rearrange("h c -> (h c)").partition_broadcast(P)).then_inc(weights, 16)
                for i, n in enumerate(("b", "bsk")):
                    sp.dma_start(b1[:, i:i + 1], one[n].unsqueeze(1)).then_inc(weights, 16)
                    sp.dma_start(b2[:, i, :], two[n].partition_broadcast(P)).then_inc(weights, 16)
                with sp.Fori(0, NTURN) as turn:
                    for s in range(SLOT):
                        free(sp, turned, turn, s)
                        free(sp, added, turn, s)
                        sp.dma_start(xs[:, s], block_rows(x3, turn, s)).then_inc(x_in[s], 16)
                        a.load(sp, turn, s, h3, agg)

            @block.gpsimd
            def _(pool):
                pool.wait_ge(w_ready, 1)

                def add(turn, s):
                    done(pool, x_in, turn, s, 16)
                    free(pool, s_out, turn, s, 16)
                    pool.tensor_tensor(xb[:, s], xs[:, s], wide(bias2[:, :]), ALU.add).then_inc(added[s], 1)

                pipeline(pool, (1, lambda turn, s: a.combine(pool, turn, s)), (0, add))

            @block.vector
            def _(dve):
                link = linked(dve, chain)
                dve.wait_ge(weights, n_weights)
                attention_weights(dve, link, waug[:, :], wh[:, :], att[:, 0, :], att[:, 1, :], tmp[:, :])
                link(dve.tensor_tensor(bias1[:, :], b1[:, 0:1], b1[:, 1:2], ALU.add))
                link(dve.tensor_tensor(bias2[:, :], b2[:, 0, :], b2[:, 1, :], ALU.add))
                dve.sem_inc(w_ready, 1)

                def total(turn, s):
                    done(dve, product_ready, turn, s)
                    done(dve, added, turn, s)
                    dve.tensor_tensor(xb[:, s], xb[:, s], s_ps[:, :, :], ALU.add).then_inc(s_ready[s], 1)

                pipeline(dve, (1, lambda turn, s: a.last(dve, turn, s)), (2, total), (0, lambda turn, s: a.first(dve, turn, s)))

            @block.tensor
            def _(pe):
                pe.wait_ge(w_ready, 1)

                def turn_over(turn, s):
                    done(pe, x_in, turn, s, 16)
                    bank_free(pe, moved, turn, s)
                    for g in range(GB):
                        ins = pe.transpose(t_ps[:, g, :], xs[:, s, g, :], keep.ident[:, :])
                    ins.then_inc(turned[s], 1)

                def residual(turn, s):
                    done(pe, moved, turn, s)
                    done(pe, a.u_ready, turn, s)
                    bank_free(pe, relued, turn, s)
                    pe.matmul(r_ps[:, :, :], wsk1[:, :], xt[:, s], start=True, stop=False, skip_group_check=True)
                    for g in range(GB):
                        ins = pe.matmul(r_ps[:, g, :], a.u[:, s, 0, g, :], keep.ident[:, :], start=False, stop=g == GB - 1,
                                        skip_group_check=True)
                    ins.then_inc(r_ready[s], 1)

                def product(turn, s):
                    done(pe, relued, turn, s)
                    bank_free(pe, s_ready, turn, s)
                    bank_free(pe, h_kept, turn, s, 2)
                    for g in range(GB):
                        pe.matmul(s_ps[:, g, :], ht[:, s, g, :], wsk2[:, :], start=True, stop=True)
                    for g in range(GB):
                        ins = pe.matmul(h_ps[g // 2][:, g % 2, :], ht[:, s, g, :], waug[:, :], start=True, stop=True)
                    ins.then_inc(product_ready[s], 1)

                pipeline(pe, (2, product), (0, turn_over), (1, residual))

            @block.scalar
            def _(act):
                act.wait_ge(w_ready, 1)

                def store(turn, s):
                    done(act, s_ready, turn, s)
                    act.dma_start(block_rows(s2, turn, s), xb[:, s]).then_inc(s_out[s], 16)
                    done(act, h_kept, turn, s, 2)
                    act.dma_start(block_rows(h2, turn, s), ho[:, s]).then_inc(h_out[s], 16)

                def keep_h(turn, s):
                    done(act, product_ready, turn, s)
                    free(act, h_out, turn, s, 16)
                    for j in range(2):
                        act.activation(ho[:, s, 2 * j:2 * j + 2, :], h_ps[j][:, :, :], ACT.Copy).then_inc(h_kept[s], 1)

                def move(turn, s):
                    done(act, turned, turn, s)
                    free(act, r_ready, turn, s)
                    act.activation(xt[:, s], t_ps[:, :, :], ACT.Copy).then_inc(moved[s], 1)

                def relu(turn, s):
                    done(act, r_ready, turn, s)
                    free(act, product_ready, turn, s)
                    act.activation(ht[:, s], r_ps[:, :, :], ACT.Relu, bias=bias1[:, 0:1]).then_inc(relued[s], 1)

                pipeline(act, (3, store), (2, keep_h), (0, move), (1, relu), (0, lambda turn, s: a.exp(act, turn, s)))
                for s in range(SLOT):
                    act.wait_ge(s_out[s], 16 * NTURN)
                    act.wait_ge(h_out[s], 16 * NTURN)


def node_last(nc, keep, s2, h2, agg, out):
    with Phase(nc, "n4") as ph:
        ss, os = ph.sb("ss", [P, SLOT, GB, D]), ph.sb("os", [P, SLOT, GB, D])
        hs, ag = (ph.sb(n, [P, SLOT, GB, ROW]) for n in ("hs", "ag"))
        a = Attend(ph, hs, ag)
        stats, mv, rstd = ph.sb("stats", [P, SLOT, GB, 6]), ph.sb("mv", [P, SLOT, GB, 2]), ph.sb("rstd", [P, SLOT, GB])
        s_in, sums_ready, rstd_ready, out_ready, stored = (slot_sems(ph, n) for n in ("s_in", "sums_ready", "rstd_ready", "out_ready", "stored"))
        dve_steps, pool_steps = ph.sem("dve_steps"), ph.sem("pool_steps")
        with nc.Block() as block:
            @block.sync
            def _(sp):
                with sp.Fori(0, NTURN) as turn:
                    for s in range(SLOT):
                        free(sp, out_ready, turn, s)
                        sp.dma_start(ss[:, s], block_rows(s2, turn, s)).then_inc(s_in[s], 16)
                        a.load(sp, turn, s, h2, agg)

            @block.gpsimd
            def _(pool):
                def deviation(turn, s):
                    done(pool, sums_ready, turn, s)
                    norm_scale(pool, keep, Steps(pool, pool_steps, turn * SLOT + s, 1), mv[:, s], rstd[:, s, :], rstd_ready[s])

                def combine(turn, s):
                    free(pool, sums_ready, turn, s)
                    a.combine(pool, turn, s)

                pipeline(pool, (2, deviation), (1, combine))

            @block.vector
            def _(dve):
                def sums(turn, s):
                    done(dve, a.u_ready, turn, s)
                    done(dve, s_in, turn, s, 16)
                    st = Steps(dve, dve_steps, turn * SLOT + s, NORM_STEPS + 1)
                    st(dve.tensor_tensor(ss[:, s], ss[:, s], a.u[:, s, 0], ALU.add))
                    st.wait()
                    norm_sums(dve, st, ss[:, s], stats[:, s], mv[:, s], sums_ready[s])

                def apply(turn, s):
                    done(dve, rstd_ready, turn, s)
                    free(dve, stored, turn, s, 16)
                    norm_apply(dve, ss[:, s], mv[:, s], rstd[:, s], os[:, s]).then_inc(out_ready[s], 1)

                pipeline(dve, (2, sums), (1, lambda turn, s: a.last(dve, turn, s)), (3, apply),
                         (0, lambda turn, s: a.first(dve, turn, s)))

            @block.scalar
            def _(act):
                def store(turn, s):
                    done(act, out_ready, turn, s)
                    act.dma_start(block_rows(out, turn, s), os[:, s]).then_inc(stored[s], 16)

                pipeline(act, (4, store), (0, lambda turn, s: a.exp(act, turn, s)))
                for s in range(SLOT):
                    act.wait_ge(stored[s], 16 * NTURN)


def gnn(nc, x, src, dst, attr, sage, gcn, gat2, gat, out):
    def dram(name, shape):
        return nc.dram_tensor(name, shape, F32, kind="Internal").ap()

    by_dst, by_src = [dram(f"by_dst{i}", (EPAD, WD)) for i in range(2)], [dram(f"by_src{i}", (EPAD, WS)) for i in range(2)]
    agg_dst, agg_src = dram("agg_dst", (NPAD, ROW)), dram("agg_src", (NPAD, D))
    x1, z1, h3, h4 = (dram(n, (NPAD, ROW)) for n in ("x1", "z1", "h3", "h4"))
    x2, x3, s4 = (dram(n, (NPAD, D)) for n in ("x2", "x3", "s4"))
    with ExitStack() as stack:
        keep = Keep()
        constants(nc, keep, stack)
        sort_pass(nc, keep, "d1", WD, LOW, False, load_edges(nc, src, dst, attr), by_dst[0], [agg_dst, agg_src])
        sort_pass(nc, keep, "d2", WD, HIGH, True, load_sorted(by_dst[0]), by_dst[1])
        sort_pass(nc, keep, "s1", WS, LOW, False, load_edges(nc, src, dst, None), by_src[0])
        sort_pass(nc, keep, "s2", WS, HIGH, True, load_sorted(by_src[0]), by_src[1])
        to_dst = edge_tables(nc, keep, "d", by_dst[1], WD, stack, True)
        with ExitStack() as src_stack:
            to_src = edge_tables(nc, keep, "s", by_src[1], WS, src_stack, False)
            degrees(nc, keep, to_dst)
            edge_sum(nc, keep, "e0", to_dst, agg_dst, PrepareMean(to_dst), x, D)
            node_sage(nc, keep, x, agg_dst, sage["W"], sage["b"], x1)
            edge_sum(nc, keep, "e1a", to_src, agg_src, PrepareNorm(), x1, ROW)
            node_gcn(nc, keep, "n1a", x1, agg_src, gcn["W1"], GCN_BETA[0], z1)
            edge_sum(nc, keep, "e1b", to_src, agg_src, PrepareNorm(), z1, ROW)
            node_gcn(nc, keep, "n1b", z1, agg_src, gcn["W2"], GCN_BETA[1], x2, x1)
        gatv2_edges(nc, keep, to_dst, gat2, x2, agg_dst)
        node_gatv2(nc, keep, x2, agg_dst, gat2, gat[0], x3, h3)
        gat_edges(nc, keep, "e3", to_dst, h3, agg_dst)
        node_gat(nc, keep, x3, h3, agg_dst, gat[0], gat[1], s4, h4)
        gat_edges(nc, keep, "e4", to_dst, h4, agg_dst)
        node_last(nc, keep, s4, h4, agg_dst, out)


def kernel(**inputs):
    import concourse.bacc as bacc
    from concourse.bass_utils import run_bass_kernel_spmd

    nc = bacc.Bacc("TRN2", target_bir_lowering=False, num_devices=1)
    arrays = {}

    def take(name, a):
        arrays[name] = np.ascontiguousarray(a)
        return nc.dram_tensor(name, arrays[name].shape, mybir.dt.from_np(arrays[name].dtype), kind="ExternalInput").ap()

    def padded(a, rows, fill):
        a = np.asarray(a)
        return np.concatenate([a, np.full((rows - a.shape[0],) + a.shape[1:], fill, a.dtype)])

    def layer(prefix, names, **more):
        w = {n: take(prefix + n, np.asarray(inputs[prefix + n])) for n in names}
        w.update({n: take(prefix + n, np.asarray(inputs[prefix + n]).T) for n in more.get("transposed", ())})
        return w

    x = take("x", padded(inputs["x"], NPAD, 0))
    src, dst = (take(n, padded(inputs[n], EPAD, NPAD - 1)) for n in ("src", "dst"))
    attr = take("edge_attr_16", padded(inputs["edge_attr_16"], EPAD, 0))
    sage = layer("L0_gnn_", ("W_neigh", "b_neigh"))
    gcn = layer("L1_gnn_", ("W1", "W2"))
    gat2 = layer("L2_gnn_", ("bl", "br", "att", "conv_bias", "g1", "beta1", "b1", "b2", "g2", "beta2"),
                 transposed=("Wl", "Wr", "We", "W1", "W2"))
    both = layer("L3_gnn_", [f"{n}{i}" for i in (1, 2) for n in ("W", "att_src", "att_dst", "b", "Wsk", "bsk")])
    gat = [{n: both[f"{n}{i}"] for n in ("W", "att_src", "att_dst", "b", "Wsk", "bsk")} for i in (1, 2)]
    out = nc.dram_tensor("out", (NPAD, D), F32, kind="ExternalOutput").ap()
    gnn(nc, x, src, dst, attr, {"W": sage["W_neigh"], "b": sage["b_neigh"]}, gcn, gat2, gat, out)
    r = run_bass_kernel_spmd(nc, [arrays], core_ids=[0])
    return r.results[0]["out"][:NODES]
```

```python
from contextlib import ExitStack
import numpy as np
import concourse.bass as bass
from concourse import mybir

F32, I32, F16, BF16 = mybir.dt.float32, mybir.dt.int32, mybir.dt.float16, mybir.dt.bfloat16
ALU, ACT, AX = mybir.AluOpType, mybir.ActivationFunctionType, mybir.AxisListType

P = 128
D = 128
NODES, EDGES = 50000, 25000
GB = 4
BLOCK = P * GB
SLOT = 4
NB = SLOT * -(-NODES // (SLOT * BLOCK))
NPAD = NB * BLOCK
GC, SLOTS = 7, 4
TURN = GC * SLOTS
J = TURN * -(-EDGES // (P * TURN))
EPAD = P * J
TURNS = J // TURN
ROW = D + 4
HEADS, HD = 4, 4 * D
ATT_IN = 16
WD = 3 + ATT_IN
WS = 2
LOW = 256
HIGH = NPAD // LOW
BIG = 1.0e30
GCN_BETA = (float(np.log(np.float32(1.5))), float(np.log(np.float32(1.25))))
FAR = 65536.0
assert NPAD % LOW == 0 and HIGH <= LOW and J % TURN == 0


class Phase:

    def __init__(self, nc, name, freed=""):
        self.nc, self.name, self.stack, self.sems = nc, name, ExitStack(), []
        self.freed_names, self.freed = freed.split(), []

    def free_slots(self, engine):
        for sems in self.freed:
            for s in sems:
                engine.sem_inc(s, 1)

    def sb(self, name, shape, dt=F32):
        return self.stack.enter_context(self.nc.sbuf_tensor(f"{self.name}_{name}", shape, dt))

    def ps(self, name, shape, dt=F32):
        return self.stack.enter_context(self.nc.psum_tensor(f"{self.name}_{name}", shape, dt))

    def sem(self, name):
        s = self.nc.alloc_semaphore(f"{self.name}_{name}")
        self.sems.append(s)
        return s

    def __enter__(self):
        return self

    def __exit__(self, *e):
        if e[0] is None:
            self.nc.clear_and_free_semaphores(self.sems)
            self.nc.all_engine_barrier()
        self.stack.close()


class Slots(list):
    base = 0


def slot_sems(ph, name, slots=SLOT):
    sems = Slots(ph.sem(f"{name}{s}") for s in range(slots))
    if name in ph.freed_names:
        sems.base = 1
        ph.freed.append(sems)
    return sems


def done(engine, sems, turn, s, per_turn=1):
    engine.wait_ge(sems[s], (turn + 1) * per_turn + sems.base)


def free(engine, sems, turn, s, per_turn=1):
    assert sems.base == 1
    engine.wait_ge(sems[s], turn * per_turn + 1)


def bank_free(engine, sems, turn, s, per_turn=1, banks=1):
    n = (turn + (s - banks) // SLOT + 1) * per_turn + sems.base
    if not isinstance(n, int) or n > 0:
        engine.wait_ge(sems[(s - banks) % SLOT], n)


def pass_on(sp, sems, to):
    with sp.Fori(0, TURNS) as turn:
        for s in range(SLOTS):
            done(sp, sems, turn, s, 16 * GC)
            sp.sem_inc(to[s], 1)



class Keep:
    pass


def constants(nc, keep, stack):
    def sb(name, shape, dt=F32):
        return stack.enter_context(nc.sbuf_tensor(name, shape, dt))

    keep.ident, keep.ones = sb("ident", [P, P]), sb("ones", [P, P])
    keep.ident_h, keep.ones_h = sb("ident_h", [P, P], F16), sb("ones_h", [P, P], F16)
    keep.tri_h, keep.iota_h = sb("tri_h", [P, P], F16), sb("iota_h", [P, LOW], F16)
    keep.ones_b = sb("ones_b", [P, P], BF16)
    keep.eps, keep.minus_half, keep.minus_one = (sb(n, [P, GB]) for n in ("eps", "minus_half", "minus_one"))
    with Phase(nc, "const") as ph:
        iota_i, filled, iota_done = ph.sb("iota_i", [P, LOW], I32), ph.sem("filled"), ph.sem("iota_done")
        shaped = ph.sem("shaped")
        with nc.Block() as block:
            @block.gpsimd
            def _(pool):
                pool.memset(keep.ident[:, :], 0.0).then_inc(filled, 1)
                pool.memset(keep.ones[:, :], 1.0).then_inc(filled, 1)
                pool.memset(keep.ones_h[:, :], 1.0).then_inc(filled, 1)
                pool.iota(iota_i[:, :], [[1, LOW]], base=0, channel_multiplier=0).then_inc(iota_done, 1)
                pool.wait_ge(filled, 3)
                pool.affine_select(out=keep.ident[:, :], in_=keep.ident[:, :], compare_op=ALU.not_equal, fill=1.0,
                                   base=0, pattern=[[-1, P]], channel_multiplier=1).then_inc(shaped, 1)
                pool.affine_select(out=keep.tri_h[:, :], in_=keep.ones_h[:, :], compare_op=ALU.is_gt, fill=0.0,
                                   base=0, pattern=[[1, P]], channel_multiplier=-1).then_inc(shaped, 1)

            @block.vector
            def _(dve):
                dve.memset(keep.eps[:, :], LN_EPS)
                dve.memset(keep.minus_half[:, :], -0.5)
                dve.memset(keep.minus_one[:, :], -1.0)
                dve.memset(keep.ones_b[:, :], 1.0)
                dve.wait_ge(iota_done, 1)
                dve.tensor_copy(keep.iota_h[:, :], iota_i[:, :])
                dve.wait_ge(shaped, 1)
                dve.tensor_copy(keep.ident_h[:, :], keep.ident[:, :])


def sort_pass(nc, keep, name, words, digits, high, load, target, zero_fill=None):
    with Phase(nc, name, freed="written") as ph:
        pay = ph.sb("pay", [P, J, words])
        dig = ph.sb("dig", [P, J])
        key_i = ph.sb("key_i", [P, J], I32)
        onehot = ph.sb("onehot", [P, SLOTS, GC, digits], F16)
        digs = ph.sb("digs", [P, SLOTS, GC])
        place = ph.sb("place", [P, SLOTS, GC])
        place_i = ph.sb("place_i", [P, SLOTS, GC], I32)
        pay_s = ph.sb("pay_s", [P, SLOTS, GC, words])
        junk = ph.sb("junk", [P, 4, digits])
        hist = ph.sb("hist", [P, digits], F16)
        zero_h = ph.sb("zero_h", [P, P], F16)
        one_row = ph.sb("one_row", [P, digits])
        upto = ph.sb("upto", [P, digits])
        base = ph.sb("base", [P, digits])
        hist_ps = ph.ps("hist_ps", [P, 512])
        total_ps = ph.ps("total_ps", [P, 512])
        before_ps = ph.ps("before_ps", [P, 512])
        run_ps = [ph.ps(f"run_ps{q}", [P, 512]) for q in range(4)]
        loaded, digit_ready = ph.sem("loaded"), ph.sem("digit_ready")
        prepared, chain = ph.sem("prepared"), ph.sem("chain")
        digs_ready, hot_ready, hot_used = ph.sem("digs_ready"), ph.sem("hot_ready"), ph.sem("hot_used")
        hist_done, hist_read = ph.sem("hist_done"), ph.sem("hist_read")
        sums_done, base_ready = ph.sem("sums_done"), ph.sem("base_ready")
        digs2_ready, hot2_ready = ph.sem("digs2_ready"), ph.sem("hot2_ready")
        run_ready, ranked = ph.sem("run_ready"), ph.sem("ranked")
        placed, go = ph.sem("placed"), ph.sem("go")
        scattered, written = slot_sems(ph, "scattered", SLOTS), slot_sems(ph, "written", SLOTS)
        zeroed, zero_ready = ph.sem("zeroed"), ph.sem("zero_ready")
        n_zero = 0
        if zero_fill:
            zeros = ph.sb("zeros", [P, 8 * ROW])
        with nc.Block() as block:
            n_loads = load(block, ph, pay, loaded, prepared)

            @block.sync
            def _(sp):
                pass_on(sp, scattered, written)

            @block.scalar
            def _(act):
                ph.free_slots(act)
                n = 0
                if zero_fill:
                    act.wait_ge(zero_ready, 1)
                    for a in zero_fill:
                        flat = a.rearrange("(p n) d -> p (n d)", p=P)
                        step = 8 * a.shape[1]
                        for k in range(0, flat.shape[1], step):
                            act.dma_start(flat[:, k:k + step], zeros[:, 0:step]).then_inc(zeroed, 16)
                            n += 16
                    act.wait_ge(zeroed, n)

            @block.vector
            def _(dve):
                if zero_fill:
                    dve.memset(zeros[:, :], 0.0).then_inc(zero_ready, 1)
                dve.memset(zero_h[:, :], 0.0)
                dve.memset(one_row[:, :], 1.0)
                dve.sem_inc(hot_used, SLOTS)
                dve.sem_inc(ranked, 4)
                dve.memset(onehot[:, :], 0.0).then_inc(digit_ready, 1)
                dve.wait_ge(loaded, n_loads)
                dve.wait_ge(digit_ready, 1)
                dve.tensor_copy(key_i[:, :], pay[:, :, 0]).then_inc(chain, 1)
                dve.wait_ge(chain, 1)
                op, by = (ALU.logical_shift_right, LOW.bit_length() - 1) if high else (ALU.bitwise_and, LOW - 1)
                dve.tensor_scalar(key_i[:, :], key_i[:, :], by, None, op).then_inc(chain, 1)
                dve.wait_ge(chain, 2)
                dve.tensor_copy(dig[:, :], key_i[:, :]).then_inc(chain, 1)
                dve.wait_ge(chain, 3)

                def hot(turn, s, copied, made):
                    dve.tensor_copy(digs[:, s, :], dig[:, bass.ds(turn * TURN + s * GC, GC)]).then_inc(copied, 1)
                    dve.wait_ge(copied, turn * SLOTS + s + 1)
                    for k in range(GC):
                        ins = dve.tensor_scalar(onehot[:, s, k, :], keep.iota_h[:, 0:digits], digs[:, s, k:k + 1],
                                                None, ALU.is_equal)
                    ins.then_inc(made, 1)

                with dve.Fori(0, TURNS) as turn:
                    for s in range(SLOTS):
                        dve.wait_ge(hot_used, turn * SLOTS + s + 1)
                        hot(turn, s, digs_ready, hot_ready)
                dve.wait_ge(hist_done, 1)
                dve.tensor_copy(hist[:, :], hist_ps[:, 0:digits]).then_inc(hist_read, 1)
                dve.memset(onehot[:, SLOTS - 1, :, :], 0.0).then_inc(chain, 1)
                dve.wait_ge(sums_done, 1)
                dve.tensor_tensor_scan(upto[:, :], one_row[:, :], total_ps[:, 0:digits], 0.0, ALU.mult, ALU.add).then_inc(chain, 1)
                dve.wait_ge(chain, 5)
                dve.tensor_tensor(base[:, :], upto[:, :], total_ps[:, 0:digits], ALU.subtract).then_inc(chain, 1)
                dve.wait_ge(chain, 6)
                dve.tensor_tensor(base[:, :], base[:, :], before_ps[:, 0:digits], ALU.add).then_inc(base_ready, 1)
                with dve.Fori(0, TURNS) as turn:
                    for s in range(SLOTS):
                        hot(turn, s, digs2_ready, hot2_ready)
                        dve.wait_ge(hot2_ready, turn * SLOTS + s + 1)
                        for k in range(GC):
                            c = s * GC + k
                            dve.wait_ge(run_ready, turn * TURN + c + 1)
                            dve.tensor_tensor_reduce(junk[:, c % 4, :], onehot[:, s, k, :], run_ps[c % 4][:, 0:digits],
                                                     1.0, 0.0, ALU.mult, ALU.add, place[:, s, k:k + 1]).then_inc(ranked, 1)
                        free(dve, written, turn, s)
                        dve.wait_ge(ranked, turn * TURN + (s + 1) * GC + 4)
                        dve.tensor_copy(place_i[:, s, :], place[:, s, :]).then_inc(placed, 1)
                        dve.tensor_copy(pay_s[:, s, :, :], pay[:, bass.ds(turn * TURN + s * GC, GC), :]).then_inc(placed, 1)

            @block.tensor
            def _(pe):
                pe.wait_ge(digit_ready, 1)
                pe.matmul(hist_ps[:, 0:digits], zero_h[:, :], keep.iota_h[:, 0:digits], start=True, stop=False,
                          skip_group_check=True)
                with pe.Fori(0, TURNS) as turn:
                    for s in range(SLOTS):
                        pe.wait_ge(hot_ready, turn * SLOTS + s + 1)
                        for k in range(GC):
                            ins = pe.matmul(hist_ps[:, 0:digits], keep.ident_h[:, :], onehot[:, s, k, :],
                                            start=False, stop=False, skip_group_check=True)
                        ins.then_inc(hot_used, 1)
                pe.matmul(hist_ps[:, 0:digits], zero_h[:, :], keep.iota_h[:, 0:digits], start=False, stop=True,
                          skip_group_check=True).then_inc(hist_done, 1)
                pe.wait_ge(hist_read, 1)
                pe.matmul(total_ps[:, 0:digits], keep.ones_h[:, :], hist[:, :], start=True, stop=True)
                pe.matmul(before_ps[:, 0:digits], keep.tri_h[:, :], hist[:, :], start=True, stop=True).then_inc(sums_done, 1)
                pe.wait_ge(base_ready, 1)
                for q in range(4):
                    pe.matmul(run_ps[q][:, 0:digits], keep.ident[:, :], base[:, :], start=True, stop=False,
                              skip_group_check=True)
                with pe.Fori(0, TURNS) as turn:
                    for c in range(TURN):
                        if c % GC == 1:
                            pe.wait_ge(hot2_ready, turn * SLOTS + c // GC + 1)
                        pe.wait_ge(ranked, turn * TURN + c + 1)
                        for b in range(c - 4, c):
                            b = b % TURN
                            ins = pe.matmul(run_ps[c % 4][:, 0:digits], keep.ident_h[:, :], onehot[:, b // GC, b % GC, :],
                                            start=False, stop=False, skip_group_check=True)
                        ins.then_inc(run_ready, 1)

            @block.gpsimd
            def _(pool):
                with pool.Fori(0, TURNS) as turn:
                    for s in range(SLOTS):
                        pool.wait_ge(placed, turn * (2 * SLOTS) + 2 * s + 2)
                        pool.sem_inc(go, 1)
                        for k in range(GC):
                            pool.indirect_dma_start(
                                out=target, out_offset=bass.IndirectOffsetOnAxis(ap=place_i[:, s, k:k + 1], axis=0),
                                in_=pay_s[:, s, k, :], in_offset=None).then_inc(scattered[s], 16)
                for s in range(SLOTS):
                    done(pool, scattered, TURNS - 1, s, 16 * GC)


def load_edges(nc, src, dst, attr):
    def load(block, ph, pay, loaded, prepared):
        ends = ph.sb("ends", [P, 2, J], I32)
        ends_in = ph.sem("ends_in")
        n = 16 if attr is not None else 0

        @block.sync
        def _(sp):
            keys = (dst, src) if attr is not None else (src, dst)
            for i, a in enumerate(keys):
                sp.dma_start(ends[:, i, :], a.rearrange("(p j) -> p j", p=P)).then_inc(ends_in, 16)
            if attr is not None:
                sp.wait_ge(prepared, 1)
                sp.dma_start(pay[:, :, 2:2 + ATT_IN], attr.rearrange("(p j) a -> p j a", p=P)).then_inc(loaded, 16)

        @block.gpsimd
        def _(pool):
            if attr is not None:
                pool.memset(pay[:, :, :], 1.0).then_inc(prepared, 1)
                pool.wait_ge(prepared, 1)
            pool.wait_ge(ends_in, 32)
            pool.tensor_copy(pay[:, :, 0], ends[:, 0, :]).then_inc(loaded, 1)
            pool.tensor_copy(pay[:, :, 1], ends[:, 1, :]).then_inc(loaded, 1)
        return n + 2
    return load


def load_sorted(rows):
    def load(block, ph, pay, loaded, prepared):
        @block.sync
        def _(sp):
            sp.dma_start(pay[:, :, :], rows.rearrange("(p j) w -> p j w", p=P)).then_inc(loaded, 16)
        return 16
    return load


def linked(engine, sem):
    n = [0]

    def link(ins):
        n[0] += 1
        ins.then_inc(sem, 1)
        engine.wait_ge(sem, n[0])
    return link


class Edges:
    pass


def edge_tables(nc, keep, name, rows, words, stack, full):
    e = Edges()

    def sb(n, shape, dt=F32):
        return stack.enter_context(nc.sbuf_tensor(f"{name}_{n}", shape, dt))

    e.other_i = sb("other_i", [P, J], I32)
    e.put_i = sb("put_i", [P, J], I32)
    e.fix_i = sb("fix_i", [P, 1], I32)
    e.cont = sb("cont", [P, J])
    e.carry = sb("carry", [P, P])
    if full:
        e.key_i = sb("key_i", [P, J], I32)
        e.att = sb("att", [P, J, ATT_IN + 1])
        e.cont_h = sb("cont_h", [P, HEADS, J])
        e.reset_h = sb("reset_h", [P, HEADS, J])
        e.end_h = sb("end_h", [P, HEADS, J])
        e.next_h = sb("next_h", [P, HEADS, J])
        e.same = [sb(f"same{t}", [P, 2, P]) for t in range(2)]
        e.same_add = [sb(f"same_add{t}", [P, 2, P]) for t in range(2)]
        e.in_add = [sb(f"in_add{t}", [P, J]) for t in range(2)]
        e.split = sb("split", [P, 1])
        e.deg, e.rdeg = sb("deg", [P, J]), sb("rdeg", [P, J])
    with Phase(nc, name + "t") as ph:
        key, other = ph.sb("key", [P, J]), ph.sb("other", [P, J])
        after, before = ph.sb("after", [P, 1]), ph.sb("before", [P, 1])
        tmp, end = ph.sb("tmp", [P, J]), ph.sb("end", [P, J])
        diag, off = ph.sb("diag", [P, 2, P]), ph.sb("off", [P, P])
        goes_on, whole, owns = ph.sb("goes_on", [P, 1]), ph.sb("whole", [P, 1]), ph.sb("owns", [P, 1])
        fix = ph.sb("fix", [P, 1])
        spread = ph.ps("spread", [P, 2, P])
        loaded, chain, preset = ph.sem("loaded"), ph.sem("chain"), ph.sem("preset")
        diag_ready, spread_done = ph.sem("diag_ready"), ph.sem("spread_done")
        view = rows.rearrange("(p j) w -> p j w", p=P)
        with nc.Block() as block, nc.allow_non_contiguous_dma(reason="one word of an edge's payload"):
            @block.sync
            def _(sp):
                sp.dma_start(key[:, :], view[:, :, 0]).then_inc(loaded, 16)
                sp.dma_start(other[:, :], view[:, :, 1]).then_inc(loaded, 16)
                sp.wait_ge(preset, 2)
                sp.dma_start(after[0:P - 1, :], view[1:P, 0, 0:1]).then_inc(loaded, 16)
                sp.dma_start(before[1:P, :], view[0:P - 1, J - 1, 0:1]).then_inc(loaded, 16)
                if full:
                    sp.dma_start(e.att[:, :, :], view[:, :, 2:WD]).then_inc(loaded, 16)

            @block.vector
            def _(dve):
                link = linked(dve, chain)
                dve.memset(after[:, :], -1.0).then_inc(preset, 1)
                dve.memset(before[:, :], -1.0).then_inc(preset, 1)
                link(dve.memset(e.cont[:, :], 0.0))
                link(dve.memset(end[:, :], 1.0))
                link(dve.tensor_scalar(off[:, :], keep.ident[:, :], -1.0, 1.0, ALU.mult, ALU.add))
                dve.wait_ge(loaded, 80 if full else 64)
                first, last = key[:, 0:1], key[:, J - 1:J]
                link(dve.tensor_copy(e.other_i[:, :], other[:, :]))
                link(dve.tensor_tensor(e.cont[:, 1:J], key[:, 1:J], key[:, 0:J - 1], ALU.is_equal))
                link(dve.tensor_scalar(end[:, 0:J - 1], e.cont[:, 1:J], -1.0, 1.0, ALU.mult, ALU.add))
                if full:
                    link(dve.tensor_copy(e.key_i[:, :], key[:, :]))
                    for h in range(HEADS):
                        dve.tensor_copy(e.cont_h[:, h, :], e.cont[:, :])
                        dve.tensor_copy(e.end_h[:, h, :], end[:, :])
                        dve.tensor_scalar(e.next_h[:, h, :], end[:, :], -1.0, 1.0, ALU.mult, ALU.add)
                        link(dve.tensor_scalar(e.reset_h[:, h, :], e.cont[:, :], -1.0, BIG, ALU.add, ALU.mult))
                link(dve.tensor_tensor(goes_on[:, :], last, after[:, :], ALU.is_equal))
                link(dve.tensor_scalar(end[:, J - 1:J], goes_on[:, :], -1.0, 1.0, ALU.mult, ALU.add))
                link(dve.tensor_scalar(tmp[:, :], end[:, :], -FAR, FAR, ALU.mult, ALU.add))
                link(dve.tensor_tensor(tmp[:, :], tmp[:, :], key[:, :], ALU.add))
                link(dve.tensor_copy(e.put_i[:, :], tmp[:, :]))
                link(dve.tensor_tensor(whole[:, :], first, last, ALU.is_equal))
                link(dve.tensor_tensor(owns[:, :], whole[:, :], goes_on[:, :], ALU.mult))
                link(dve.tensor_scalar(owns[:, :], owns[:, :], -1.0, 1.0, ALU.mult, ALU.add))
                link(dve.tensor_tensor(fix[:, :], first, before[:, :], ALU.is_equal))
                link(dve.tensor_tensor(fix[:, :], fix[:, :], owns[:, :], ALU.mult))
                link(dve.tensor_scalar(fix[:, :], fix[:, :], -FAR, FAR, ALU.mult, ALU.add))
                link(dve.tensor_tensor(fix[:, :], fix[:, :], first, ALU.add))
                link(dve.tensor_copy(e.fix_i[:, :], fix[:, :]))
                dve.tensor_scalar(diag[:, 0, :], keep.ident[:, :], last, None, ALU.mult).then_inc(diag_ready, 1)
                dve.tensor_scalar(diag[:, 1, :], keep.ident[:, :], first, None, ALU.mult).then_inc(diag_ready, 1)
                dve.wait_ge(spread_done, 1)
                link(dve.tensor_scalar(e.carry[:, :], spread[:, 1, :], last, None, ALU.is_equal))
                link(dve.tensor_tensor(e.carry[:, :], e.carry[:, :], off[:, :], ALU.mult))
                if full:
                    for t, mine in enumerate((first, last)):
                        link(dve.tensor_scalar(e.same[t][:, :, :], spread[:, :, :], mine, None, ALU.is_equal))
                        link(dve.tensor_scalar(e.same_add[t][:, :, :], e.same[t][:, :, :], -1.0, BIG, ALU.add, ALU.mult))
                        link(dve.tensor_scalar(e.in_add[t][:, :], key[:, :], mine, None, ALU.is_equal))
                        link(dve.tensor_scalar(e.in_add[t][:, :], e.in_add[t][:, :], -1.0, BIG, ALU.add, ALU.mult))
                    link(dve.tensor_scalar(e.split[:, :], whole[:, :], -1.0, 1.0, ALU.mult, ALU.add))

            @block.tensor
            def _(pe):
                pe.wait_ge(diag_ready, 2)
                pe.matmul(spread[:, :, :], keep.ones[:, :], diag[:, :, :], start=True, stop=True).then_inc(spread_done, 1)
    return e


def spread_ends(pe, keep, heads, diag, spread_ps, diag_ready, spread_done, n):
    pe.wait_ge(diag_ready, n)
    pe.matmul(spread_ps[0][:, 0:heads * P], keep.ones[:, :], diag[:, 0, 0:heads, :], start=True, stop=True)
    pe.matmul(spread_ps[1][:, 0:heads * P], keep.ones[:, :], diag[:, 1, 0:heads, :], start=True, stop=True)\
        .then_inc(spread_done, 1)


def key_reduce(dve, link, keep, e, kind, heads, values, out, run, diag, cand, whole, ends, spread_ps, diag_ready,
               spread_done, n):
    def flat(a):
        return a[:, 0:heads, :].rearrange("p h j -> p (h j)")

    if kind == "max":
        link(dve.tensor_tensor_scan(flat(run), flat(e.reset_h), flat(values), -BIG, ALU.add, ALU.max))
    else:
        link(dve.tensor_tensor_scan(flat(run), flat(e.cont_h), flat(values), 0.0, ALU.mult, ALU.add))
    link(dve.tensor_tensor(flat(run), flat(run), flat(e.end_h), ALU.mult))
    link(dve.tensor_tensor_scan(flat(out)[:, ::-1], flat(e.next_h)[:, ::-1], flat(run)[:, ::-1], 0.0, ALU.mult, ALU.add))
    link(dve.tensor_copy(ends[:, 0, 0:heads], out[:, 0:heads, J - 1]))
    if kind == "max":
        link(dve.tensor_copy(ends[:, 1, 0:heads], out[:, 0:heads, 0]))
    else:
        link(dve.tensor_scalar(ends[:, 1, 0:heads], out[:, 0:heads, 0], e.split[:, 0:1], None, ALU.mult))
    for t in range(2):
        for h in range(heads):
            dve.tensor_scalar(diag[:, t, h, :], keep.ident[:, :], ends[:, t, h:h + 1], None, ALU.mult)\
                .then_inc(diag_ready, 1)
    dve.wait_ge(spread_done, n)
    for t in range(2):
        for u in range(2):
            mask = (e.same_add if kind == "max" else e.same)[t][:, u, :].unsqueeze(1).broadcast_to([P, heads, P])
            link(dve.tensor_tensor(cand[:, 0:heads, u, :], spread_ps[u][:, 0:heads * P].rearrange("p (h q) -> p h q", h=heads),
                                   mask, ALU.add if kind == "max" else ALU.mult))
        link(dve.tensor_reduce(whole[:, 0:heads], cand[:, 0:heads, :, :], AX.XY, ALU.max if kind == "max" else ALU.add))
        for h in range(heads):
            link(dve.scalar_tensor_tensor(out[:, h, :], e.in_add[t][:, :], whole[:, h:h + 1], out[:, h, :], ALU.add, ALU.max))


def reduce_memory(ph, heads):
    run, diag = ph.sb("run", [P, heads, J]), ph.sb("diag", [P, 2, heads, P])
    cand, whole, ends = ph.sb("cand", [P, heads, 2, P]), ph.sb("whole", [P, heads]), ph.sb("ends", [P, 2, heads])
    spread_ps = [ph.ps(f"spread_ps{t}", [P, 512]) for t in range(2)]
    return run, diag, cand, whole, ends, spread_ps, ph.sem("diag_ready"), ph.sem("spread_done")


def degrees(nc, keep, e):
    with Phase(nc, "deg") as ph:
        mem = reduce_memory(ph, 1)
        ones = ph.sb("ones", [P, 1, J])
        chain = ph.sem("chain")
        with nc.Block() as block:
            @block.vector
            def _(dve):
                link = linked(dve, chain)
                link(dve.memset(ones[:, :, :], 1.0))
                key_reduce(dve, link, keep, e, "sum", 1, ones, e.deg[:, :].unsqueeze(1), *mem, 1)
                link(dve.tensor_scalar(e.rdeg[:, :], e.deg[:, :], 1.0, None, ALU.max))
                link(dve.reciprocal(e.rdeg[:, :], e.rdeg[:, :]))

            @block.tensor
            def _(pe):
                spread_ends(pe, keep, 1, mem[1], mem[5], mem[6], mem[7], 2)


def edge_sum(nc, keep, name, e, agg, prepare, table=None, fetched=0):
    out_width = agg.shape[1]
    with Phase(nc, name, freed="written") as ph:
        msg = ph.sb("msg", [P, SLOTS, GC, ROW])
        get_s = ph.sb("get_s", [P, SLOTS, GC], I32)
        put_s = ph.sb("put_s", [P, SLOTS, GC], I32)
        fixed = ph.sb("fixed", [P, ROW])
        carry_ps = ph.ps("carry_ps", [P, 512])
        cleared, staged, go = ph.sem("cleared"), ph.sem("staged"), ph.sem("go")
        gathered = slot_sems(ph, "gathered", SLOTS)
        scattered, written = slot_sems(ph, "scattered", SLOTS), slot_sems(ph, "written", SLOTS)
        step, summed = ph.sem("step"), ph.sem("summed")
        carried, fix_in, fix_done, fix_out = ph.sem("carried"), ph.sem("fix_in"), ph.sem("fix_done"), ph.sem("fix_out")
        with nc.Block() as block:

            @block.scalar
            def _(act):
                ph.free_slots(act)

            @block.sync
            def _(sp):
                pass_on(sp, scattered, written)

            prepare.start(block, ph)

            @block.gpsimd
            def _(pool):
                bound = pool.to_reg(NPAD - 1)
                pool.wait_ge(cleared, 2)

                def stage(turn, s, of, to, n):
                    pool.tensor_copy(to[:, s, :], of[:, bass.ds(turn * TURN + s * GC, GC)]).then_inc(staged, 1)
                    pool.wait_ge(staged, n)

                def gather(turn, s, n):
                    free(pool, written, turn, s)
                    stage(turn, s, e.other_i, get_s, n)
                    pool.sem_inc(go, 1)
                    for k in range(GC):
                        pool.indirect_dma_start(out=msg[:, s, k, 0:fetched], out_offset=None, in_=table,
                                                in_offset=bass.IndirectOffsetOnAxis(ap=get_s[:, s, k:k + 1], axis=0))\
                            .then_inc(gathered[s], 16)

                def scatter(turn, s, n):
                    pool.wait_ge(summed, turn * SLOTS + s + 1)
                    stage(turn, s, e.put_i, put_s, n)
                    pool.sem_inc(go, 1)
                    for k in range(GC):
                        pool.indirect_dma_start(out=agg, out_offset=bass.IndirectOffsetOnAxis(ap=put_s[:, s, k:k + 1], axis=0),
                                                in_=msg[:, s, k, 0:out_width], in_offset=None, bounds_check=bound,
                                                oob_is_err=False).then_inc(scattered[s], 16)

                if table is None:
                    with pool.Fori(0, TURNS) as turn:
                        for s in range(SLOTS):
                            scatter(turn, s, turn * SLOTS + s + 1)
                else:
                    gather(0, 0, 1)
                    gather(0, 1, 2)

                    def groups(turn, last):
                        for s in range(SLOTS):
                            n = turn * (2 * SLOTS) + 2 * s + 2
                            ahead = (s + 2) // SLOTS
                            more = not (last and ahead)
                            if more:
                                gather(turn + ahead, (s + 2) % SLOTS, n + 1)
                            scatter(turn, s, n + 2 if more else turn * (2 * SLOTS) + 6 + s - 1)

                    with pool.Fori(0, TURNS - 1) as turn:
                        groups(turn, False)
                    groups(TURNS - 1, True)
                for s in range(SLOTS):
                    done(pool, scattered, TURNS - 1, s, 16 * GC)
                pool.indirect_dma_start(out=fixed[:, 0:out_width], out_offset=None, in_=agg,
                                        in_offset=bass.IndirectOffsetOnAxis(ap=e.fix_i[:, 0:1], axis=0),
                                        bounds_check=bound, oob_is_err=False).then_inc(fix_in, 16)
                pool.wait_ge(fix_done, 1)
                pool.indirect_dma_start(out=agg, out_offset=bass.IndirectOffsetOnAxis(ap=e.fix_i[:, 0:1], axis=0),
                                        in_=fixed[:, 0:out_width], in_offset=None, bounds_check=bound,
                                        oob_is_err=False).then_inc(fix_out, 16)
                pool.wait_ge(fix_out, 16)

            @block.vector
            def _(dve):
                dve.memset(msg[:, :, :, :], 0.0).then_inc(cleared, 1)
                dve.memset(fixed[:, :], 0.0).then_inc(cleared, 1)
                dve.wait_ge(cleared, 1)
                per_turn = SLOTS * (GC + prepare.steps)
                with dve.Fori(0, TURNS) as turn:
                    n = 0
                    for s in range(SLOTS):
                        if table is None:
                            free(dve, written, turn, s)
                        else:
                            dve.wait_ge(gathered[s], turn * (16 * GC) + 16 * GC)
                        for ins in prepare(dve, turn, s, msg, lambda: dve.wait_ge(step, turn * per_turn + n)):
                            ins.then_inc(step, 1)
                            n += 1
                        for k in range(GC):
                            before = msg[:, s, k - 1, 0:D] if k else msg[:, (s - 1) % SLOTS, GC - 1, 0:D]
                            dve.wait_ge(step, turn * per_turn + n)
                            ins = dve.scalar_tensor_tensor(msg[:, s, k, 0:D], before,
                                                           e.cont[:, bass.ds(turn * TURN + s * GC + k, 1)],
                                                           msg[:, s, k, 0:D], ALU.mult, ALU.add)
                            ins.then_inc(step, 1)
                            n += 1
                        dve.wait_ge(step, turn * per_turn + n)
                        dve.sem_inc(summed, 1)
                    assert n == per_turn
                dve.wait_ge(carried, 1)
                dve.wait_ge(fix_in, 16)
                dve.tensor_tensor(fixed[:, 0:D], fixed[:, 0:D], carry_ps[:, 0:D], ALU.add).then_inc(fix_done, 1)

            @block.tensor
            def _(pe):
                pe.wait_ge(summed, TURNS * SLOTS)
                pe.matmul(carry_ps[:, 0:D], e.carry[:, :], msg[:, SLOTS - 1, GC - 1, 0:D], start=True, stop=True)\
                    .then_inc(carried, 1)


class PrepareMean:
    steps = 2

    def __init__(self, e):
        self.e = e

    def start(self, block, ph):
        pass

    def __call__(self, dve, turn, s, msg, settle):
        cols = bass.ds(turn * TURN + s * GC, GC)
        yield dve.tensor_tensor(msg[:, s, :, 0:D], msg[:, s, :, 0:D],
                                self.e.rdeg[:, cols].unsqueeze(2).broadcast_to([P, GC, D]), ALU.mult)
        yield dve.tensor_copy(msg[:, s, :, D], self.e.deg[:, cols])


class PrepareNorm:
    steps = 1

    def start(self, block, ph):
        pass

    def __call__(self, dve, turn, s, msg, settle):
        yield dve.tensor_tensor(msg[:, s, :, 0:D], msg[:, s, :, 0:D],
                                msg[:, s, :, D:D + 1].broadcast_to([P, GC, D]), ALU.mult)


class PrepareAttention:
    steps = 2

    def __init__(self, rows, weight, tail):
        self.rows, self.weight, self.tail = rows, weight, tail

    def start(self, block, ph):
        pass

    def __call__(self, dve, turn, s, msg, settle):
        cols = bass.ds(turn * TURN + s * GC, GC)
        yield dve.tensor_tensor(
            msg[:, s, :, 0:D].rearrange("p k (h d) -> p k h d", h=GAT_HEADS),
            self.rows[:, cols, 0:D].rearrange("p k (h d) -> p k h d", h=GAT_HEADS),
            self.weight[:, :, cols].rearrange("p h k -> p k h").unsqueeze(3).broadcast_to([P, GC, GAT_HEADS, GAT_D]), ALU.mult)
        yield dve.tensor_copy(msg[:, s, :, D:ROW], self.tail[:, :, cols].rearrange("p w k -> p k w"))


class PrepareGatv2:
    steps = HEADS * GC

    def __init__(self, keep, xt, wl, bl_parts, alpha):
        self.keep, self.xt, self.wl, self.bl_parts, self.alpha = keep, xt, wl, bl_parts, alpha

    def start(self, block, ph):
        xg = ph.sb("xg", [P, 2, GC, P])
        self.xl_ps = [ph.ps(f"xl_ps{q}", [P, HD]) for q in range(XL_BANKS)]
        copied = ph.sem("copied")
        self.xl_ready, self.used = ph.sem("xl_ready"), ph.sem("used")

        @block.scalar
        def _(act):
            def copy(turn, s):
                after(act, self.xl_ready, turn, s * GC, GC + 1, TURN)
                act.activation(xg[:, s % 2].rearrange("p k n -> p (k n)"),
                               self.xt[:, bass.ds((turn * TURN + s * GC) * P, GC * P)], ACT.Copy).then_inc(copied, 1)
            pipeline(act, (0, copy), per_turn=SLOTS, total=TURNS * SLOTS)

        @block.tensor
        def _(pe):
            def product(turn, c):
                s, k = c // GC, c % GC
                if k == 0:
                    pe.wait_ge(copied, turn * SLOTS + s + 1)
                after(pe, self.used, turn, c, XL_BANKS, TURN)
                pe.matmul(self.xl_ps[c % XL_BANKS][:, :], xg[:, s % 2, k, :], self.wl[:, :], start=True, stop=False)
                pe.matmul(self.xl_ps[c % XL_BANKS][:, :], self.keep.ones_b[0:3, :], self.bl_parts[0:3, :],
                          start=False, stop=True).then_inc(self.xl_ready, 1)
            pipeline(pe, (0, product), per_turn=TURN, total=J)

    def __call__(self, dve, turn, s, msg, settle):
        for k in range(GC):
            c = s * GC + k
            col = bass.ds(turn * TURN + c, 1)
            dve.wait_ge(self.xl_ready, turn * TURN + c + 1)
            for h in range(HEADS):
                part, weight = self.xl_ps[c % XL_BANKS][:, h * D:(h + 1) * D], self.alpha[:, h, col]
                if h == 0:
                    yield dve.tensor_scalar(msg[:, s, k, 0:D], part, weight, None, ALU.mult)
                else:
                    settle()
                    yield dve.scalar_tensor_tensor(msg[:, s, k, 0:D], part, weight, msg[:, s, k, 0:D], ALU.mult, ALU.add)
            settle()
            dve.sem_inc(self.used, 1)


XL_BANKS = 4
GAT_HEADS, GAT_D = 2, D // 2


def after(engine, sem, turn, place, lag, per_turn):
    n = turn * per_turn + place + 1 - lag
    if not isinstance(n, int) or n > 0:
        engine.wait_ge(sem, n)


class Steps:

    def __init__(self, engine, sem, turn, per_turn):
        self.engine, self.sem, self.first, self.per_turn, self.n = engine, sem, turn * per_turn, per_turn, 0

    def __call__(self, ins):
        ins.then_inc(self.sem, 1)
        self.n += 1

    def wait(self):
        self.engine.wait_ge(self.sem, self.first + self.n)



LN_EPS = 1e-05
BANKS = 2
NTURN = NB // SLOT


def norm_sums(dve, aside, r, stats, mv, done):
    for g in range(GB):
        ins = dve.bn_stats(stats[:, g, :], r[:, g, :])
    aside(ins)
    aside.wait()
    dve.sem_inc(aside.sem, 1)
    aside.n += 1
    for g in range(GB):
        ins = dve.bn_aggr(mv[:, g, :], stats[:, g, :])
    ins.then_inc(done, 1)


NORM_STEPS = 2


def norm_scale(pool, keep, st, mv, rstd, done):
    st(pool.tensor_tensor(rstd, mv[:, :, 1], keep.eps[:, :], ALU.add))
    st.wait()
    pool.tensor_tensor(rstd, rstd, keep.minus_half[:, :], ALU.pow).then_inc(done, 1)


def norm_shift(pool, keep, st, mv, rstd, shift, done):
    st(pool.tensor_tensor(rstd, mv[:, :, 1], keep.eps[:, :], ALU.add))
    st.wait()
    st(pool.tensor_tensor(rstd, rstd, keep.minus_half[:, :], ALU.pow))
    st.wait()
    st(pool.tensor_tensor(shift, mv[:, :, 0], rstd, ALU.mult))
    st.wait()
    pool.tensor_tensor(shift, shift, keep.minus_one[:, :], ALU.mult).then_inc(done, 1)


SHIFT_STEPS = 3


def norm_act(act, r, rstd, shift, out):
    for g in range(GB):
        ins = act.activation(out[:, g, 0:D], r[:, g, :], ACT.Identity, bias=shift[:, g:g + 1], scale=rstd[:, g:g + 1])
    return ins


def norm_apply(dve, r, mv, rstd, out):
    for g in range(GB):
        ins = dve.tensor_scalar(out[:, g, 0:D], r[:, g, :], mv[:, g, 0:1], rstd[:, g:g + 1], ALU.subtract, ALU.mult)
    return ins


def block_rows(a, turn, s):
    return a.rearrange("(t s p g) d -> t s p g d", s=SLOT, p=P, g=GB)[turn, s] if isinstance(turn, int) else \
        a.rearrange("(t s p g) d -> t s p g d", s=SLOT, p=P, g=GB)[bass.ds(turn, 1), s].squeeze(0)


def pipeline(engine, *stages, per_turn=SLOT, total=NB):
    first = max(1, -(-max(lag for lag, _ in stages) // per_turn))

    def steps(turn, peeled):
        for s in range(per_turn):
            for lag, fn in stages:
                if not peeled or 0 <= turn * per_turn + s - lag < total:
                    fn(turn + (s - lag) // per_turn, (s - lag) % per_turn)

    for turn in range(first):
        steps(turn, True)
    with engine.Fori(first, total // per_turn) as turn:
        steps(turn, False)
    for turn in range(total // per_turn, total // per_turn + first):
        steps(turn, True)


def node_sage(nc, keep, x, agg, w, bias, x1):
    with Phase(nc, "n0", freed="turned added stored y_ready") as ph:
        wa, wb, b = ph.sb("wa", [P, D]), ph.sb("wb", [P, D]), ph.sb("b", [P, D])
        xs, ag = ph.sb("xs", [P, SLOT, GB, D]), ph.sb("ag", [P, SLOT, GB, ROW])
        xb, r = ph.sb("xb", [P, SLOT, GB, D]), ph.sb("r", [P, SLOT, GB, D])
        o = ph.sb("o", [P, SLOT, GB, ROW])
        xt, at = ph.sb("xt", [P, SLOT, GB, P]), ph.sb("at", [P, SLOT, GB, P])
        stats, mv, rstd = ph.sb("stats", [P, SLOT, GB, 6]), ph.sb("mv", [P, SLOT, GB, 2]), ph.sb("rstd", [P, SLOT, GB])
        xt_ps = [ph.ps(f"xt_ps{q}", [P, GB, P]) for q in range(BANKS)]
        at_ps = [ph.ps(f"at_ps{q}", [P, GB, P]) for q in range(BANKS)]
        y_ps = [ph.ps(f"y_ps{q}", [P, GB, D]) for q in range(BANKS)]
        weights, added = ph.sem("weights"), slot_sems(ph, "added")
        x_in, ag_in = slot_sems(ph, "x_in"), slot_sems(ph, "ag_in")
        stored = slot_sems(ph, "stored")
        turned, moved, y_ready, x1_ready, steps = (
            slot_sems(ph, "turned"), slot_sems(ph, "moved"), slot_sems(ph, "y_ready"), slot_sems(ph, "x1_ready"), ph.sem("steps"))
        sums_ready, rstd_ready, cleared, pool_step, norm_step = (
            slot_sems(ph, "sums_ready"), slot_sems(ph, "rstd_ready"), ph.sem("cleared"), ph.sem("pool_step"), ph.sem("norm_step"))
        with nc.Block() as block:
            @block.sync
            def _(sp):
                sp.dma_start(wa[:, :], w[0:D, :]).then_inc(weights, 16)
                sp.dma_start(wb[:, :], w[D:2 * D, :]).then_inc(weights, 16)
                sp.dma_start(b[:, :], bias.partition_broadcast(P)).then_inc(weights, 16)
                with sp.Fori(0, NTURN) as turn:
                    used = sp.snap(turn + 1)
                    for s in range(SLOT):
                        sp.wait_ge(added[s], used)
                        sp.wait_ge(turned[s], used)
                        sp.dma_start(xs[:, s], block_rows(x, turn, s)).then_inc(x_in[s], 16)
                        sp.dma_start(ag[:, s], block_rows(agg, turn, s)).then_inc(ag_in[s], 16)

            @block.gpsimd
            def _(pool):
                pool.wait_ge(weights, 48)
                pool.wait_ge(cleared, 1)

                def add_bias(turn, s):
                    st = Steps(pool, pool_step, turn * SLOT + s, 1)
                    done(pool, x_in, turn, s, 16)
                    pool.tensor_tensor(xb[:, s], xs[:, s], b[:, :].unsqueeze(1).broadcast_to([P, GB, D]), ALU.add)
                    done(pool, ag_in, turn, s, 16)
                    free(pool, stored, turn, s, 16)
                    st(pool.tensor_tensor(o[:, s, :, D], ag[:, s, :, D], keep.ones[:, 0:GB], ALU.add))
                    st.wait()
                    pool.tensor_tensor(o[:, s, :, D], o[:, s, :, D], keep.minus_half[:, :], ALU.pow).then_inc(added[s], 1)

                def scale(turn, s):
                    done(pool, sums_ready, turn, s)
                    st = Steps(pool, norm_step, turn * SLOT + s, 1)
                    norm_scale(pool, keep, st, mv[:, s], rstd[:, s, :], rstd_ready[s])

                pipeline(pool, (3, scale), (0, add_bias))

            @block.tensor
            def _(pe):
                pe.wait_ge(weights, 48)

                def turn_over(turn, s):
                    done(pe, x_in, turn, s, 16)
                    done(pe, ag_in, turn, s, 16)
                    bank_free(pe, moved, turn, s, 2, BANKS)
                    for g in range(GB):
                        pe.transpose(xt_ps[s % BANKS][:, g, :], xs[:, s, g, :], keep.ident[:, :])
                    for g in range(GB):
                        ins = pe.transpose(at_ps[s % BANKS][:, g, :], ag[:, s, g, 0:D], keep.ident[:, :])
                    ins.then_inc(turned[s], 1)

                def product(turn, s):
                    done(pe, moved, turn, s, 2)
                    bank_free(pe, sums_ready, turn, s, 1, BANKS)
                    for g in range(GB):
                        pe.matmul(y_ps[s % BANKS][:, g, :], xt[:, s, g, :], wa[:, :], start=True, stop=False)
                        ins = pe.matmul(y_ps[s % BANKS][:, g, :], at[:, s, g, :], wb[:, :], start=False, stop=True)
                    ins.then_inc(y_ready[s], 1)

                pipeline(pe, (2, product), (0, turn_over))

            @block.scalar
            def _(act):
                ph.free_slots(act)
                def store(turn, s):
                    done(act, x1_ready, turn, s)
                    act.dma_start(block_rows(x1, turn, s), o[:, s]).then_inc(stored[s], 16)

                def move(turn, s):
                    done(act, turned, turn, s)
                    free(act, y_ready, turn, s)
                    act.activation(xt[:, s], xt_ps[s % BANKS][:, :, :], ACT.Copy).then_inc(moved[s], 1)
                    act.activation(at[:, s], at_ps[s % BANKS][:, :, :], ACT.Copy).then_inc(moved[s], 1)

                pipeline(act, (5, store), (0, move))
                for s in range(SLOT):
                    done(act, stored, NTURN - 1, s, 16)

            @block.vector
            def _(dve):
                dve.memset(o[:, :, :, :], 0.0).then_inc(cleared, 1)

                def sums(turn, s):
                    st = Steps(dve, steps, turn * SLOT + s, NORM_STEPS + 1)
                    done(dve, y_ready, turn, s)
                    done(dve, added, turn, s)
                    st(dve.tensor_tensor(r[:, s], y_ps[s % BANKS][:, :, :], xb[:, s], ALU.add))
                    st.wait()
                    norm_sums(dve, st, r[:, s], stats[:, s], mv[:, s], sums_ready[s])

                def apply(turn, s):
                    done(dve, rstd_ready, turn, s)
                    norm_apply(dve, r[:, s], mv[:, s], rstd[:, s], o[:, s]).then_inc(x1_ready[s], 1)

                pipeline(dve, (4, apply), (2, sums))


def node_gcn(nc, keep, name, z, agg, w, beta, out, x1=None):
    with Phase(nc, name, freed="scaled xp_ready turned y_ready sums_ready stored") as ph:
        wm = ph.sb("wm", [P, D])
        zs, ag = ph.sb("zs", [P, SLOT, GB, ROW]), ph.sb("ag", [P, SLOT, GB, D])
        t, c1, c2 = ph.sb("t", [P, SLOT, GB, D]), ph.sb("c1", [P, SLOT, GB]), ph.sb("c2", [P, SLOT, GB])
        xp, xt = ph.sb("xp", [P, SLOT, GB, D]), ph.sb("xt", [P, SLOT, GB, P])
        width = out.shape[1]
        o = ph.sb("o", [P, SLOT, GB, width])
        xr = ph.sb("xr", [P, SLOT, GB, ROW]) if x1 is not None else None
        r = ph.sb("r", [P, SLOT, GB, D])
        stats, mv, rstd = ph.sb("stats", [P, SLOT, GB, 6]), ph.sb("mv", [P, SLOT, GB, 2]), ph.sb("rstd", [P, SLOT, GB])
        t_ps = [ph.ps(f"t_ps{q}", [P, GB, P]) for q in range(BANKS)]
        y_ps = [ph.ps(f"y_ps{q}", [P, GB, D]) for q in range(BANKS)]
        shift, own_ready = ph.sb("shift", [P, SLOT, GB]), slot_sems(ph, "own_ready")
        weights, mixed, w_ready = ph.sem("weights"), ph.sem("mixed"), ph.sem("w_ready")
        z_in = slot_sems(ph, "z_in")
        ag_in = slot_sems(ph, "ag_in")
        r_in = slot_sems(ph, "r_in")
        stored = slot_sems(ph, "stored")
        pstep, scaled, xp_ready, turned, moved, y_ready, out_ready, steps = (
            ph.sem("pstep"), slot_sems(ph, "scaled"), slot_sems(ph, "xp_ready"), slot_sems(ph, "turned"), slot_sems(ph, "moved"),
            slot_sems(ph, "y_ready"), slot_sems(ph, "out_ready"), ph.sem("steps"))
        sums_ready, rstd_ready, pool_step = slot_sems(ph, "sums_ready"), slot_sems(ph, "rstd_ready"), ph.sem("pool_step")
        last = x1 is not None
        with nc.Block() as block:
            @block.sync
            def _(sp):
                sp.dma_start(wm[:, :], w).then_inc(weights, 16)
                with sp.Fori(0, NTURN) as turn:
                    used = sp.snap(turn + 1)
                    for s in range(SLOT):
                        sp.wait_ge(scaled[s], used)
                        sp.wait_ge(xp_ready[s], used)
                        sp.dma_start(zs[:, s], block_rows(z, turn, s)).then_inc(z_in[s], 16)
                        sp.dma_start(ag[:, s], block_rows(agg, turn, s)).then_inc(ag_in[s], 16)
                        if last:
                            sp.wait_ge(sums_ready[s], used)
                            sp.dma_start(xr[:, s], block_rows(x1, turn, s)).then_inc(r_in[s], 16)

            @block.gpsimd
            def _(pool):
                def scale(turn, s):
                    st = Steps(pool, pstep, turn * SLOT + s, 4 if last else 5)
                    done(pool, z_in, turn, s, 16)
                    free(pool, xp_ready, turn, s)
                    pool.sem_inc(pstep, 1)
                    st.n += 1
                    if not last:
                        free(pool, stored, turn, s, 16)
                        st(pool.tensor_tensor(o[:, s, :, D:ROW], zs[:, s, :, D:ROW],
                                              keep.ones[:, 0:GB * (ROW - D)].rearrange("p (g w) -> p g w", g=GB), ALU.mult))
                    st(pool.tensor_scalar(c1[:, s, :], zs[:, s, :, D], 0.9, None, ALU.mult))
                    st.wait()
                    st(pool.tensor_tensor(c2[:, s, :], c1[:, s, :], zs[:, s, :, D], ALU.mult))
                    st.wait()
                    pool.sem_inc(pstep, 1)
                    st.n += 1
                    pool.tensor_scalar(c2[:, s, :], c2[:, s, :], 0.1, None, ALU.add).then_inc(scaled[s], 1)

                def deviation(turn, s):
                    done(pool, sums_ready, turn, s)
                    norm_shift(pool, keep, Steps(pool, pool_step, turn * SLOT + s, SHIFT_STEPS), mv[:, s], rstd[:, s, :],
                               shift[:, s, :], rstd_ready[s])

                pipeline(pool, *([(3, deviation)] if last else []), (0, scale))

            @block.tensor
            def _(pe):
                pe.wait_ge(w_ready, 1)

                def turn_over(turn, s):
                    done(pe, xp_ready, turn, s)
                    bank_free(pe, moved, turn, s, 1, BANKS)
                    for g in range(GB):
                        ins = pe.transpose(t_ps[s % BANKS][:, g, :], xp[:, s, g, :], keep.ident[:, :])
                    ins.then_inc(turned[s], 1)

                def product(turn, s):
                    done(pe, moved, turn, s)
                    bank_free(pe, sums_ready if last else out_ready, turn, s, 1, BANKS)
                    for g in range(GB):
                        ins = pe.matmul(y_ps[s % BANKS][:, g, :], xt[:, s, g, :], wm[:, :], start=True, stop=True)
                    ins.then_inc(y_ready[s], 1)

                pipeline(pe, (2, product), (1, turn_over))

            @block.scalar
            def _(act):
                ph.free_slots(act)
                def own(turn, s):
                    done(act, scaled, turn, s)
                    free(act, xp_ready, turn, s)
                    for g in range(GB):
                        ins = act.activation(t[:, s, g, :], zs[:, s, g, 0:D], ACT.Copy, scale=c2[:, s, g:g + 1])
                    ins.then_inc(own_ready[s], 1)

                def apply(turn, s):
                    done(act, rstd_ready, turn, s)
                    free(act, stored, turn, s, 16)
                    norm_act(act, r[:, s], rstd[:, s], shift[:, s], o[:, s]).then_inc(out_ready[s], 1)

                def move(turn, s):
                    done(act, turned, turn, s)
                    free(act, y_ready, turn, s)
                    act.activation(xt[:, s], t_ps[s % BANKS][:, :, :], ACT.Copy).then_inc(moved[s], 1)

                def keep_z(turn, s):
                    done(act, y_ready, turn, s)
                    free(act, stored, turn, s, 16)
                    act.activation(o[:, s, :, 0:D], y_ps[s % BANKS][:, :, :], ACT.Copy).then_inc(out_ready[s], 1)

                def store(turn, s):
                    done(act, out_ready, turn, s)
                    act.dma_start(block_rows(out, turn, s), o[:, s]).then_inc(stored[s], 16)

                if last:
                    pipeline(act, (4, store), (3, apply), (0, own), (1, move))
                else:
                    pipeline(act, (3, store), (2, keep_z), (0, own), (1, move))
                for s in range(SLOT):
                    done(act, stored, NTURN - 1, s, 16)

            @block.vector
            def _(dve):
                dve.wait_ge(weights, 16)
                dve.tensor_scalar(r[:, 0, 0, :], keep.ident[:, :], 1.0 - beta, None, ALU.mult).then_inc(mixed, 1)
                dve.wait_ge(mixed, 1)
                dve.scalar_tensor_tensor(wm[:, :], wm[:, :], beta, r[:, 0, 0, :], ALU.mult, ALU.add).then_inc(w_ready, 1)
                dve.wait_ge(w_ready, 1)

                def mix(turn, s):
                    done(dve, own_ready, turn, s)
                    done(dve, ag_in, turn, s, 16)
                    free(dve, turned, turn, s)
                    for g in range(GB):
                        ins = dve.scalar_tensor_tensor(xp[:, s, g, :], ag[:, s, g, :], c1[:, s, g:g + 1], t[:, s, g, :],
                                                       ALU.mult, ALU.add)
                    ins.then_inc(xp_ready[s], 1)

                def sums(turn, s):
                    st = Steps(dve, steps, turn * SLOT + s, NORM_STEPS + 1)
                    done(dve, y_ready, turn, s)
                    done(dve, r_in, turn, s, 16)
                    st(dve.tensor_tensor(r[:, s], y_ps[s % BANKS][:, :, :], xr[:, s, :, 0:D], ALU.add))
                    st.wait()
                    norm_sums(dve, st, r[:, s], stats[:, s], mv[:, s], sums_ready[s])

                pipeline(dve, *([(2, sums)] if last else []), (0, mix))


def split_bf16(engine, link, value, rest, parts):
    link(engine.tensor_copy(parts[0], value))
    link(engine.tensor_tensor(rest, value, parts[0], ALU.subtract))
    link(engine.tensor_copy(parts[1], rest))
    link(engine.tensor_tensor(rest, rest, parts[1], ALU.subtract))
    link(engine.tensor_copy(parts[2], rest))


def gatv2_weights(nc, keep, stack, w):
    g = Keep()

    def sb(name, shape, dt=F32):
        return stack.enter_context(nc.sbuf_tensor(f"gat2_{name}", shape, dt))

    g.wl, g.wr, g.att = sb("wl", [P, HD]), sb("wr", [P, HD]), sb("att", [P, HD])
    g.edge, g.bl_parts = sb("edge", [ATT_IN + 1, HD]), sb("bl_parts", [3, HD], BF16)
    with Phase(nc, "g2w") as ph:
        both = ph.sb("both", [1, 3, HD])
        part = [ph.sb(f"part{i}", [1, HD], BF16) for i in range(3)]
        loaded, chain, summed, edge_in, spread = (ph.sem("loaded"), ph.sem("chain"), ph.sem("summed"), ph.sem("edge_in"),
                                                 ph.sem("spread"))
        with nc.Block() as block:
            @block.sync
            def _(sp):
                sp.dma_start(both[0:1, 0, :], w["bl"].unsqueeze(0)).then_inc(loaded, 16)
                sp.dma_start(both[0:1, 1, :], w["br"].unsqueeze(0)).then_inc(loaded, 16)
                sp.dma_start(g.wl[:, :], w["Wl"]).then_inc(edge_in, 16)
                sp.dma_start(g.wr[:, :], w["Wr"]).then_inc(edge_in, 16)
                sp.dma_start(g.att[:, :], w["att"].rearrange("h d -> (h d)").partition_broadcast(P)).then_inc(edge_in, 16)
                sp.dma_start(g.edge[0:ATT_IN, :], w["We"]).then_inc(edge_in, 16)
                sp.wait_ge(summed, 1)
                sp.dma_start(g.edge[ATT_IN:ATT_IN + 1, :], both[0:1, 2, :]).then_inc(spread, 16)
                for i in range(3):
                    sp.dma_start(g.bl_parts[i:i + 1, :], part[i][0:1, :]).then_inc(spread, 16)
                sp.wait_ge(edge_in, 64)
                sp.wait_ge(spread, 64)

            @block.vector
            def _(dve):
                link = linked(dve, chain)
                dve.wait_ge(loaded, 32)
                link(dve.tensor_tensor(both[0:1, 2, :], both[0:1, 0, :], both[0:1, 1, :], ALU.add))
                split_bf16(dve, link, both[0:1, 0, :], both[0:1, 1, :], [p[0:1, :] for p in part])
                dve.sem_inc(summed, 1)
    return g


def gatv2_logits(nc, keep, e, g, x, xt, logits):
    with Phase(nc, "lg", freed="turned") as ph:
        rows = ph.sb("rows", [P, SLOTS, GC, 2, D])
        get_s = ph.sb("get_s", [P, SLOTS, 2, GC], I32)
        att_s = ph.sb("att_s", [P, SLOTS, GC, ATT_IN + 1])
        tr = ph.sb("tr", [P, 2, 2, P])
        at = ph.sb("at", [ATT_IN + 1, 2, P])
        z = ph.sb("z", [P, 2, HD])
        junk = ph.sb("junk", [P, 2, HD])
        sums = ph.sb("sums", [P, 2, HEADS, GC])
        tr_ps = [ph.ps(f"tr_ps{q}", [P, 4, P]) for q in range(2)]
        at_ps = [ph.ps(f"at_ps{q}", [P, 512]) for q in range(2)]
        z_ps = [ph.ps(f"z_ps{q}", [P, HD]) for q in range(2)]
        gathered = slot_sems(ph, "gathered", SLOTS)
        turned = slot_sems(ph, "turned", SLOTS)
        staged, go, moved, moved_att, kept = ph.sem("staged"), ph.sem("go"), ph.sem("moved"), ph.sem("moved_att"), ph.sem("kept")
        z_low = ph.sem("z_low")
        z_ready, z_out, scored, grouped, stage_go = (ph.sem("z_ready"), ph.sem("z_out"), ph.sem("scored"), ph.sem("grouped"), ph.sem("stage_go"))
        with nc.Block() as block:
            @block.gpsimd
            def _(pool):
                with pool.Fori(0, TURNS) as turn:
                    for s in range(SLOTS):
                        free(pool, turned, turn, s, GC)
                        cols = bass.ds(turn * TURN + s * GC, GC)
                        pool.sem_inc(stage_go, 1)
                        pool.tensor_copy(get_s[:, s, 0, :], e.other_i[:, cols]).then_inc(staged, 1)
                        pool.tensor_copy(get_s[:, s, 1, :], e.key_i[:, cols]).then_inc(staged, 1)
                        pool.tensor_copy(att_s[:, s], e.att[:, cols, :]).then_inc(staged, 1)
                        pool.wait_ge(staged, turn * (3 * SLOTS) + 3 * s + 3)
                        pool.sem_inc(go, 1)
                        for k in range(GC):
                            for i in range(2):
                                pool.indirect_dma_start(out=rows[:, s, k, i, :], out_offset=None, in_=x,
                                                        in_offset=bass.IndirectOffsetOnAxis(ap=get_s[:, s, i, k:k + 1], axis=0))\
                                    .then_inc(gathered[s], 16)

            @block.tensor
            def _(pe):
                def turn_over(turn, c):
                    s, k, q = c // GC, c % GC, c % 2
                    if k == 0:
                        pe.wait_ge(gathered[s], turn * (32 * GC) + 32 * GC)
                        pe.wait_ge(staged, turn * (3 * SLOTS) + 3 * s + 3)
                    after(pe, moved, turn, c, 2, TURN)
                    after(pe, moved_att, turn, c, 2, TURN)
                    for i in range(2):
                        pe.transpose(tr_ps[q][:, i, :], rows[:, s, k, i, :], keep.ident[:, :])
                    pe.transpose(at_ps[q][0:ATT_IN + 1, 0:P], att_s[:, s, k, :], keep.ident[:, :]).then_inc(turned[s], 1)

                def product(turn, c):
                    q = c % 2
                    pe.wait_ge(moved, turn * TURN + c + 1)
                    pe.wait_ge(moved_att, turn * TURN + c + 1)
                    after(pe, z_out, turn, c, 2, TURN)
                    pe.matmul(z_ps[q][:, :], tr[:, q, 0, :], g.wl[:, :], start=True, stop=False)
                    pe.matmul(z_ps[q][:, :], tr[:, q, 1, :], g.wr[:, :], start=False, stop=False)
                    pe.matmul(z_ps[q][:, :], at[:, q, :], g.edge[:, :], start=False, stop=True).then_inc(z_ready, 1)

                pipeline(pe, (0, turn_over), (1, product), per_turn=TURN, total=J)

            @block.scalar
            def _(act):
                ph.free_slots(act)
                def move(turn, c):
                    s, k, q = c // GC, c % GC, c % 2
                    act.wait_ge(turned[s], turn * GC + k + 1 + turned.base)
                    after(act, z_ready, turn, c, 2, TURN)
                    after(act, kept, turn, c, 2, TURN)
                    act.activation(tr[:, q, :, :], tr_ps[q][:, 0:2, :], ACT.Copy).then_inc(moved, 1)

                def low(turn, c):
                    act.wait_ge(z_ready, turn * TURN + c + 1)
                    after(act, scored, turn, c, 2, TURN)
                    act.activation(z[:, c % 2, :], z_ps[c % 2][:, :], ACT.Copy, scale=SLOPE).then_inc(z_low, 1)

                pipeline(act, (0, move), (1, low), per_turn=TURN, total=J)

            @block.vector
            def _(dve):
                def move(turn, c):
                    s, k, q = c // GC, c % GC, c % 2
                    dve.wait_ge(turned[s], turn * GC + k + 1 + turned.base)
                    after(dve, z_ready, turn, c, 2, TURN)
                    dve.tensor_copy(at[:, q, :], at_ps[q][0:ATT_IN + 1, 0:P]).then_inc(moved_att, 1)

                def score(turn, c):
                    s, k, q = c // GC, c % GC, c % 2
                    dve.wait_ge(moved, turn * TURN + c + 1)
                    dve.tensor_copy(xt[:, bass.ds((turn * TURN + c) * P, P)], tr[:, q, 0, :]).then_inc(kept, 1)
                    dve.wait_ge(z_low, turn * TURN + c + 1)
                    dve.tensor_tensor(z[:, q, :], z_ps[q][:, :], z[:, q, :], ALU.max).then_inc(z_out, 1)
                    dve.wait_ge(z_out, turn * TURN + c + 1)
                    if k == 0:
                        after(dve, grouped, turn, s, 2, SLOTS)
                    for h in range(HEADS):
                        part = slice(h * D, (h + 1) * D)
                        ins = dve.tensor_tensor_reduce(junk[:, q, part], z[:, q, part], g.att[:, part], 1.0, 0.0,
                                                       ALU.mult, ALU.add, sums[:, s % 2, h, k:k + 1])
                    ins.then_inc(scored, 1)
                    if k == GC - 1:
                        dve.wait_ge(scored, turn * TURN + c + 1)
                        dve.tensor_copy(logits[:, :, bass.ds(turn * TURN + s * GC, GC)], sums[:, s % 2]).then_inc(grouped, 1)

                pipeline(dve, (0, move), (1, score), per_turn=TURN, total=J)


SLOPE = 0.2


def softmax(nc, keep, e, heads, logits, out, name, make_logits=None, top=None, total=None):
    with Phase(nc, name) as ph:
        mem = reduce_memory(ph, heads)
        red = ph.sb("red", [P, heads, J])
        chain, ready, done = ph.sem("chain"), ph.sem("ready"), ph.sem("done")
        top = top if top is not None else red[:, :, :]
        with nc.Block() as block:
            @block.vector
            def _(dve):
                link = linked(dve, chain)
                if make_logits is not None:
                    make_logits(dve, link)
                key_reduce(dve, link, keep, e, "max", heads, logits, top, *mem, 1)
                link(dve.tensor_tensor(logits, logits, top, ALU.subtract))
                dve.sem_inc(ready, 1)
                dve.wait_ge(done, 1)
                sums = total if total is not None else red[:, :, :]
                key_reduce(dve, link, keep, e, "sum", heads, out, sums, *mem, 2)
                if total is None:
                    link(dve.tensor_scalar(sums, sums, 1e-16, float(heads), ALU.add, ALU.mult))
                    link(dve.reciprocal(sums, sums))
                    link(dve.tensor_tensor(out, out, sums, ALU.mult))

            @block.scalar
            def _(act):
                act.wait_ge(ready, 1)
                act.activation(out, logits, ACT.Exp).then_inc(done, 1)

            @block.tensor
            def _(pe):
                for n in range(2):
                    spread_ends(pe, keep, heads, mem[1], mem[5], mem[6], mem[7], 2 * heads * (n + 1))


def gatv2_edges(nc, keep, e, w, x, agg):
    with ExitStack() as stack:
        g = gatv2_weights(nc, keep, stack, w)
        xt = stack.enter_context(nc.sbuf_tensor("xt_kept", [P, J * P], F32))
        logits = stack.enter_context(nc.sbuf_tensor("logits", [P, HEADS, J], F32))
        alpha = stack.enter_context(nc.sbuf_tensor("alpha", [P, HEADS, J], F32))
        gatv2_logits(nc, keep, e, g, x, xt, logits)
        softmax(nc, keep, e, HEADS, logits[:, :, :], alpha[:, :, :], "sm2")
        edge_sum(nc, keep, "e2", e, agg, PrepareGatv2(keep, xt, g.wl, g.bl_parts, alpha))


def gat_edges(nc, keep, name, e, h, agg):
    with ExitStack() as stack:
        def sb(n, shape):
            return stack.enter_context(nc.sbuf_tensor(f"{name}_{n}", shape, F32))

        rows, a_dst = sb("rows", [P, J, ROW]), sb("a_dst", [P, J, GAT_HEADS])
        logits, weight = sb("logits", [P, GAT_HEADS, J]), sb("weight", [P, GAT_HEADS, J])
        tail = sb("tail", [P, 2 * GAT_HEADS, J])
        pairs = h.rearrange("n (a b) -> (n a) b", b=GAT_HEADS)
        with Phase(nc, name + "g", freed="kept") as ph:
            got, got_a = ph.sb("got", [P, SLOTS, GC, ROW]), ph.sb("got_a", [P, SLOTS, GC, GAT_HEADS])
            a_row = ph.sb("a_row", [P, J], I32)
            get_s = ph.sb("get_s", [P, SLOTS, 2, GC], I32)
            gathered, kept = slot_sems(ph, "gathered", SLOTS), slot_sems(ph, "kept", SLOTS)
            rows_known, staged, go = ph.sem("rows_known"), ph.sem("staged"), ph.sem("go")
            with nc.Block() as block:
                @block.scalar
                def _(act):
                    ph.free_slots(act)

                @block.vector
                def _(dve):
                    dve.tensor_scalar(a_row[:, :], e.key_i[:, :], ROW // GAT_HEADS, ROW // GAT_HEADS - 1, ALU.mult, ALU.add)\
                        .then_inc(rows_known, 1)
                    with dve.Fori(0, TURNS) as turn:
                        for s in range(SLOTS):
                            dve.wait_ge(gathered[s], turn * (32 * GC) + 32 * GC)
                            cols = bass.ds(turn * TURN + s * GC, GC)
                            dve.tensor_copy(rows[:, cols, :], got[:, s]).then_inc(kept[s], 1)
                            dve.tensor_copy(a_dst[:, cols, :], got_a[:, s]).then_inc(kept[s], 1)

                @block.gpsimd
                def _(pool):
                    pool.wait_ge(rows_known, 1)
                    with pool.Fori(0, TURNS) as turn:
                        for s in range(SLOTS):
                            free(pool, kept, turn, s, 2)
                            cols = bass.ds(turn * TURN + s * GC, GC)
                            pool.sem_inc(go, 1)
                            pool.tensor_copy(get_s[:, s, 0, :], e.other_i[:, cols]).then_inc(staged, 1)
                            pool.tensor_copy(get_s[:, s, 1, :], a_row[:, cols]).then_inc(staged, 1)
                            pool.wait_ge(staged, turn * (2 * SLOTS) + 2 * s + 2)
                            pool.sem_inc(go, 1)
                            for k in range(GC):
                                for table, to, i in ((h, got, 0), (pairs, got_a, 1)):
                                    pool.indirect_dma_start(out=to[:, s, k, :], out_offset=None, in_=table,
                                                            in_offset=bass.IndirectOffsetOnAxis(ap=get_s[:, s, i, k:k + 1], axis=0))\
                                        .then_inc(gathered[s], 16)

        def make_logits(dve, link):
            link(dve.tensor_tensor(logits[:, :, :], rows[:, :, D:D + GAT_HEADS].rearrange("p j h -> p h j"),
                                   a_dst[:, :, :].rearrange("p j h -> p h j"), ALU.add))
            link(dve.scalar_tensor_tensor(logits[:, :, :], logits[:, :, :], SLOPE, logits[:, :, :], ALU.mult, ALU.max))

        softmax(nc, keep, e, GAT_HEADS, logits[:, :, :], weight[:, :, :], name + "s", make_logits,
                tail[:, 0:GAT_HEADS, :], tail[:, GAT_HEADS:, :])
        edge_sum(nc, keep, name + "m", e, agg, PrepareAttention(rows, weight, tail))


def wide(v):
    return v.unsqueeze(1).broadcast_to([P, GB, D])


def attention_weights(dve, link, out, w, att_src, att_dst, tmp):
    link(dve.tensor_copy(out[:, 0:D], w))
    for i, att in enumerate((att_src, att_dst)):
        link(dve.tensor_tensor(tmp, w, att, ALU.mult))
        link(dve.tensor_reduce(out[:, D + GAT_HEADS * i:D + GAT_HEADS * (i + 1)],
                               tmp.rearrange("p (h c) -> p h c", h=GAT_HEADS), AX.X, ALU.add))


def node_gatv2(nc, keep, x2, agg, w, gat, x3, h3):
    with Phase(nc, "n2", freed="f_ready h_out h_ready y_ready turned3 x3_out turned1 x3_ready scaled2 sums1") as ph:
        names = ("conv_bias", "g1", "beta1", "b2", "g2", "beta2")
        vec = {n: ph.sb(n, [P, D]) for n in names}
        w1, b1, w2 = ph.sb("w1", [P, 2, D]), ph.sb("b1", [P, 2]), ph.sb("w2", [P, 2, D])
        w1g, b1g, column = ph.sb("w1g", [P, 2, D]), ph.sb("b1g", [P, 2]), ph.sb("column", [P, 2])
        wh, att, waug, tmp = ph.sb("wh", [P, D]), ph.sb("att", [P, 2, D]), ph.sb("waug", [P, ROW]), ph.sb("tmp", [P, D])
        xs, ag = ph.sb("xs", [P, SLOT, GB, D]), ph.sb("ag", [P, SLOT, GB, D])
        r1, r2, x3s = ph.sb("r1", [P, SLOT, GB, D]), ph.sb("r2", [P, SLOT, GB, D]), ph.sb("x3s", [P, SLOT, GB, D])
        xt1, xt3, gt = ph.sb("xt1", [P, SLOT, GB, P]), ph.sb("xt3", [P, SLOT, GB, P]), ph.sb("gt", [P, SLOT, 2, GB, P])
        ho = ph.sb("ho", [P, SLOT, GB, ROW])
        shift = [ph.sb(f"shift{i}", [P, SLOT, GB]) for i in range(3)]
        stats = [ph.sb(f"stats{i}", [P, SLOT, GB, 6]) for i in range(3)]
        mv, rstd = [ph.sb(f"mv{i}", [P, SLOT, GB, 2]) for i in range(3)], [ph.sb(f"rstd{i}", [P, SLOT, GB]) for i in range(3)]
        t1_ps, t3_ps, y_ps = (ph.ps(n, [P, GB, P]) for n in ("t1_ps", "t3_ps", "y_ps"))
        f_ps, h_ps = [ph.ps(f"f_ps{j}", [P, GB, P]) for j in range(2)], [ph.ps(f"h_ps{j}", [P, 2, ROW]) for j in range(2)]
        weights, chain, w_ready, folded = ph.sem("weights"), ph.sem("chain"), ph.sem("w_ready"), ph.sem("folded")
        x_in, ag_in, x3_out, h_out = (slot_sems(ph, n) for n in ("x_in", "ag_in", "x3_out", "h_out"))
        x_added = slot_sems(ph, "x_added")
        scaled2a = ph.sem("scaled2a")
        added, sums1, rstd1, normed1, scaled1 = (slot_sems(ph, n) for n in ("added", "sums1", "rstd1", "normed1", "scaled1"))
        turned1, moved1, f_ready, gelued, y_ready = (slot_sems(ph, n) for n in ("turned1", "moved1", "f_ready", "gelued", "y_ready"))
        sums2, rstd2, scaled2 = (slot_sems(ph, n) for n in ("sums2", "rstd2", "scaled2"))
        sums3, rstd3, x3_ready = (slot_sems(ph, n) for n in ("sums3", "rstd3", "x3_ready"))
        turned3, moved3, h_ready, h_kept = (slot_sems(ph, n) for n in ("turned3", "moved3", "h_ready", "h_kept"))
        pool_steps = [ph.sem(f"pool_steps{i}") for i in range(3)]
        dve_steps = [ph.sem(f"dve_steps{i}") for i in range(4)]
        n_weights = 16 * (len(names) + 8)
        with nc.Block() as block, nc.allow_non_contiguous_dma(reason="the FFN's first bias, a column for each half"):
            @block.sync
            def _(sp):
                for n in names:
                    sp.dma_start(vec[n][:, :], w[n].partition_broadcast(P)).then_inc(weights, 16)
                sp.dma_start(w1[:, :, :], w["W1"].rearrange("d (j f) -> d j f", j=2)).then_inc(weights, 16)
                sp.dma_start(w2[:, :, :], w["W2"].rearrange("(j f) d -> f j d", j=2)).then_inc(weights, 16)
                sp.dma_start(b1[:, :], w["b1"].rearrange("(j f) -> f j", j=2)).then_inc(weights, 16)
                sp.dma_start(wh[:, :], gat["W"]).then_inc(weights, 16)
                for i, n in enumerate(("g1", "beta1")):
                    sp.dma_start(column[:, i:i + 1], w[n].unsqueeze(1)).then_inc(weights, 16)
                for i, n in enumerate(("att_src", "att_dst")):
                    sp.dma_start(att[:, i, :], gat[n].rearrange("h c -> (h c)").partition_broadcast(P)).then_inc(weights, 16)
                with sp.Fori(0, NTURN) as turn:
                    used = sp.snap(turn + 1)
                    for s in range(SLOT):
                        sp.wait_ge(scaled2[s], used)
                        sp.wait_ge(sums1[s], used)
                        sp.dma_start(xs[:, s], block_rows(x2, turn, s)).then_inc(x_in[s], 16)
                        sp.dma_start(ag[:, s], block_rows(agg, turn, s)[:, :, 0:D]).then_inc(ag_in[s], 16)

            @block.gpsimd
            def _(pool):
                pool.wait_ge(w_ready, 1)

                def add(turn, s):
                    done(pool, x_in, turn, s, 16)
                    free(pool, turned1, turn, s)
                    pool.tensor_tensor(r1[:, s], xs[:, s], wide(vec["conv_bias"][:, :]), ALU.add).then_inc(added[s], 1)
                    done(pool, added, turn, s)
                    pool.tensor_tensor(xs[:, s], xs[:, s], wide(vec["beta2"][:, :]), ALU.add).then_inc(x_added[s], 1)

                def deviation(i, sums, out):
                    def fn(turn, s):
                        done(pool, sums, turn, s)
                        if i == 1:
                            norm_scale(pool, keep, Steps(pool, pool_steps[i], turn * SLOT + s, 1), mv[i][:, s],
                                       rstd[i][:, s, :], out[s])
                        else:
                            norm_shift(pool, keep, Steps(pool, pool_steps[i], turn * SLOT + s, SHIFT_STEPS), mv[i][:, s],
                                       rstd[i][:, s, :], shift[i][:, s, :], out[s])
                    return fn

                pipeline(pool, (1, deviation(0, sums1, rstd1)), (3, deviation(2, sums3, rstd3)), (2, deviation(1, sums2, rstd2)),
                         (0, add))

            @block.vector
            def _(dve):
                link = linked(dve, chain)
                dve.wait_ge(weights, n_weights)
                attention_weights(dve, link, waug[:, :], wh[:, :], att[:, 0, :], att[:, 1, :], tmp[:, :])
                link(dve.tensor_scalar(w1g[:, :, :], w1[:, :, :], column[:, 0:1], None, ALU.mult))
                link(dve.tensor_tensor(vec["beta1"][:, :], vec["beta1"][:, :], vec["b2"][:, :], ALU.add))
                dve.wait_ge(folded, 1)
                link(dve.tensor_tensor(b1g[:, :], y_ps[:, 0, 0:2], b1[:, :], ALU.add))
                dve.sem_inc(w_ready, 1)

                def sums(i, turn, s, r, out, other):
                    st = Steps(dve, dve_steps[i], turn * SLOT + s, 2 + (other is not None))
                    if other is not None:
                        st(dve.tensor_tensor(r, r, other, ALU.add))
                        st.wait()
                    norm_sums(dve, st, r, stats[i][:, s], mv[i][:, s], out[s])

                def first_sums(turn, s):
                    done(dve, added, turn, s)
                    done(dve, ag_in, turn, s, 16)
                    sums(0, turn, s, r1[:, s], sums1, ag[:, s])

                def second_sums(turn, s):
                    done(dve, y_ready, turn, s)
                    done(dve, scaled1, turn, s)
                    sums(1, turn, s, r2[:, s], sums2, y_ps[:, :, :])

                def third_sums(turn, s):
                    done(dve, scaled2, turn, s)
                    sums(2, turn, s, r2[:, s], sums3, None)

                def scale1(turn, s):
                    st = Steps(dve, dve_steps[3], turn * SLOT + s, 1)
                    done(dve, normed1, turn, s)
                    free(dve, x3_ready, turn, s)
                    st(dve.tensor_tensor(r2[:, s], r1[:, s], wide(vec["g1"][:, :]), ALU.mult))
                    st.wait()
                    dve.tensor_tensor(r2[:, s], r2[:, s], wide(vec["beta1"][:, :]), ALU.add).then_inc(scaled1[s], 1)

                def second_norm(turn, s):
                    done(dve, rstd2, turn, s)
                    done(dve, x_added, turn, s)
                    st = Steps(dve, scaled2a, turn * SLOT + s, 1)
                    for g in range(GB):
                        ins = dve.scalar_tensor_tensor(r2[:, s, g, :], r2[:, s, g, :], mv[1][:, s, g, 0:1], vec["g2"][:, :],
                                                       ALU.subtract, ALU.mult)
                    st(ins)
                    st.wait()
                    for g in range(GB):
                        ins = dve.scalar_tensor_tensor(r2[:, s, g, :], r2[:, s, g, :], rstd[1][:, s, g:g + 1], xs[:, s, g, :],
                                                       ALU.mult, ALU.add)
                    ins.then_inc(scaled2[s], 1)

                pipeline(dve, (3, third_sums), (2, second_sums), (1, scale1), (2, second_norm), (0, first_sums))

            @block.tensor
            def _(pe):
                pe.wait_ge(weights, n_weights)
                for j in range(2):
                    ins = pe.matmul(y_ps[:, 0, j:j + 1], w1[:, j, :], column[:, 1:2], start=True, stop=True)
                ins.then_inc(folded, 1)
                pe.wait_ge(w_ready, 1)

                def ffn2(turn, s):
                    done(pe, gelued, turn, s, 2)
                    bank_free(pe, sums2, turn, s)
                    for g in range(GB):
                        for j in range(2):
                            ins = pe.matmul(y_ps[:, g, :], gt[:, s, j, g, :], w2[:, j, :], start=j == 0, stop=j == 1)
                    ins.then_inc(y_ready[s], 1)

                def turn3(turn, s):
                    done(pe, x3_ready, turn, s)
                    bank_free(pe, moved3, turn, s)
                    for g in range(GB):
                        ins = pe.transpose(t3_ps[:, g, :], x3s[:, s, g, :], keep.ident[:, :])
                    ins.then_inc(turned3[s], 1)

                def product3(turn, s):
                    done(pe, moved3, turn, s)
                    bank_free(pe, h_kept, turn, s, 2)
                    for g in range(GB):
                        ins = pe.matmul(h_ps[g // 2][:, g % 2, :], xt3[:, s, g, :], waug[:, :], start=True, stop=True)
                    ins.then_inc(h_ready[s], 1)

                def turn1(turn, s):
                    done(pe, normed1, turn, s)
                    bank_free(pe, moved1, turn, s)
                    for g in range(GB):
                        ins = pe.transpose(t1_ps[:, g, :], r1[:, s, g, :], keep.ident[:, :])
                    ins.then_inc(turned1[s], 1)

                def ffn1(turn, s):
                    done(pe, moved1, turn, s)
                    bank_free(pe, gelued, turn, s, 2)
                    for j in range(2):
                        ins = pe.matmul(f_ps[j][:, :, :], w1g[:, j, :], xt1[:, s], start=True, stop=True)
                    ins.then_inc(f_ready[s], 1)

                pipeline(pe, (2, ffn2), (1, turn1), (1, ffn1), (3, turn3), (3, product3))

            @block.scalar
            def _(act):
                ph.free_slots(act)
                def store_h(turn, s):
                    done(act, h_kept, turn, s, 2)
                    act.dma_start(block_rows(h3, turn, s), ho[:, s]).then_inc(h_out[s], 16)

                def store_x3(turn, s):
                    done(act, x3_ready, turn, s)
                    act.dma_start(block_rows(x3, turn, s), x3s[:, s]).then_inc(x3_out[s], 16)

                def first_norm(turn, s):
                    done(act, rstd1, turn, s)
                    norm_act(act, r1[:, s], rstd[0][:, s], shift[0][:, s], r1[:, s]).then_inc(normed1[s], 1)

                def third_norm(turn, s):
                    done(act, rstd3, turn, s)
                    free(act, x3_out, turn, s, 16)
                    free(act, turned3, turn, s)
                    norm_act(act, r2[:, s], rstd[2][:, s], shift[2][:, s], x3s[:, s]).then_inc(x3_ready[s], 1)

                def move3(turn, s):
                    done(act, turned3, turn, s)
                    free(act, h_ready, turn, s)
                    act.activation(xt3[:, s], t3_ps[:, :, :], ACT.Copy).then_inc(moved3[s], 1)

                def keep_h(turn, s):
                    done(act, h_ready, turn, s)
                    free(act, h_out, turn, s, 16)
                    for j in range(2):
                        act.activation(ho[:, s, 2 * j:2 * j + 2, :], h_ps[j][:, :, :], ACT.Copy).then_inc(h_kept[s], 1)

                def move1(turn, s):
                    done(act, turned1, turn, s)
                    free(act, f_ready, turn, s)
                    act.activation(xt1[:, s], t1_ps[:, :, :], ACT.Copy).then_inc(moved1[s], 1)

                def gelu(turn, s):
                    done(act, f_ready, turn, s)
                    free(act, y_ready, turn, s)
                    for j in range(2):
                        act.activation(gt[:, s, j], f_ps[j][:, :, :], ACT.Gelu, bias=b1g[:, j:j + 1]).then_inc(gelued[s], 1)

                pipeline(act, (4, store_h), (1, first_norm), (1, move1), (3, third_norm), (1, gelu), (3, move3), (3, store_x3),
                         (3, keep_h))
                for s in range(SLOT):
                    done(act, x3_out, NTURN - 1, s, 16)
                    done(act, h_out, NTURN - 1, s, 16)


class Attend:
    FIRST_STEPS, LAST_STEPS = 6, 3

    def __init__(self, ph, hs, ag):
        self.hs, self.ag = hs, ag
        self.own, self.top = ph.sb("own", [P, SLOT, GB, GAT_HEADS]), ph.sb("top", [P, SLOT, GB, GAT_HEADS])
        self.most = ph.sb("most", [P, SLOT, GB, GAT_HEADS])
        self.less, self.exps = ph.sb("less", [P, SLOT, 2, GB, GAT_HEADS]), ph.sb("exps", [P, SLOT, 2, GB, GAT_HEADS])
        self.total, self.share = ph.sb("total", [P, SLOT, GB, GAT_HEADS]), ph.sb("share", [P, SLOT, 2, GB, GAT_HEADS])
        self.u = ph.sb("u", [P, SLOT, 2, GB, D])
        self.steps = [ph.sem(f"attend_steps{i}") for i in range(3)]
        self.h_in, self.ag_in = slot_sems(ph, "h_in"), slot_sems(ph, "ag_in")
        self.less_ready, self.exps_ready, self.share_ready = (slot_sems(ph, n) for n in ("less_ready", "exps_ready", "share_ready"))
        self.u_ready = slot_sems(ph, "u_ready")

    def load(self, sp, turn, s, used, h, agg):
        sp.wait_ge(self.u_ready[s], used)
        sp.dma_start(self.hs[:, s], block_rows(h, turn, s)).then_inc(self.h_in[s], 16)
        sp.dma_start(self.ag[:, s], block_rows(agg, turn, s)).then_inc(self.ag_in[s], 16)

    def first(self, dve, turn, s):
        a, h = self, GAT_HEADS
        st = Steps(dve, a.steps[0], turn * SLOT + s, a.FIRST_STEPS)
        done(dve, a.h_in, turn, s, 16)
        done(dve, a.ag_in, turn, s, 16)
        free(dve, a.exps_ready, turn, s)
        st(dve.tensor_tensor(a.own[:, s], a.hs[:, s, :, D:D + h], a.hs[:, s, :, D + h:ROW], ALU.add))
        st(dve.tensor_scalar(a.top[:, s], a.ag[:, s, :, D + h:ROW], 0.0, -BIG, ALU.is_equal, ALU.mult))
        st.wait()
        st(dve.scalar_tensor_tensor(a.own[:, s], a.own[:, s], SLOPE, a.own[:, s], ALU.mult, ALU.max))
        st(dve.tensor_tensor(a.top[:, s], a.top[:, s], a.ag[:, s, :, D:D + h], ALU.add))
        st.wait()
        st(dve.tensor_tensor(a.most[:, s], a.top[:, s], a.own[:, s], ALU.max))
        st.wait()
        st(dve.tensor_tensor(a.less[:, s, 0], a.top[:, s], a.most[:, s], ALU.subtract))
        dve.tensor_tensor(a.less[:, s, 1], a.own[:, s], a.most[:, s], ALU.subtract).then_inc(a.less_ready[s], 1)

    def exp(self, act, turn, s):
        done(act, self.less_ready, turn, s)
        free(act, self.share_ready, turn, s)
        act.activation(self.exps[:, s], self.less[:, s], ACT.Exp).then_inc(self.exps_ready[s], 1)

    def last(self, dve, turn, s):
        a = self
        st = Steps(dve, a.steps[1], turn * SLOT + s, a.LAST_STEPS)
        done(dve, a.exps_ready, turn, s)
        st(dve.tensor_tensor(a.total[:, s], a.ag[:, s, :, D + GAT_HEADS:ROW], a.exps[:, s, 0], ALU.mult))
        st.wait()
        st(dve.scalar_tensor_tensor(a.total[:, s], a.total[:, s], 1e-16, a.exps[:, s, 1], ALU.add, ALU.add))
        st.wait()
        free(dve, a.u_ready, turn, s)
        st(dve.reciprocal(a.total[:, s], a.total[:, s]))
        st.wait()
        dve.tensor_tensor(a.share[:, s], a.exps[:, s], a.total[:, s].unsqueeze(1).broadcast_to([P, 2, GB, GAT_HEADS]),
                          ALU.mult).then_inc(a.share_ready[s], 1)

    def weigh(self, engine, turn, s, which):
        a = self
        done(engine, a.share_ready, turn, s)
        rows = (a.ag, a.hs)[which]
        return engine.tensor_tensor(a.u[:, s, which].rearrange("p g (h c) -> p g h c", h=GAT_HEADS),
                                    rows[:, s, :, 0:D].rearrange("p g (h c) -> p g h c", h=GAT_HEADS),
                                    a.share[:, s, which].unsqueeze(3).broadcast_to([P, GB, GAT_HEADS, GAT_D]), ALU.mult)


def node_gat(nc, keep, x3, h3, agg, one, two, s2, h2):
    with Phase(nc, "n3", freed="h_out product_ready r_ready share_ready exps_ready u_ready s_out turned added") as ph:
        wsk1, wsk2, wh, att = ph.sb("wsk1", [P, D]), ph.sb("wsk2", [P, D]), ph.sb("wh", [P, D]), ph.sb("att", [P, 2, D])
        waug, tmp, b1, b2 = ph.sb("waug", [P, ROW]), ph.sb("tmp", [P, D]), ph.sb("b1", [P, 2]), ph.sb("b2", [P, 2, D])
        bias1, bias2 = ph.sb("bias1", [P, 1]), ph.sb("bias2", [P, D])
        xs, xb, xt, ht = (ph.sb(n, [P, SLOT, GB, D]) for n in ("xs", "xb", "xt", "ht"))
        hs, ag, ho = (ph.sb(n, [P, SLOT, GB, ROW]) for n in ("hs", "ag", "ho"))
        a = Attend(ph, hs, ag)
        t_ps, r_ps, s_ps = (ph.ps(n, [P, GB, P]) for n in ("t_ps", "r_ps", "s_ps"))
        h_ps = [ph.ps(f"h_ps{j}", [P, 2, ROW]) for j in range(2)]
        weights, chain, w_ready = ph.sem("weights"), ph.sem("chain"), ph.sem("w_ready")
        x_in, added, turned, moved, r_ready, relued = (slot_sems(ph, n) for n in ("x_in", "added", "turned", "moved", "r_ready", "relued"))
        weighed = slot_sems(ph, "weighed")
        product_ready, s_ready, h_kept, s_out, h_out = (slot_sems(ph, n) for n in ("product_ready", "s_ready", "h_kept", "s_out", "h_out"))
        n_weights = 16 * 9
        with nc.Block() as block, nc.allow_non_contiguous_dma(reason="two biases, a float on each partition"):
            @block.sync
            def _(sp):
                for to, of in ((wsk1, one["Wsk"]), (wsk2, two["Wsk"]), (wh, two["W"])):
                    sp.dma_start(to[:, :], of).then_inc(weights, 16)
                for i, n in enumerate(("att_src", "att_dst")):
                    sp.dma_start(att[:, i, :], two[n].rearrange("h c -> (h c)").partition_broadcast(P)).then_inc(weights, 16)
                for i, n in enumerate(("b", "bsk")):
                    sp.dma_start(b1[:, i:i + 1], one[n].unsqueeze(1)).then_inc(weights, 16)
                    sp.dma_start(b2[:, i, :], two[n].partition_broadcast(P)).then_inc(weights, 16)
                with sp.Fori(0, NTURN) as turn:
                    used = sp.snap(turn + 1)
                    for s in range(SLOT):
                        sp.wait_ge(turned[s], used)
                        sp.wait_ge(added[s], used)
                        sp.dma_start(xs[:, s], block_rows(x3, turn, s)).then_inc(x_in[s], 16)
                        a.load(sp, turn, s, used, h3, agg)

            @block.gpsimd
            def _(pool):
                pool.wait_ge(w_ready, 1)

                def add(turn, s):
                    done(pool, x_in, turn, s, 16)
                    free(pool, s_out, turn, s, 16)
                    pool.tensor_tensor(xb[:, s], xs[:, s], wide(bias2[:, :]), ALU.add).then_inc(added[s], 1)

                def combine(turn, s):
                    done(pool, weighed, turn, s, 2)
                    pool.tensor_tensor(a.u[:, s, 0], a.u[:, s, 0], a.u[:, s, 1], ALU.add).then_inc(a.u_ready[s], 1)

                pipeline(pool, (1, combine), (0, add))

            @block.vector
            def _(dve):
                link = linked(dve, chain)
                dve.wait_ge(weights, n_weights)
                attention_weights(dve, link, waug[:, :], wh[:, :], att[:, 0, :], att[:, 1, :], tmp[:, :])
                link(dve.tensor_tensor(bias1[:, :], b1[:, 0:1], b1[:, 1:2], ALU.add))
                link(dve.tensor_tensor(bias2[:, :], b2[:, 0, :], b2[:, 1, :], ALU.add))
                dve.sem_inc(w_ready, 1)

                def total(turn, s):
                    done(dve, product_ready, turn, s)
                    done(dve, added, turn, s)
                    dve.tensor_tensor(xb[:, s], xb[:, s], s_ps[:, :, :], ALU.add).then_inc(s_ready[s], 1)

                def weigh(turn, s):
                    a.last(dve, turn, s)
                    free(dve, r_ready, turn, s)
                    for i in range(2):
                        a.weigh(dve, turn, s, i).then_inc(weighed[s], 1)

                pipeline(dve, (0, lambda turn, s: a.first(dve, turn, s)), (1, weigh), (3, total))

            @block.tensor
            def _(pe):
                pe.wait_ge(w_ready, 1)

                def turn_over(turn, s):
                    done(pe, x_in, turn, s, 16)
                    bank_free(pe, moved, turn, s)
                    for g in range(GB):
                        ins = pe.transpose(t_ps[:, g, :], xs[:, s, g, :], keep.ident[:, :])
                    ins.then_inc(turned[s], 1)

                def residual(turn, s):
                    done(pe, moved, turn, s)
                    done(pe, a.u_ready, turn, s)
                    bank_free(pe, relued, turn, s)
                    pe.matmul(r_ps[:, :, :], wsk1[:, :], xt[:, s], start=True, stop=False, skip_group_check=True)
                    for g in range(GB):
                        ins = pe.matmul(r_ps[:, g, :], a.u[:, s, 0, g, :], keep.ident[:, :], start=False, stop=g == GB - 1,
                                        skip_group_check=True)
                    ins.then_inc(r_ready[s], 1)

                def product(turn, s):
                    done(pe, relued, turn, s)
                    bank_free(pe, s_ready, turn, s)
                    bank_free(pe, h_kept, turn, s, 2)
                    for g in range(GB):
                        pe.matmul(s_ps[:, g, :], ht[:, s, g, :], wsk2[:, :], start=True, stop=True)
                    for g in range(GB):
                        ins = pe.matmul(h_ps[g // 2][:, g % 2, :], ht[:, s, g, :], waug[:, :], start=True, stop=True)
                    ins.then_inc(product_ready[s], 1)

                pipeline(pe, (3, product), (2, residual), (0, turn_over))

            @block.scalar
            def _(act):
                ph.free_slots(act)
                act.wait_ge(w_ready, 1)

                def store(turn, s):
                    done(act, s_ready, turn, s)
                    act.dma_start(block_rows(s2, turn, s), xb[:, s]).then_inc(s_out[s], 16)
                    done(act, h_kept, turn, s, 2)
                    act.dma_start(block_rows(h2, turn, s), ho[:, s]).then_inc(h_out[s], 16)

                def keep_h(turn, s):
                    done(act, product_ready, turn, s)
                    free(act, h_out, turn, s, 16)
                    for j in range(2):
                        act.activation(ho[:, s, 2 * j:2 * j + 2, :], h_ps[j][:, :, :], ACT.Copy).then_inc(h_kept[s], 1)

                def move(turn, s):
                    done(act, turned, turn, s)
                    free(act, r_ready, turn, s)
                    act.activation(xt[:, s], t_ps[:, :, :], ACT.Copy).then_inc(moved[s], 1)

                def relu(turn, s):
                    done(act, r_ready, turn, s)
                    free(act, product_ready, turn, s)
                    act.activation(ht[:, s], r_ps[:, :, :], ACT.Relu, bias=bias1[:, 0:1]).then_inc(relued[s], 1)

                pipeline(act, (4, store), (0, lambda turn, s: a.exp(act, turn, s)), (3, keep_h), (0, move), (2, relu))
                for s in range(SLOT):
                    done(act, s_out, NTURN - 1, s, 16)
                    done(act, h_out, NTURN - 1, s, 16)


def node_last(nc, keep, s2, h2, agg, out):
    with Phase(nc, "n4", freed="weighed stored share_ready exps_ready u_ready out_ready sums_ready") as ph:
        ss, os, r = (ph.sb(n, [P, SLOT, GB, D]) for n in ("ss", "os", "r"))
        hs, ag = (ph.sb(n, [P, SLOT, GB, ROW]) for n in ("hs", "ag"))
        a = Attend(ph, hs, ag)
        stats, mv, rstd = ph.sb("stats", [P, SLOT, GB, 6]), ph.sb("mv", [P, SLOT, GB, 2]), ph.sb("rstd", [P, SLOT, GB])
        s_in, sums_ready, rstd_ready, out_ready, stored = (slot_sems(ph, n) for n in ("s_in", "sums_ready", "rstd_ready", "out_ready", "stored"))
        shift, own_steps, weighed = ph.sb("shift", [P, SLOT, GB]), ph.sem("own_steps"), slot_sems(ph, "weighed")
        dve_steps, pool_steps = ph.sem("dve_steps"), ph.sem("pool_steps")
        with nc.Block() as block:
            @block.sync
            def _(sp):
                with sp.Fori(0, NTURN) as turn:
                    used = sp.snap(turn + 1)
                    for s in range(SLOT):
                        sp.wait_ge(weighed[s], used)
                        a.load(sp, turn, s, used, h2, agg)
                        sp.dma_start(ss[:, s], block_rows(s2, turn, s)).then_inc(s_in[s], 16)

            @block.gpsimd
            def _(pool):
                def deviation(turn, s):
                    done(pool, sums_ready, turn, s)
                    norm_shift(pool, keep, Steps(pool, pool_steps, turn * SLOT + s, SHIFT_STEPS), mv[:, s], rstd[:, s, :],
                               shift[:, s, :], rstd_ready[s])

                def own(turn, s):
                    free(pool, sums_ready, turn, s)
                    st = Steps(pool, own_steps, turn * SLOT + s, 1)
                    st(a.weigh(pool, turn, s, 1))
                    st.wait()
                    done(pool, s_in, turn, s, 16)
                    pool.tensor_tensor(a.u[:, s, 1], ss[:, s], a.u[:, s, 1], ALU.add).then_inc(a.u_ready[s], 1)

                pipeline(pool, (3, deviation), (1, own))

            @block.vector
            def _(dve):
                def sums(turn, s):
                    done(dve, a.u_ready, turn, s)
                    done(dve, weighed, turn, s)
                    st = Steps(dve, dve_steps, turn * SLOT + s, NORM_STEPS + 1)
                    free(dve, out_ready, turn, s)
                    st(dve.tensor_tensor(r[:, s], a.u[:, s, 1], a.u[:, s, 0], ALU.add))
                    st.wait()
                    norm_sums(dve, st, r[:, s], stats[:, s], mv[:, s], sums_ready[s])

                def weigh(turn, s):
                    a.last(dve, turn, s)
                    free(dve, sums_ready, turn, s)
                    a.weigh(dve, turn, s, 0).then_inc(weighed[s], 1)

                pipeline(dve, (0, lambda turn, s: a.first(dve, turn, s)), (1, weigh), (2, sums))

            @block.scalar
            def _(act):
                ph.free_slots(act)
                def store(turn, s):
                    done(act, out_ready, turn, s)
                    act.dma_start(block_rows(out, turn, s), os[:, s]).then_inc(stored[s], 16)

                def apply(turn, s):
                    done(act, rstd_ready, turn, s)
                    free(act, stored, turn, s, 16)
                    norm_act(act, r[:, s], rstd[:, s], shift[:, s], os[:, s]).then_inc(out_ready[s], 1)

                pipeline(act, (4, store), (3, apply), (0, lambda turn, s: a.exp(act, turn, s)))
                for s in range(SLOT):
                    done(act, stored, NTURN - 1, s, 16)


def find_descents(nc, keep, dst, descents):
    with Phase(nc, "fd") as ph:
        key, after_i = ph.sb("key", [P, J], I32), ph.sb("after_i", [P, 1], I32)
        flags, count = ph.sb("flags", [P, J]), ph.sb("count", [P, 1])
        total_ps = ph.ps("total_ps", [P, 1])
        loaded, chain, counted, summed, preset = (ph.sem(n) for n in ("loaded", "chain", "counted", "summed", "preset"))
        view = dst.rearrange("(p j) -> p j", p=P)
        with nc.Block() as block, nc.allow_non_contiguous_dma(reason="the first edge of each partition"):
            @block.sync
            def _(sp):
                sp.dma_start(key[:, :], view).then_inc(loaded, 16)
                sp.wait_ge(preset, 1)
                sp.dma_start(after_i[0:P - 1, :], view[1:P, 0:1]).then_inc(loaded, 16)

            @block.vector
            def _(dve):
                link = linked(dve, chain)
                dve.memset(after_i[:, :], NPAD).then_inc(preset, 1)
                dve.wait_ge(loaded, 32)
                dve.tensor_tensor(flags[:, 0:J - 1], key[:, 0:J - 1], key[:, 1:J], ALU.is_gt)
                link(dve.tensor_tensor(flags[:, J - 1:J], key[:, J - 1:J], after_i[:, :], ALU.is_gt))
                dve.tensor_reduce(count[:, :], flags[:, :], AX.X, ALU.add).then_inc(counted, 1)
                dve.wait_ge(summed, 1)
                link(dve.tensor_copy(descents[:, :], total_ps[:, :]))

            @block.tensor
            def _(pe):
                pe.wait_ge(counted, 1)
                pe.matmul(total_ps[:, :], keep.ones[:, :], count[:, :], start=True, stop=True).then_inc(summed, 1)


def lay_out_sorted(nc, src, dst, attr, target):
    with Phase(nc, "lo") as ph:
        pay = ph.sb("pay", [P, J, WD])
        loaded, prepared, stored = ph.sem("loaded"), ph.sem("prepared"), ph.sem("stored")
        with nc.Block() as block:
            n_loads = load_edges(nc, src, dst, attr)(block, ph, pay, loaded, prepared)

            @block.scalar
            def _(act):
                act.wait_ge(loaded, n_loads)
                act.dma_start(target.rearrange("(p j) w -> p j w", p=P), pay[:, :, :]).then_inc(stored, 16)
                act.wait_ge(stored, 16)


def gnn(nc, x, src, dst, attr, sage, gcn, gat2, gat, out):
    def dram(name, shape):
        return nc.dram_tensor(name, shape, F32, kind="Internal").ap()

    by_dst, by_src = [dram(f"by_dst{i}", (EPAD, WD)) for i in range(2)], [dram(f"by_src{i}", (EPAD, WS)) for i in range(2)]
    agg_dst, agg_src = dram("agg_dst", (NPAD, ROW)), dram("agg_src", (NPAD, D))
    x1, z1, h3, h4 = (dram(n, (NPAD, ROW)) for n in ("x1", "z1", "h3", "h4"))
    x2, x3, s4 = (dram(n, (NPAD, D)) for n in ("x2", "x3", "s4"))
    with ExitStack() as stack:
        keep = Keep()
        constants(nc, keep, stack)
        descents = stack.enter_context(nc.sbuf_tensor("descents", [P, 1], I32))
        find_descents(nc, keep, dst, descents)
        unsorted = nc.values_load(descents[0:1, 0:1], min_val=0, max_val=EPAD)
        with nc.If(unsorted > 0):
            sort_pass(nc, keep, "d1", WD, LOW, False, load_edges(nc, src, dst, attr), by_dst[0])
            sort_pass(nc, keep, "d2", WD, HIGH, True, load_sorted(by_dst[0]), by_dst[1])
        with nc.Else():
            lay_out_sorted(nc, src, dst, attr, by_dst[1])
        sort_pass(nc, keep, "s1", WS, LOW, False, load_edges(nc, src, dst, None), by_src[0], [agg_dst, agg_src])
        sort_pass(nc, keep, "s2", WS, HIGH, True, load_sorted(by_src[0]), by_src[1])
        to_dst = edge_tables(nc, keep, "d", by_dst[1], WD, stack, True)
        with ExitStack() as src_stack:
            to_src = edge_tables(nc, keep, "s", by_src[1], WS, src_stack, False)
            degrees(nc, keep, to_dst)
            edge_sum(nc, keep, "e0", to_dst, agg_dst, PrepareMean(to_dst), x, D)
            node_sage(nc, keep, x, agg_dst, sage["W"], sage["b"], x1)
            edge_sum(nc, keep, "e1a", to_src, agg_src, PrepareNorm(), x1, ROW)
            node_gcn(nc, keep, "n1a", x1, agg_src, gcn["W1"], GCN_BETA[0], z1)
            edge_sum(nc, keep, "e1b", to_src, agg_src, PrepareNorm(), z1, ROW)
            node_gcn(nc, keep, "n1b", z1, agg_src, gcn["W2"], GCN_BETA[1], x2, x1)
        gatv2_edges(nc, keep, to_dst, gat2, x2, agg_dst)
        node_gatv2(nc, keep, x2, agg_dst, gat2, gat[0], x3, h3)
        gat_edges(nc, keep, "e3", to_dst, h3, agg_dst)
        node_gat(nc, keep, x3, h3, agg_dst, gat[0], gat[1], s4, h4)
        gat_edges(nc, keep, "e4", to_dst, h4, agg_dst)
        node_last(nc, keep, s4, h4, agg_dst, out)


def kernel(**inputs):
    import concourse.bacc as bacc
    from concourse.bass_utils import run_bass_kernel_spmd

    nc = bacc.Bacc("TRN2", target_bir_lowering=False, num_devices=1)
    arrays = {}

    def take(name, a):
        arrays[name] = np.ascontiguousarray(a)
        return nc.dram_tensor(name, arrays[name].shape, mybir.dt.from_np(arrays[name].dtype), kind="ExternalInput").ap()

    def padded(a, rows, fill):
        a = np.asarray(a)
        return np.concatenate([a, np.full((rows - a.shape[0],) + a.shape[1:], fill, a.dtype)])

    def layer(prefix, names, **more):
        w = {n: take(prefix + n, np.asarray(inputs[prefix + n])) for n in names}
        w.update({n: take(prefix + n, np.asarray(inputs[prefix + n]).T) for n in more.get("transposed", ())})
        return w

    x = take("x", padded(inputs["x"], NPAD, 0))
    src, dst = (take(n, padded(inputs[n], EPAD, NPAD - 1)) for n in ("src", "dst"))
    attr = take("edge_attr_16", padded(inputs["edge_attr_16"], EPAD, 0))
    sage = layer("L0_gnn_", ("W_neigh", "b_neigh"))
    gcn = layer("L1_gnn_", ("W1", "W2"))
    gat2 = layer("L2_gnn_", ("bl", "br", "att", "conv_bias", "g1", "beta1", "b1", "b2", "g2", "beta2"),
                 transposed=("Wl", "Wr", "We", "W1", "W2"))
    both = layer("L3_gnn_", [f"{n}{i}" for i in (1, 2) for n in ("W", "att_src", "att_dst", "b", "Wsk", "bsk")])
    gat = [{n: both[f"{n}{i}"] for n in ("W", "att_src", "att_dst", "b", "Wsk", "bsk")} for i in (1, 2)]
    out = nc.dram_tensor("out", (NPAD, D), F32, kind="ExternalOutput").ap()
    gnn(nc, x, src, dst, attr, {"W": sage["W_neigh"], "b": sage["b_neigh"]}, gcn, gat2, gat, out)
    r = run_bass_kernel_spmd(nc, [arrays], core_ids=[0])
    return r.results[0]["out"][:NODES]
```

```python
from contextlib import ExitStack
import numpy as np
import concourse.bass as bass
from concourse import mybir

F32, I32, F16, BF16 = mybir.dt.float32, mybir.dt.int32, mybir.dt.float16, mybir.dt.bfloat16
ALU, ACT, AX = mybir.AluOpType, mybir.ActivationFunctionType, mybir.AxisListType

P = 128
D = 128
NODES, EDGES = 50000, 25000
GB = 4
BLOCK = P * GB
SLOT = 4
NB = SLOT * -(-NODES // (SLOT * BLOCK))
NPAD = NB * BLOCK
GC, SLOTS = 7, 4
TURN = GC * SLOTS
J = TURN * -(-EDGES // (P * TURN))
EPAD = P * J
TURNS = J // TURN
ROW = D + 4
HEADS, HD = 4, 4 * D
ATT_IN = 16
WD = 2 + ATT_IN
WS = 2
LOW = 256
HIGH = NPAD // LOW
BIG = 1.0e30
GCN_BETA = (float(np.log(np.float32(1.5))), float(np.log(np.float32(1.25))))
FAR = 65536.0
assert NPAD % LOW == 0 and HIGH <= LOW and J % TURN == 0


class Phase:

    def __init__(self, nc, name, freed=""):
        self.nc, self.name, self.stack, self.sems = nc, name, ExitStack(), []
        self.freed_names, self.freed = freed.split(), []

    def free_slots(self, engine):
        for sems in self.freed:
            for s in sems:
                engine.sem_inc(s, 1)

    def sb(self, name, shape, dt=F32):
        return self.stack.enter_context(self.nc.sbuf_tensor(f"{self.name}_{name}", shape, dt))

    def ps(self, name, shape, dt=F32):
        return self.stack.enter_context(self.nc.psum_tensor(f"{self.name}_{name}", shape, dt))

    def sem(self, name):
        s = self.nc.alloc_semaphore(f"{self.name}_{name}")
        self.sems.append(s)
        return s

    def __enter__(self):
        return self

    def __exit__(self, *e):
        if e[0] is None:
            self.nc.clear_and_free_semaphores(self.sems)
            self.nc.all_engine_barrier()
        self.stack.close()


class Slots(list):
    base = 0


def slot_sems(ph, name, slots=SLOT):
    sems = Slots(ph.sem(f"{name}{s}") for s in range(slots))
    if name in ph.freed_names:
        sems.base = 1
        ph.freed.append(sems)
    return sems


def done(engine, sems, turn, s, per_turn=1):
    engine.wait_ge(sems[s], (turn + 1) * per_turn + sems.base)


def free(engine, sems, turn, s, per_turn=1):
    assert sems.base == 1
    engine.wait_ge(sems[s], turn * per_turn + 1)


def bank_free(engine, sems, turn, s, per_turn=1, banks=1):
    n = (turn + (s - banks) // SLOT + 1) * per_turn + sems.base
    if not isinstance(n, int) or n > 0:
        engine.wait_ge(sems[(s - banks) % SLOT], n)


def pass_on(sp, sems, to):
    with sp.Fori(0, TURNS) as turn:
        for s in range(SLOTS):
            done(sp, sems, turn, s, 16 * GC)
            sp.sem_inc(to[s], 1)



class Keep:
    pass


def constants(nc, keep, stack):
    def sb(name, shape, dt=F32):
        return stack.enter_context(nc.sbuf_tensor(name, shape, dt))

    keep.ident, keep.ones = sb("ident", [P, P]), sb("ones", [P, P])
    keep.ident_h, keep.ones_h = sb("ident_h", [P, P], F16), sb("ones_h", [P, P], F16)
    keep.tri_h, keep.iota_h = sb("tri_h", [P, P], F16), sb("iota_h", [P, LOW], F16)
    keep.ones_b, keep.ident_b = sb("ones_b", [P, P], BF16), sb("ident_b", [P, P], BF16)
    keep.eps, keep.minus_half, keep.minus_one = (sb(n, [P, GB]) for n in ("eps", "minus_half", "minus_one"))
    with Phase(nc, "const") as ph:
        iota_i, filled, iota_done = ph.sb("iota_i", [P, LOW], I32), ph.sem("filled"), ph.sem("iota_done")
        shaped = ph.sem("shaped")
        with nc.Block() as block:
            @block.gpsimd
            def _(pool):
                pool.memset(keep.ident[:, :], 0.0).then_inc(filled, 1)
                pool.memset(keep.ones[:, :], 1.0).then_inc(filled, 1)
                pool.memset(keep.ones_h[:, :], 1.0).then_inc(filled, 1)
                pool.iota(iota_i[:, :], [[1, LOW]], base=0, channel_multiplier=0).then_inc(iota_done, 1)
                pool.wait_ge(filled, 3)
                pool.affine_select(out=keep.ident[:, :], in_=keep.ident[:, :], compare_op=ALU.not_equal, fill=1.0,
                                   base=0, pattern=[[-1, P]], channel_multiplier=1).then_inc(shaped, 1)
                pool.affine_select(out=keep.tri_h[:, :], in_=keep.ones_h[:, :], compare_op=ALU.is_gt, fill=0.0,
                                   base=0, pattern=[[1, P]], channel_multiplier=-1).then_inc(shaped, 1)

            @block.vector
            def _(dve):
                dve.memset(keep.eps[:, :], LN_EPS)
                dve.memset(keep.minus_half[:, :], -0.5)
                dve.memset(keep.minus_one[:, :], -1.0)
                dve.memset(keep.ones_b[:, :], 1.0)
                dve.wait_ge(iota_done, 1)
                dve.tensor_copy(keep.iota_h[:, :], iota_i[:, :])
                dve.wait_ge(shaped, 1)
                dve.tensor_copy(keep.ident_h[:, :], keep.ident[:, :])
                dve.tensor_copy(keep.ident_b[:, :], keep.ident[:, :])


def sort_pass(nc, keep, name, words, digits, high, load, target, zero_fill=None):
    with Phase(nc, name, freed="written") as ph:
        pay = ph.sb("pay", [P, J, words])
        dig = ph.sb("dig", [P, J])
        key_i = ph.sb("key_i", [P, J], I32)
        onehot = ph.sb("onehot", [P, SLOTS, GC, digits], F16)
        digs = ph.sb("digs", [P, SLOTS, GC])
        place = ph.sb("place", [P, SLOTS, GC])
        place_i = ph.sb("place_i", [P, SLOTS, GC], I32)
        pay_s = ph.sb("pay_s", [P, SLOTS, GC, words])
        junk = ph.sb("junk", [P, 4, digits])
        hist = ph.sb("hist", [P, digits], F16)
        zero_h = ph.sb("zero_h", [P, P], F16)
        one_row = ph.sb("one_row", [P, digits])
        upto = ph.sb("upto", [P, digits])
        base = ph.sb("base", [P, digits])
        hist_ps = ph.ps("hist_ps", [P, 512])
        total_ps = ph.ps("total_ps", [P, 512])
        before_ps = ph.ps("before_ps", [P, 512])
        run_ps = [ph.ps(f"run_ps{q}", [P, 512]) for q in range(4)]
        loaded, digit_ready = ph.sem("loaded"), ph.sem("digit_ready")
        chain = ph.sem("chain")
        digs_ready, hot_ready, hot_used = ph.sem("digs_ready"), ph.sem("hot_ready"), ph.sem("hot_used")
        hist_done, hist_read = ph.sem("hist_done"), ph.sem("hist_read")
        sums_done, base_ready = ph.sem("sums_done"), ph.sem("base_ready")
        digs2_ready, hot2_ready = ph.sem("digs2_ready"), ph.sem("hot2_ready")
        run_ready, ranked = ph.sem("run_ready"), ph.sem("ranked")
        placed, go = ph.sem("placed"), ph.sem("go")
        scattered, written = slot_sems(ph, "scattered", SLOTS), slot_sems(ph, "written", SLOTS)
        zeroed, zero_ready = ph.sem("zeroed"), ph.sem("zero_ready")
        if zero_fill:
            zeros = ph.sb("zeros", [P, 8 * ROW])
        with nc.Block() as block:
            n_loads = load(block, ph, pay, loaded)

            @block.sync
            def _(sp):
                pass_on(sp, scattered, written)

            @block.scalar
            def _(act):
                ph.free_slots(act)
                n = 0
                if zero_fill:
                    act.wait_ge(zero_ready, 1)
                    for a in zero_fill:
                        flat = a.rearrange("(p n) d -> p (n d)", p=P)
                        step = 8 * a.shape[1]
                        for k in range(0, flat.shape[1], step):
                            act.dma_start(flat[:, k:k + step], zeros[:, 0:step]).then_inc(zeroed, 16)
                            n += 16
                    act.wait_ge(zeroed, n)

            @block.vector
            def _(dve):
                if zero_fill:
                    dve.memset(zeros[:, :], 0.0).then_inc(zero_ready, 1)
                dve.memset(zero_h[:, :], 0.0)
                dve.memset(one_row[:, :], 1.0)
                dve.sem_inc(hot_used, SLOTS)
                dve.sem_inc(ranked, 4)
                dve.memset(onehot[:, :], 0.0).then_inc(digit_ready, 1)
                dve.wait_ge(loaded, n_loads)
                dve.wait_ge(digit_ready, 1)
                dve.tensor_copy(key_i[:, :], pay[:, :, 0]).then_inc(chain, 1)
                dve.wait_ge(chain, 1)
                op, by = (ALU.logical_shift_right, LOW.bit_length() - 1) if high else (ALU.bitwise_and, LOW - 1)
                dve.tensor_scalar(key_i[:, :], key_i[:, :], by, None, op).then_inc(chain, 1)
                dve.wait_ge(chain, 2)
                dve.tensor_copy(dig[:, :], key_i[:, :]).then_inc(chain, 1)
                dve.wait_ge(chain, 3)

                def hot(turn, s, copied, made):
                    dve.tensor_copy(digs[:, s, :], dig[:, bass.ds(turn * TURN + s * GC, GC)]).then_inc(copied, 1)
                    dve.wait_ge(copied, turn * SLOTS + s + 1)
                    for k in range(GC):
                        ins = dve.tensor_scalar(onehot[:, s, k, :], keep.iota_h[:, 0:digits], digs[:, s, k:k + 1],
                                                None, ALU.is_equal)
                    ins.then_inc(made, 1)

                with dve.Fori(0, TURNS) as turn:
                    for s in range(SLOTS):
                        dve.wait_ge(hot_used, turn * SLOTS + s + 1)
                        hot(turn, s, digs_ready, hot_ready)
                dve.wait_ge(hist_done, 1)
                dve.tensor_copy(hist[:, :], hist_ps[:, 0:digits]).then_inc(hist_read, 1)
                dve.memset(onehot[:, SLOTS - 1, :, :], 0.0).then_inc(chain, 1)
                dve.wait_ge(sums_done, 1)
                dve.tensor_tensor_scan(upto[:, :], one_row[:, :], total_ps[:, 0:digits], 0.0, ALU.mult, ALU.add).then_inc(chain, 1)
                dve.wait_ge(chain, 5)
                dve.tensor_tensor(base[:, :], upto[:, :], total_ps[:, 0:digits], ALU.subtract).then_inc(chain, 1)
                dve.wait_ge(chain, 6)
                dve.tensor_tensor(base[:, :], base[:, :], before_ps[:, 0:digits], ALU.add).then_inc(base_ready, 1)
                with dve.Fori(0, TURNS) as turn:
                    for s in range(SLOTS):
                        hot(turn, s, digs2_ready, hot2_ready)
                        dve.wait_ge(hot2_ready, turn * SLOTS + s + 1)
                        for k in range(GC):
                            c = s * GC + k
                            dve.wait_ge(run_ready, turn * TURN + c + 1)
                            dve.tensor_tensor_reduce(junk[:, c % 4, :], onehot[:, s, k, :], run_ps[c % 4][:, 0:digits],
                                                     1.0, 0.0, ALU.mult, ALU.add, place[:, s, k:k + 1]).then_inc(ranked, 1)
                        free(dve, written, turn, s)
                        dve.wait_ge(ranked, turn * TURN + (s + 1) * GC + 4)
                        dve.tensor_copy(place_i[:, s, :], place[:, s, :]).then_inc(placed, 1)
                        dve.tensor_copy(pay_s[:, s, :, :], pay[:, bass.ds(turn * TURN + s * GC, GC), :]).then_inc(placed, 1)

            @block.tensor
            def _(pe):
                pe.wait_ge(digit_ready, 1)
                pe.matmul(hist_ps[:, 0:digits], zero_h[:, :], keep.iota_h[:, 0:digits], start=True, stop=False,
                          skip_group_check=True)
                with pe.Fori(0, TURNS) as turn:
                    for s in range(SLOTS):
                        pe.wait_ge(hot_ready, turn * SLOTS + s + 1)
                        for k in range(GC):
                            ins = pe.matmul(hist_ps[:, 0:digits], keep.ident_h[:, :], onehot[:, s, k, :],
                                            start=False, stop=False, skip_group_check=True)
                        ins.then_inc(hot_used, 1)
                pe.matmul(hist_ps[:, 0:digits], zero_h[:, :], keep.iota_h[:, 0:digits], start=False, stop=True,
                          skip_group_check=True).then_inc(hist_done, 1)
                pe.wait_ge(hist_read, 1)
                pe.matmul(total_ps[:, 0:digits], keep.ones_h[:, :], hist[:, :], start=True, stop=True)
                pe.matmul(before_ps[:, 0:digits], keep.tri_h[:, :], hist[:, :], start=True, stop=True).then_inc(sums_done, 1)
                pe.wait_ge(base_ready, 1)
                for q in range(4):
                    pe.matmul(run_ps[q][:, 0:digits], keep.ident[:, :], base[:, :], start=True, stop=False,
                              skip_group_check=True)
                with pe.Fori(0, TURNS) as turn:
                    for c in range(TURN):
                        if c % GC == 1:
                            pe.wait_ge(hot2_ready, turn * SLOTS + c // GC + 1)
                        pe.wait_ge(ranked, turn * TURN + c + 1)
                        for b in range(c - 4, c):
                            b = b % TURN
                            ins = pe.matmul(run_ps[c % 4][:, 0:digits], keep.ident_h[:, :], onehot[:, b // GC, b % GC, :],
                                            start=False, stop=False, skip_group_check=True)
                        ins.then_inc(run_ready, 1)

            @block.gpsimd
            def _(pool):
                with pool.Fori(0, TURNS) as turn:
                    for s in range(SLOTS):
                        pool.wait_ge(placed, turn * (2 * SLOTS) + 2 * s + 2)
                        pool.sem_inc(go, 1)
                        for k in range(GC):
                            pool.indirect_dma_start(
                                out=target, out_offset=bass.IndirectOffsetOnAxis(ap=place_i[:, s, k:k + 1], axis=0),
                                in_=pay_s[:, s, k, :], in_offset=None).then_inc(scattered[s], 16)
                for s in range(SLOTS):
                    done(pool, scattered, TURNS - 1, s, 16 * GC)


def load_edges(nc, src, dst, attr):
    def load(block, ph, pay, loaded):
        ends = ph.sb("ends", [P, 2, J], I32)
        ends_in = ph.sem("ends_in")
        n = 16 if attr is not None else 0

        @block.sync
        def _(sp):
            keys = (dst, src) if attr is not None else (src, dst)
            for i, a in enumerate(keys):
                sp.dma_start(ends[:, i, :], a.rearrange("(p j) -> p j", p=P)).then_inc(ends_in, 16)
            if attr is not None:
                sp.dma_start(pay[:, :, 2:2 + ATT_IN], attr.rearrange("(p j) a -> p j a", p=P)).then_inc(loaded, 16)

        @block.gpsimd
        def _(pool):
            pool.wait_ge(ends_in, 32)
            pool.tensor_copy(pay[:, :, 0], ends[:, 0, :]).then_inc(loaded, 1)
            pool.tensor_copy(pay[:, :, 1], ends[:, 1, :]).then_inc(loaded, 1)
        return n + 2
    return load


def load_sorted(rows):
    def load(block, ph, pay, loaded):
        @block.sync
        def _(sp):
            sp.dma_start(pay[:, :, :], rows.rearrange("(p j) w -> p j w", p=P)).then_inc(loaded, 16)
        return 16
    return load


def linked(engine, sem):
    n = [0]

    def link(ins):
        n[0] += 1
        ins.then_inc(sem, 1)
        engine.wait_ge(sem, n[0])
    return link


class Edges:
    pass


def edge_tables(nc, keep, name, rows, words, stack, full):
    e = Edges()

    def sb(n, shape, dt=F32):
        return stack.enter_context(nc.sbuf_tensor(f"{name}_{n}", shape, dt))

    e.other_i = sb("other_i", [P, J], I32)
    e.put_i = sb("put_i", [P, J], I32)
    e.fix_i = sb("fix_i", [P, 1], I32)
    e.cont = sb("cont", [P, J])
    e.carry = sb("carry", [P, P])
    if full:
        e.key_i = sb("key_i", [P, J], I32)
        e.att = sb("att", [P, J, ATT_IN])
        e.cont_h = sb("cont_h", [P, HEADS, J])
        e.reset_h = sb("reset_h", [P, HEADS, J])
        e.end_h = sb("end_h", [P, HEADS, J])
        e.next_h = sb("next_h", [P, HEADS, J])
        e.same = [sb(f"same{t}", [P, 2, P]) for t in range(2)]
        e.same_add = [sb(f"same_add{t}", [P, 2, P]) for t in range(2)]
        e.in_add = [sb(f"in_add{t}", [P, J]) for t in range(2)]
        e.split = sb("split", [P, 1])
        e.deg, e.rdeg = sb("deg", [P, J]), sb("rdeg", [P, J])
    with Phase(nc, name + "t") as ph:
        pay, key = ph.sb("pay", [P, J, words]), ph.sb("key", [P, J])
        after, before = ph.sb("after", [P, 1]), ph.sb("before", [P, 1])
        tmp, end = ph.sb("tmp", [P, J]), ph.sb("end", [P, J])
        diag, off = ph.sb("diag", [P, 2, P]), ph.sb("off", [P, P])
        goes_on, whole, owns = ph.sb("goes_on", [P, 1]), ph.sb("whole", [P, 1]), ph.sb("owns", [P, 1])
        fix = ph.sb("fix", [P, 1])
        spread = ph.ps("spread", [P, 2, P])
        loaded, chain, preset = ph.sem("loaded"), ph.sem("chain"), ph.sem("preset")
        diag_ready, spread_done = ph.sem("diag_ready"), ph.sem("spread_done")
        view = rows.rearrange("(p j) w -> p j w", p=P)
        with nc.Block() as block, nc.allow_non_contiguous_dma(reason="one word of an edge's payload"):
            @block.sync
            def _(sp):
                sp.dma_start(pay[:, :, :], view).then_inc(loaded, 16)
                sp.wait_ge(preset, 2)
                sp.dma_start(after[0:P - 1, :], view[1:P, 0, 0:1]).then_inc(loaded, 16)
                sp.dma_start(before[1:P, :], view[0:P - 1, J - 1, 0:1]).then_inc(loaded, 16)

            @block.scalar
            def _(act):
                if full:
                    act.wait_ge(loaded, 48)
                    act.activation(e.att[:, :, :], pay[:, :, 2:WD], ACT.Copy)

            @block.vector
            def _(dve):
                link = linked(dve, chain)
                dve.memset(after[:, :], -1.0).then_inc(preset, 1)
                dve.memset(before[:, :], -1.0).then_inc(preset, 1)
                link(dve.memset(e.cont[:, :], 0.0))
                link(dve.memset(end[:, :], 1.0))
                link(dve.tensor_scalar(off[:, :], keep.ident[:, :], -1.0, 1.0, ALU.mult, ALU.add))
                dve.wait_ge(loaded, 48)
                first, last = key[:, 0:1], key[:, J - 1:J]
                link(dve.tensor_copy(key[:, :], pay[:, :, 0]))
                link(dve.tensor_copy(e.other_i[:, :], pay[:, :, 1]))
                link(dve.tensor_tensor(e.cont[:, 1:J], key[:, 1:J], key[:, 0:J - 1], ALU.is_equal))
                link(dve.tensor_scalar(end[:, 0:J - 1], e.cont[:, 1:J], -1.0, 1.0, ALU.mult, ALU.add))
                if full:
                    link(dve.tensor_copy(e.key_i[:, :], key[:, :]))
                    for h in range(HEADS):
                        dve.tensor_copy(e.cont_h[:, h, :], e.cont[:, :])
                        dve.tensor_copy(e.end_h[:, h, :], end[:, :])
                        dve.tensor_scalar(e.next_h[:, h, :], end[:, :], -1.0, 1.0, ALU.mult, ALU.add)
                        link(dve.tensor_scalar(e.reset_h[:, h, :], e.cont[:, :], -1.0, BIG, ALU.add, ALU.mult))
                link(dve.tensor_tensor(goes_on[:, :], last, after[:, :], ALU.is_equal))
                link(dve.tensor_scalar(end[:, J - 1:J], goes_on[:, :], -1.0, 1.0, ALU.mult, ALU.add))
                link(dve.tensor_scalar(tmp[:, :], end[:, :], -FAR, FAR, ALU.mult, ALU.add))
                link(dve.tensor_tensor(tmp[:, :], tmp[:, :], key[:, :], ALU.add))
                link(dve.tensor_copy(e.put_i[:, :], tmp[:, :]))
                link(dve.tensor_tensor(whole[:, :], first, last, ALU.is_equal))
                link(dve.tensor_tensor(owns[:, :], whole[:, :], goes_on[:, :], ALU.mult))
                link(dve.tensor_scalar(owns[:, :], owns[:, :], -1.0, 1.0, ALU.mult, ALU.add))
                link(dve.tensor_tensor(fix[:, :], first, before[:, :], ALU.is_equal))
                link(dve.tensor_tensor(fix[:, :], fix[:, :], owns[:, :], ALU.mult))
                link(dve.tensor_scalar(fix[:, :], fix[:, :], -FAR, FAR, ALU.mult, ALU.add))
                link(dve.tensor_tensor(fix[:, :], fix[:, :], first, ALU.add))
                link(dve.tensor_copy(e.fix_i[:, :], fix[:, :]))
                dve.tensor_scalar(diag[:, 0, :], keep.ident[:, :], last, None, ALU.mult).then_inc(diag_ready, 1)
                dve.tensor_scalar(diag[:, 1, :], keep.ident[:, :], first, None, ALU.mult).then_inc(diag_ready, 1)
                dve.wait_ge(spread_done, 1)
                link(dve.tensor_scalar(e.carry[:, :], spread[:, 1, :], last, None, ALU.is_equal))
                link(dve.tensor_tensor(e.carry[:, :], e.carry[:, :], off[:, :], ALU.mult))
                if full:
                    for t, mine in enumerate((first, last)):
                        link(dve.tensor_scalar(e.same[t][:, :, :], spread[:, :, :], mine, None, ALU.is_equal))
                        link(dve.tensor_scalar(e.same_add[t][:, :, :], e.same[t][:, :, :], -1.0, BIG, ALU.add, ALU.mult))
                        link(dve.tensor_scalar(e.in_add[t][:, :], key[:, :], mine, None, ALU.is_equal))
                        link(dve.tensor_scalar(e.in_add[t][:, :], e.in_add[t][:, :], -1.0, BIG, ALU.add, ALU.mult))
                    link(dve.tensor_scalar(e.split[:, :], whole[:, :], -1.0, 1.0, ALU.mult, ALU.add))

            @block.tensor
            def _(pe):
                pe.wait_ge(diag_ready, 2)
                pe.matmul(spread[:, :, :], keep.ones[:, :], diag[:, :, :], start=True, stop=True).then_inc(spread_done, 1)
    return e


def spread_ends(pe, keep, heads, diag, spread_ps, diag_ready, spread_done, n):
    pe.wait_ge(diag_ready, n)
    pe.matmul(spread_ps[0][:, 0:heads * P], keep.ones[:, :], diag[:, 0, 0:heads, :], start=True, stop=True)
    pe.matmul(spread_ps[1][:, 0:heads * P], keep.ones[:, :], diag[:, 1, 0:heads, :], start=True, stop=True)\
        .then_inc(spread_done, 1)


def key_reduce(dve, link, keep, e, kind, heads, values, out, run, diag, cand, whole, ends, spread_ps, diag_ready,
               spread_done, n):
    def flat(a):
        return a[:, 0:heads, :].rearrange("p h j -> p (h j)")

    if kind == "max":
        link(dve.tensor_tensor_scan(flat(run), flat(e.reset_h), flat(values), -BIG, ALU.add, ALU.max))
    else:
        link(dve.tensor_tensor_scan(flat(run), flat(e.cont_h), flat(values), 0.0, ALU.mult, ALU.add))
    link(dve.tensor_tensor(flat(run), flat(run), flat(e.end_h), ALU.mult))
    link(dve.tensor_tensor_scan(flat(out)[:, ::-1], flat(e.next_h)[:, ::-1], flat(run)[:, ::-1], 0.0, ALU.mult, ALU.add))
    link(dve.tensor_copy(ends[:, 0, 0:heads], out[:, 0:heads, J - 1]))
    if kind == "max":
        link(dve.tensor_copy(ends[:, 1, 0:heads], out[:, 0:heads, 0]))
    else:
        link(dve.tensor_scalar(ends[:, 1, 0:heads], out[:, 0:heads, 0], e.split[:, 0:1], None, ALU.mult))
    for t in range(2):
        for h in range(heads):
            dve.tensor_scalar(diag[:, t, h, :], keep.ident[:, :], ends[:, t, h:h + 1], None, ALU.mult)\
                .then_inc(diag_ready, 1)
    dve.wait_ge(spread_done, n)
    for t in range(2):
        for u in range(2):
            mask = (e.same_add if kind == "max" else e.same)[t][:, u, :].unsqueeze(1).broadcast_to([P, heads, P])
            link(dve.tensor_tensor(cand[:, 0:heads, u, :], spread_ps[u][:, 0:heads * P].rearrange("p (h q) -> p h q", h=heads),
                                   mask, ALU.add if kind == "max" else ALU.mult))
        link(dve.tensor_reduce(whole[:, 0:heads], cand[:, 0:heads, :, :], AX.XY, ALU.max if kind == "max" else ALU.add))
        for h in range(heads):
            link(dve.scalar_tensor_tensor(out[:, h, :], e.in_add[t][:, :], whole[:, h:h + 1], out[:, h, :], ALU.add, ALU.max))


def reduce_memory(ph, heads):
    run, diag = ph.sb("run", [P, heads, J]), ph.sb("diag", [P, 2, heads, P])
    cand, whole, ends = ph.sb("cand", [P, heads, 2, P]), ph.sb("whole", [P, heads]), ph.sb("ends", [P, 2, heads])
    spread_ps = [ph.ps(f"spread_ps{t}", [P, 512]) for t in range(2)]
    return run, diag, cand, whole, ends, spread_ps, ph.sem("diag_ready"), ph.sem("spread_done")


def degrees(nc, keep, e):
    with Phase(nc, "deg") as ph:
        mem = reduce_memory(ph, 1)
        ones = ph.sb("ones", [P, 1, J])
        chain = ph.sem("chain")
        with nc.Block() as block:
            @block.vector
            def _(dve):
                link = linked(dve, chain)
                link(dve.memset(ones[:, :, :], 1.0))
                key_reduce(dve, link, keep, e, "sum", 1, ones, e.deg[:, :].unsqueeze(1), *mem, 1)
                link(dve.tensor_scalar(e.rdeg[:, :], e.deg[:, :], 1.0, None, ALU.max))
                link(dve.reciprocal(e.rdeg[:, :], e.rdeg[:, :]))

            @block.tensor
            def _(pe):
                spread_ends(pe, keep, 1, mem[1], mem[5], mem[6], mem[7], 2)


class Places:

    def __init__(self, engine, sem, first):
        self.engine, self.sem, self.first, self.n = engine, sem, first, 0

    def __call__(self, ins):
        ins.then_inc(self.sem, 1)
        self.n += 1
        return self.n

    def wait(self, place):
        self.engine.wait_ge(self.sem, self.first + place)


def edge_sum(nc, keep, name, e, agg, prepare, table=None, fetched=0):
    out_width = agg.shape[1]
    with Phase(nc, name, freed="written") as ph:
        msg = ph.sb("msg", [P, SLOTS, GC, ROW])
        get_s = ph.sb("get_s", [P, SLOTS, GC], I32)
        put_s = ph.sb("put_s", [P, SLOTS, GC], I32)
        fixed = ph.sb("fixed", [P, ROW])
        carry_ps = ph.ps("carry_ps", [P, 512])
        cleared, staged, go = ph.sem("cleared"), ph.sem("staged"), ph.sem("go")
        gathered = slot_sems(ph, "gathered", SLOTS)
        scattered, written = slot_sems(ph, "scattered", SLOTS), slot_sems(ph, "written", SLOTS)
        step, summed = ph.sem("step"), ph.sem("summed")
        carried, fix_in, fix_done, fix_out = ph.sem("carried"), ph.sem("fix_in"), ph.sem("fix_done"), ph.sem("fix_out")
        with nc.Block() as block:

            @block.scalar
            def _(act):
                ph.free_slots(act)

            @block.sync
            def _(sp):
                pass_on(sp, scattered, written)

            prepare.start(block, ph, msg, cleared, written)

            @block.gpsimd
            def _(pool):
                bound = pool.to_reg(NPAD - 1)
                pool.wait_ge(cleared, 2)

                def stage(turn, s, of, to, n):
                    pool.tensor_copy(to[:, s, :], of[:, bass.ds(turn * TURN + s * GC, GC)]).then_inc(staged, 1)
                    pool.wait_ge(staged, n)

                def gather(turn, s, n):
                    free(pool, written, turn, s)
                    stage(turn, s, e.other_i, get_s, n)
                    pool.sem_inc(go, 1)
                    for k in range(GC):
                        pool.indirect_dma_start(out=msg[:, s, k, 0:fetched], out_offset=None, in_=table,
                                                in_offset=bass.IndirectOffsetOnAxis(ap=get_s[:, s, k:k + 1], axis=0))\
                            .then_inc(gathered[s], 16)

                def scatter(turn, s, n):
                    pool.wait_ge(summed, turn * SLOTS + s + 1)
                    stage(turn, s, e.put_i, put_s, n)
                    pool.sem_inc(go, 1)
                    for k in range(GC):
                        pool.indirect_dma_start(out=agg, out_offset=bass.IndirectOffsetOnAxis(ap=put_s[:, s, k:k + 1], axis=0),
                                                in_=msg[:, s, k, 0:out_width], in_offset=None, bounds_check=bound,
                                                oob_is_err=False).then_inc(scattered[s], 16)

                if table is None:
                    with pool.Fori(0, TURNS) as turn:
                        for s in range(SLOTS):
                            scatter(turn, s, turn * SLOTS + s + 1)
                else:
                    gather(0, 0, 1)
                    gather(0, 1, 2)

                    def groups(turn, last):
                        for s in range(SLOTS):
                            n = turn * (2 * SLOTS) + 2 * s + 2
                            ahead = (s + 2) // SLOTS
                            more = not (last and ahead)
                            if more:
                                gather(turn + ahead, (s + 2) % SLOTS, n + 1)
                            scatter(turn, s, n + 2 if more else turn * (2 * SLOTS) + 6 + s - 1)

                    with pool.Fori(0, TURNS - 1) as turn:
                        groups(turn, False)
                    groups(TURNS - 1, True)
                for s in range(SLOTS):
                    done(pool, scattered, TURNS - 1, s, 16 * GC)
                pool.indirect_dma_start(out=fixed[:, 0:out_width], out_offset=None, in_=agg,
                                        in_offset=bass.IndirectOffsetOnAxis(ap=e.fix_i[:, 0:1], axis=0),
                                        bounds_check=bound, oob_is_err=False).then_inc(fix_in, 16)
                pool.wait_ge(fix_done, 1)
                pool.indirect_dma_start(out=agg, out_offset=bass.IndirectOffsetOnAxis(ap=e.fix_i[:, 0:1], axis=0),
                                        in_=fixed[:, 0:out_width], in_offset=None, bounds_check=bound,
                                        oob_is_err=False).then_inc(fix_out, 16)
                pool.wait_ge(fix_out, 16)

            @block.vector
            def _(dve):
                dve.memset(msg[:, :, :, :], 0.0).then_inc(cleared, 1)
                dve.memset(fixed[:, :], 0.0).then_inc(cleared, 1)
                dve.wait_ge(cleared, 1)
                per_turn = SLOTS * (GC + prepare.steps)
                with dve.Fori(0, TURNS) as turn:
                    count = Places(dve, step, turn * per_turn)
                    for s in range(SLOTS):
                        if table is None:
                            free(dve, written, turn, s)
                        else:
                            done(dve, gathered, turn, s, 16 * GC)

                        def add_before(k, ready):
                            before = msg[:, s, k - 1, 0:D] if k else msg[:, (s - 1) % SLOTS, GC - 1, 0:D]
                            count.wait(max(ready, add_before.last))
                            add_before.last = count(dve.scalar_tensor_tensor(
                                msg[:, s, k, 0:D], before, e.cont[:, bass.ds(turn * TURN + s * GC + k, 1)],
                                msg[:, s, k, 0:D], ALU.mult, ALU.add))

                        add_before.last = count.n
                        prepare(dve, turn, s, msg, count, add_before)
                        count.wait(count.n)
                        dve.sem_inc(summed, 1)
                    assert count.n == per_turn
                dve.wait_ge(carried, 1)
                dve.wait_ge(fix_in, 16)
                dve.tensor_tensor(fixed[:, 0:D], fixed[:, 0:D], carry_ps[:, 0:D], ALU.add).then_inc(fix_done, 1)

            @block.tensor
            def _(pe):
                pe.wait_ge(summed, TURNS * SLOTS)
                pe.matmul(carry_ps[:, 0:D], e.carry[:, :], msg[:, SLOTS - 1, GC - 1, 0:D], start=True, stop=True)\
                    .then_inc(carried, 1)


class PrepareMean:
    steps = 2

    def __init__(self, e):
        self.e = e

    def start(self, block, ph, msg, cleared, written):
        pass

    def __call__(self, dve, turn, s, msg, count, add_before):
        cols = bass.ds(turn * TURN + s * GC, GC)
        ready = count(dve.tensor_tensor(msg[:, s, :, 0:D], msg[:, s, :, 0:D],
                                        self.e.rdeg[:, cols].unsqueeze(2).broadcast_to([P, GC, D]), ALU.mult))
        count(dve.tensor_copy(msg[:, s, :, D], self.e.deg[:, cols]))
        for k in range(GC):
            add_before(k, ready)


class PrepareNorm:
    steps = 1

    def start(self, block, ph, msg, cleared, written):
        pass

    def __call__(self, dve, turn, s, msg, count, add_before):
        ready = count(dve.tensor_tensor(msg[:, s, :, 0:D], msg[:, s, :, 0:D],
                                        msg[:, s, :, D:D + 1].broadcast_to([P, GC, D]), ALU.mult))
        for k in range(GC):
            add_before(k, ready)


class PrepareAttention:
    steps = 2

    def __init__(self, rows, weight, tail):
        self.rows, self.weight, self.tail = rows, weight, tail

    def start(self, block, ph, msg, cleared, written):
        pass

    def __call__(self, dve, turn, s, msg, count, add_before):
        cols = bass.ds(turn * TURN + s * GC, GC)
        ready = count(dve.tensor_tensor(
            msg[:, s, :, 0:D].rearrange("p k (h d) -> p k h d", h=GAT_HEADS),
            self.rows[:, cols, 0:D].rearrange("p k (h d) -> p k h d", h=GAT_HEADS),
            self.weight[:, :, cols].rearrange("p h k -> p k h").unsqueeze(3).broadcast_to([P, GC, GAT_HEADS, GAT_D]), ALU.mult))
        count(dve.tensor_copy(msg[:, s, :, D:ROW], self.tail[:, :, cols].rearrange("p w k -> p k w")))
        for k in range(GC):
            add_before(k, ready)


class PrepareGatv2:
    steps = (HEADS - 1) * GC

    def __init__(self, keep, xt, wl, bl_parts, alpha):
        self.keep, self.xt, self.wl, self.bl_parts, self.alpha = keep, xt, wl, bl_parts, alpha

    def start(self, block, ph, msg, cleared, written):
        xg, alpha_s = ph.sb("xg", [P, 2, GC, P]), ph.sb("alpha_s", [P, 2, GC])
        self.xl_ps = [ph.ps(f"xl_ps{q}", [P, HD]) for q in range(GC)]
        copied, staged = ph.sem("copied"), ph.sem("alpha_staged")
        self.xl_ready, self.used, self.first_head = ph.sem("xl_ready"), ph.sem("used"), ph.sem("first_head")

        @block.scalar
        def _(act):
            def copy(turn, c):
                if c % GC == 0:
                    s = c // GC
                    after(act, self.xl_ready, turn, c, GC + 1, TURN)
                    act.activation(xg[:, s % 2].rearrange("p k n -> p (k n)"),
                                   self.xt[:, bass.ds((turn * TURN + c) * P, GC * P)], ACT.Copy).then_inc(copied, 1)
                    after(act, self.first_head, turn, c, GC + 1, TURN)
                    act.activation(alpha_s[:, s % 2, :], self.alpha[:, 0, bass.ds(turn * TURN + c, GC)], ACT.Copy)\
                        .then_inc(staged, 1)

            def head(turn, c):
                s, k = c // GC, c % GC
                if k == 0:
                    free(act, written, turn, s)
                    act.wait_ge(staged, turn * SLOTS + s + 1)
                act.wait_ge(self.xl_ready, turn * TURN + c + 1)
                act.activation(msg[:, s, k, 0:D], self.xl_ps[k][:, 0:D], ACT.Copy, scale=alpha_s[:, s % 2, k:k + 1])\
                    .then_inc(self.first_head, 1)

            act.wait_ge(cleared, 1)
            pipeline(act, (GC + 1, head), (0, copy), per_turn=TURN, total=J)

        @block.tensor
        def _(pe):
            def product(turn, c):
                s, k = c // GC, c % GC
                if k == 0:
                    pe.wait_ge(copied, turn * SLOTS + s + 1)
                after(pe, self.used, turn, c, GC, TURN)
                pe.matmul(self.xl_ps[k][:, :], xg[:, s % 2, k, :], self.wl[:, :], start=True, stop=False)
                pe.matmul(self.xl_ps[k][:, :], self.keep.ones_b[0:3, :], self.bl_parts[0:3, :],
                          start=False, stop=True).then_inc(self.xl_ready, 1)
            pipeline(pe, (0, product), per_turn=TURN, total=J)

    def __call__(self, dve, turn, s, msg, count, add_before):
        ready = [0] * GC

        def head(k, h):
            c = s * GC + k
            part, weight = self.xl_ps[k][:, h * D:(h + 1) * D], self.alpha[:, h, bass.ds(turn * TURN + c, 1)]
            if h == 1:
                dve.wait_ge(self.first_head, turn * TURN + c + 1)
            else:
                count.wait(ready[k])
            ready[k] = count(dve.scalar_tensor_tensor(msg[:, s, k, 0:D], part, weight, msg[:, s, k, 0:D],
                                                      ALU.mult, ALU.add))

        for k in range(0, GC, 2):
            pair = range(k, min(k + 2, GC))
            for h in range(1, HEADS):
                for q in pair:
                    head(q, h)
                if k and h < 3:
                    add_before(k - 3 + h, ready[k - 3 + h])
            count.wait(ready[pair[-1]])
            dve.sem_inc(self.used, len(pair))
        for k in range(GC - 1 - (GC - 1) % 2, GC):
            add_before(k, ready[k])


GAT_HEADS, GAT_D = 2, D // 2


def after(engine, sem, turn, place, lag, per_turn):
    n = turn * per_turn + place + 1 - lag
    if not isinstance(n, int) or n > 0:
        engine.wait_ge(sem, n)


class Steps:

    def __init__(self, engine, sem, turn, per_turn):
        self.engine, self.sem, self.first, self.per_turn, self.n = engine, sem, turn * per_turn, per_turn, 0

    def __call__(self, ins):
        ins.then_inc(self.sem, 1)
        self.n += 1

    def wait(self):
        self.engine.wait_ge(self.sem, self.first + self.n)



LN_EPS = 1e-05
BANKS = 2
NTURN = NB // SLOT


def norm_sums(dve, aside, r, stats, mv, done):
    for g in range(GB):
        ins = dve.bn_stats(stats[:, g, :], r[:, g, :])
    aside(ins)
    aside.wait()
    dve.sem_inc(aside.sem, 1)
    aside.n += 1
    for g in range(GB):
        ins = dve.bn_aggr(mv[:, g, :], stats[:, g, :])
    ins.then_inc(done, 1)


NORM_STEPS = 2


def norm_scale(pool, keep, st, mv, rstd, done):
    st(pool.tensor_tensor(rstd, mv[:, :, 1], keep.eps[:, :], ALU.add))
    st.wait()
    pool.tensor_tensor(rstd, rstd, keep.minus_half[:, :], ALU.pow).then_inc(done, 1)


def norm_shift(pool, keep, st, mv, rstd, shift, done):
    st(pool.tensor_tensor(rstd, mv[:, :, 1], keep.eps[:, :], ALU.add))
    st.wait()
    st(pool.tensor_tensor(rstd, rstd, keep.minus_half[:, :], ALU.pow))
    st.wait()
    st(pool.tensor_tensor(shift, mv[:, :, 0], rstd, ALU.mult))
    st.wait()
    pool.tensor_tensor(shift, shift, keep.minus_one[:, :], ALU.mult).then_inc(done, 1)


SHIFT_STEPS = 3


def norm_act(act, r, rstd, shift, out):
    for g in range(GB):
        ins = act.activation(out[:, g, 0:D], r[:, g, :], ACT.Identity, bias=shift[:, g:g + 1], scale=rstd[:, g:g + 1])
    return ins


def norm_apply(dve, r, mv, rstd, out):
    for g in range(GB):
        ins = dve.tensor_scalar(out[:, g, 0:D], r[:, g, :], mv[:, g, 0:1], rstd[:, g:g + 1], ALU.subtract, ALU.mult)
    return ins


def block_rows(a, turn, s):
    return a.rearrange("(t s p g) d -> t s p g d", s=SLOT, p=P, g=GB)[turn, s] if isinstance(turn, int) else \
        a.rearrange("(t s p g) d -> t s p g d", s=SLOT, p=P, g=GB)[bass.ds(turn, 1), s].squeeze(0)


def pipeline(engine, *stages, per_turn=SLOT, total=NB):
    first = max(lag for lag, _ in stages) // per_turn + 1

    def steps(turn, peeled):
        for s in range(per_turn):
            for lag, fn in stages:
                if not peeled or 0 <= turn * per_turn + s - lag < total:
                    fn(turn + (s - lag) // per_turn, (s - lag) % per_turn)

    for turn in range(first):
        steps(turn, True)
    with engine.Fori(first, total // per_turn) as turn:
        steps(turn, False)
    for turn in range(total // per_turn, total // per_turn + first):
        steps(turn, True)


def node_sage(nc, keep, x, agg, w, bias, x1):
    with Phase(nc, "n0", freed="turned added stored y_ready x1_ready") as ph:
        wa, wb, b, b_rest = ph.sb("wa", [P, D]), ph.sb("wb", [P, D]), ph.sb("b", [1, D]), ph.sb("b_rest", [1, D])
        bias_part, bias_parts = [ph.sb(f"bias_part{i}", [1, D], BF16) for i in range(3)], ph.sb("bias_parts", [3, GB, D], BF16)
        xs, ag = ph.sb("xs", [P, SLOT, GB, D]), ph.sb("ag", [P, SLOT, GB, ROW])
        shift = ph.sb("shift", [P, SLOT, GB])
        o = ph.sb("o", [P, SLOT, GB, ROW])
        xt, at = ph.sb("xt", [P, SLOT, GB, P]), ph.sb("at", [P, SLOT, GB, P])
        stats, mv, rstd = ph.sb("stats", [P, SLOT, GB, 6]), ph.sb("mv", [P, SLOT, GB, 2]), ph.sb("rstd", [P, SLOT, GB])
        xt_ps = [ph.ps(f"xt_ps{q}", [P, GB, P]) for q in range(BANKS)]
        at_ps = [ph.ps(f"at_ps{q}", [P, GB, P]) for q in range(BANKS)]
        y_ps = [ph.ps(f"y_ps{s}", [P, GB, D]) for s in range(SLOT)]
        w_ready = ph.sem("w_ready")
        chain, parts_split, parts_in = ph.sem("chain"), ph.sem("parts_split"), ph.sem("parts_in")
        weights, added = ph.sem("weights"), slot_sems(ph, "added")
        x_in, ag_in = slot_sems(ph, "x_in"), slot_sems(ph, "ag_in")
        stored = slot_sems(ph, "stored")
        turned, moved, y_ready, x1_ready, steps = (
            slot_sems(ph, "turned"), slot_sems(ph, "moved"), slot_sems(ph, "y_ready"), slot_sems(ph, "x1_ready"), ph.sem("steps"))
        sums_ready, rstd_ready, cleared, pool_step, norm_step = (
            slot_sems(ph, "sums_ready"), slot_sems(ph, "rstd_ready"), ph.sem("cleared"), ph.sem("pool_step"), ph.sem("norm_step"))
        with nc.Block() as block:
            @block.sync
            def _(sp):
                sp.dma_start(wa[:, :], w[0:D, :]).then_inc(weights, 16)
                sp.dma_start(wb[:, :], w[D:2 * D, :]).then_inc(weights, 16)
                sp.dma_start(b[:, :], bias.unsqueeze(0)).then_inc(weights, 16)
                sp.wait_ge(parts_split, 1)
                for i in range(3):
                    for g in range(GB):
                        sp.dma_start(bias_parts[i:i + 1, g, :], bias_part[i][:, :]).then_inc(parts_in, 16)
                with sp.Fori(0, NTURN) as turn:
                    used = sp.snap(turn + 1)
                    for s in range(SLOT):
                        sp.wait_ge(added[s], used)
                        sp.wait_ge(turned[s], used)
                        sp.dma_start(xs[:, s], block_rows(x, turn, s)).then_inc(x_in[s], 16)
                        sp.dma_start(ag[:, s], block_rows(agg, turn, s)).then_inc(ag_in[s], 16)

            @block.gpsimd
            def _(pool):
                pool.wait_ge(cleared, 1)

                def degree(turn, s):
                    st = Steps(pool, pool_step, turn * SLOT + s, 1)
                    done(pool, ag_in, turn, s, 16)
                    free(pool, stored, turn, s, 16)
                    st(pool.tensor_tensor(o[:, s, :, D], ag[:, s, :, D], keep.ones[:, 0:GB], ALU.add))
                    st.wait()
                    pool.tensor_tensor(o[:, s, :, D], o[:, s, :, D], keep.minus_half[:, :], ALU.pow).then_inc(added[s], 1)

                def deviation(turn, s):
                    done(pool, sums_ready, turn, s)
                    norm_shift(pool, keep, Steps(pool, norm_step, turn * SLOT + s, SHIFT_STEPS), mv[:, s], rstd[:, s, :],
                               shift[:, s, :], rstd_ready[s])

                pipeline(pool, (3, deviation), (1, degree))

            @block.tensor
            def _(pe):
                pe.wait_ge(w_ready, 1)
                pe.wait_ge(parts_in, 16 * 3 * GB)

                def turn_over(turn, s):
                    done(pe, x_in, turn, s, 16)
                    done(pe, ag_in, turn, s, 16)
                    bank_free(pe, moved, turn, s, 2, BANKS)
                    for g in range(GB):
                        pe.transpose(xt_ps[s % BANKS][:, g, :], xs[:, s, g, :], keep.ident[:, :])
                    for g in range(GB):
                        ins = pe.transpose(at_ps[s % BANKS][:, g, :], ag[:, s, g, 0:D], keep.ident[:, :])
                    ins.then_inc(turned[s], 1)

                def product(turn, s):
                    done(pe, moved, turn, s, 2)
                    free(pe, x1_ready, turn, s)
                    pe.matmul(y_ps[s][:, :, :], keep.ones_b[0:3, :], bias_parts[:, :, :], start=True, stop=False, skip_group_check=True)
                    for g in range(GB):
                        pe.matmul(y_ps[s][:, g, :], xt[:, s, g, :], wa[:, :], start=False, stop=False, skip_group_check=True)
                        ins = pe.matmul(y_ps[s][:, g, :], at[:, s, g, :], wb[:, :], start=False, stop=g == GB - 1,
                                        skip_group_check=True)
                    ins.then_inc(y_ready[s], 1)

                pipeline(pe, (2, product), (0, turn_over))

            @block.scalar
            def _(act):
                ph.free_slots(act)
                act.wait_ge(cleared, 1)

                def apply(turn, s):
                    done(act, rstd_ready, turn, s)
                    free(act, stored, turn, s, 16)
                    norm_act(act, y_ps[s], rstd[:, s], shift[:, s], o[:, s]).then_inc(x1_ready[s], 1)

                def store(turn, s):
                    done(act, x1_ready, turn, s)
                    done(act, added, turn, s)
                    act.dma_start(block_rows(x1, turn, s), o[:, s]).then_inc(stored[s], 16)

                def move(turn, s):
                    done(act, turned, turn, s)
                    free(act, y_ready, turn, s)
                    act.activation(xt[:, s], xt_ps[s % BANKS][:, :, :], ACT.Copy).then_inc(moved[s], 1)
                    act.activation(at[:, s], at_ps[s % BANKS][:, :, :], ACT.Copy).then_inc(moved[s], 1)

                pipeline(act, (3, apply), (0, move), (3, store))
                for s in range(SLOT):
                    done(act, stored, NTURN - 1, s, 16)

            @block.vector
            def _(dve):
                dve.memset(o[:, :, :, :], 0.0).then_inc(cleared, 1)

                link = linked(dve, chain)
                dve.wait_ge(weights, 48)
                link(dve.tensor_tensor(wa[:, :], wa[:, :], keep.ident[:, :], ALU.add))
                split_bf16(dve, link, b[:, :], b_rest[:, :], [p[:, :] for p in bias_part])
                dve.sem_inc(parts_split, 1)
                dve.sem_inc(w_ready, 1)

                def sums(turn, s):
                    done(dve, y_ready, turn, s)
                    norm_sums(dve, Steps(dve, steps, turn * SLOT + s, NORM_STEPS), y_ps[s], stats[:, s], mv[:, s], sums_ready[s])

                pipeline(dve, (2, sums))


def node_gcn(nc, keep, name, z, agg, w, beta, out, x1=None):
    with Phase(nc, name, freed="scaled dis_kept xp_ready turned y_ready sums_ready stored") as ph:
        wm = ph.sb("wm", [P, D])
        zs, ag = ph.sb("zs", [P, SLOT, GB, ROW]), ph.sb("ag", [P, SLOT, GB, D])
        t, c1, c2 = ph.sb("t", [P, SLOT, GB, D]), ph.sb("c1", [P, SLOT, GB]), ph.sb("c2", [P, SLOT, GB])
        xp, xt = ph.sb("xp", [P, SLOT, GB, D]), ph.sb("xt", [P, SLOT, GB, P])
        width = out.shape[1]
        o = ph.sb("o", [P, SLOT, GB, width])
        xr = ph.sb("xr", [P, SLOT, GB, ROW]) if x1 is not None else None
        r = ph.sb("r", [P, SLOT, GB, D])
        stats, mv, rstd = ph.sb("stats", [P, SLOT, GB, 6]), ph.sb("mv", [P, SLOT, GB, 2]), ph.sb("rstd", [P, SLOT, GB])
        t_ps = [ph.ps(f"t_ps{q}", [P, GB, P]) for q in range(BANKS)]
        y_ps = [ph.ps(f"y_ps{q}", [P, GB, D]) for q in range(BANKS)]
        shift, own_ready = ph.sb("shift", [P, SLOT, GB]), slot_sems(ph, "own_ready")
        dis_kept = slot_sems(ph, "dis_kept")
        weights, mixed, w_ready = ph.sem("weights"), ph.sem("mixed"), ph.sem("w_ready")
        z_in = slot_sems(ph, "z_in")
        ag_in = slot_sems(ph, "ag_in")
        r_in = slot_sems(ph, "r_in")
        stored = slot_sems(ph, "stored")
        pstep, scaled, xp_ready, turned, moved, y_ready, out_ready, steps = (
            ph.sem("pstep"), slot_sems(ph, "scaled"), slot_sems(ph, "xp_ready"), slot_sems(ph, "turned"), slot_sems(ph, "moved"),
            slot_sems(ph, "y_ready"), slot_sems(ph, "out_ready"), ph.sem("steps"))
        sums_ready, rstd_ready, pool_step = slot_sems(ph, "sums_ready"), slot_sems(ph, "rstd_ready"), ph.sem("pool_step")
        last = x1 is not None
        with nc.Block() as block:
            @block.sync
            def _(sp):
                sp.dma_start(wm[:, :], w).then_inc(weights, 16)
                with sp.Fori(0, NTURN) as turn:
                    used = sp.snap(turn + 1)
                    for s in range(SLOT):
                        sp.wait_ge((scaled if last else dis_kept)[s], used)
                        sp.wait_ge(xp_ready[s], used)
                        sp.dma_start(zs[:, s], block_rows(z, turn, s)).then_inc(z_in[s], 16)
                        sp.dma_start(ag[:, s], block_rows(agg, turn, s)).then_inc(ag_in[s], 16)

            @block.gpsimd
            def _(pool):
                def scale(turn, s):
                    st = Steps(pool, pstep, turn * SLOT + s, 4)
                    done(pool, z_in, turn, s, 16)
                    free(pool, xp_ready, turn, s)
                    pool.sem_inc(pstep, 1)
                    st.n += 1
                    st(pool.tensor_scalar(c1[:, s, :], zs[:, s, :, D], 0.9, None, ALU.mult))
                    st.wait()
                    st(pool.tensor_tensor(c2[:, s, :], c1[:, s, :], zs[:, s, :, D], ALU.mult))
                    st.wait()
                    pool.sem_inc(pstep, 1)
                    st.n += 1
                    pool.tensor_scalar(c2[:, s, :], c2[:, s, :], 0.1, None, ALU.add).then_inc(scaled[s], 1)

                def pass_on_dis(turn, s):
                    done(pool, z_in, turn, s, 16)
                    free(pool, stored, turn, s, 16)
                    pool.tensor_tensor(o[:, s, :, D:ROW], zs[:, s, :, D:ROW],
                                       keep.ones[:, 0:GB * (ROW - D)].rearrange("p (g w) -> p g w", g=GB), ALU.mult)\
                        .then_inc(dis_kept[s], 1)

                def deviation(turn, s):
                    done(pool, sums_ready, turn, s)
                    norm_shift(pool, keep, Steps(pool, pool_step, turn * SLOT + s, SHIFT_STEPS), mv[:, s], rstd[:, s, :],
                               shift[:, s, :], rstd_ready[s])

                pipeline(pool, (4, deviation) if last else (1, pass_on_dis), (0, scale))

            @block.tensor
            def _(pe):
                pe.wait_ge(w_ready, 1)

                def turn_over(turn, s):
                    done(pe, xp_ready, turn, s)
                    bank_free(pe, moved, turn, s, 1, BANKS)
                    for g in range(GB):
                        ins = pe.transpose(t_ps[s % BANKS][:, g, :], xp[:, s, g, :], keep.ident[:, :])
                    ins.then_inc(turned[s], 1)

                def product(turn, s):
                    done(pe, moved, turn, s)
                    bank_free(pe, sums_ready if last else out_ready, turn, s, 1, BANKS)
                    for g in range(GB):
                        ins = pe.matmul(y_ps[s % BANKS][:, g, :], xt[:, s, g, :], wm[:, :], start=True, stop=True)
                    ins.then_inc(y_ready[s], 1)

                pipeline(pe, (2, product), (1, turn_over))

            @block.scalar
            def _(act):
                ph.free_slots(act)
                def load_x1(turn, s):
                    free(act, sums_ready, turn, s)
                    act.dma_start(xr[:, s], block_rows(x1, turn, s)).then_inc(r_in[s], 16)

                def own(turn, s):
                    done(act, scaled, turn, s)
                    free(act, xp_ready, turn, s)
                    for g in range(GB):
                        ins = act.activation(t[:, s, g, :], zs[:, s, g, 0:D], ACT.Copy, scale=c2[:, s, g:g + 1])
                    ins.then_inc(own_ready[s], 1)

                def apply(turn, s):
                    done(act, rstd_ready, turn, s)
                    free(act, stored, turn, s, 16)
                    norm_act(act, r[:, s], rstd[:, s], shift[:, s], o[:, s]).then_inc(out_ready[s], 1)

                def move(turn, s):
                    done(act, turned, turn, s)
                    free(act, y_ready, turn, s)
                    act.activation(xt[:, s], t_ps[s % BANKS][:, :, :], ACT.Copy).then_inc(moved[s], 1)

                def keep_z(turn, s):
                    done(act, y_ready, turn, s)
                    free(act, stored, turn, s, 16)
                    act.activation(o[:, s, :, 0:D], y_ps[s % BANKS][:, :, :], ACT.Copy).then_inc(out_ready[s], 1)

                def store(turn, s):
                    done(act, out_ready, turn, s)
                    if not last:
                        done(act, dis_kept, turn, s)
                    act.dma_start(block_rows(out, turn, s), o[:, s]).then_inc(stored[s], 16)

                if last:
                    pipeline(act, (5, store), (4, apply), (0, load_x1), (0, own), (1, move))
                else:
                    pipeline(act, (3, store), (0, own), (1, move), (2, keep_z))
                for s in range(SLOT):
                    done(act, stored, NTURN - 1, s, 16)

            @block.vector
            def _(dve):
                dve.wait_ge(weights, 16)
                dve.tensor_scalar(r[:, 0, 0, :], keep.ident[:, :], 1.0 - beta, None, ALU.mult).then_inc(mixed, 1)
                dve.wait_ge(mixed, 1)
                dve.scalar_tensor_tensor(wm[:, :], wm[:, :], beta, r[:, 0, 0, :], ALU.mult, ALU.add).then_inc(w_ready, 1)
                dve.wait_ge(w_ready, 1)

                def mix(turn, s):
                    done(dve, own_ready, turn, s)
                    done(dve, ag_in, turn, s, 16)
                    free(dve, turned, turn, s)
                    for g in range(GB):
                        ins = dve.scalar_tensor_tensor(xp[:, s, g, :], ag[:, s, g, :], c1[:, s, g:g + 1], t[:, s, g, :],
                                                       ALU.mult, ALU.add)
                    ins.then_inc(xp_ready[s], 1)

                def sums(turn, s):
                    st = Steps(dve, steps, turn * SLOT + s, NORM_STEPS + 1)
                    done(dve, y_ready, turn, s)
                    done(dve, r_in, turn, s, 16)
                    st(dve.tensor_tensor(r[:, s], y_ps[s % BANKS][:, :, :], xr[:, s, :, 0:D], ALU.add))
                    st.wait()
                    norm_sums(dve, st, r[:, s], stats[:, s], mv[:, s], sums_ready[s])

                pipeline(dve, *([(3, sums)] if last else []), (0, mix))


def split_bf16(engine, link, value, rest, parts):
    link(engine.tensor_copy(parts[0], value))
    link(engine.tensor_tensor(rest, value, parts[0], ALU.subtract))
    link(engine.tensor_copy(parts[1], rest))
    link(engine.tensor_tensor(rest, rest, parts[1], ALU.subtract))
    link(engine.tensor_copy(parts[2], rest))


ATT_PARTS = ((0, 0), (0, 1), (0, 2), (1, 0), (1, 1), (2, 0))
PARTS_IN = len(ATT_PARTS) * ATT_IN + 3


def gatv2_weights(nc, keep, stack, w):
    g = Keep()

    def sb(name, shape, dt=F32):
        return stack.enter_context(nc.sbuf_tensor(f"gat2_{name}", shape, dt))

    g.wl, g.wr, g.att = sb("wl", [P, HD]), sb("wr", [P, HD]), sb("att", [P, HD])
    g.edge, g.bl_parts = sb("edge", [PARTS_IN, HD], BF16), sb("bl_parts", [3, HD], BF16)
    with Phase(nc, "g2w") as ph:
        both = ph.sb("both", [1, 3, HD])
        part, bias_part = ([ph.sb(f"{n}{i}", [1, HD], BF16) for i in range(3)] for n in ("part", "bias_part"))
        we, we_rest = ph.sb("we", [ATT_IN, HD]), ph.sb("we_rest", [ATT_IN, HD])
        we_part = [ph.sb(f"we_part{i}", [ATT_IN, HD], BF16) for i in range(3)]
        loaded, chain, summed, edge_in, spread = (ph.sem("loaded"), ph.sem("chain"), ph.sem("summed"), ph.sem("edge_in"),
                                                 ph.sem("spread"))
        with nc.Block() as block:
            @block.sync
            def _(sp):
                sp.dma_start(both[0:1, 0, :], w["bl"].unsqueeze(0)).then_inc(loaded, 16)
                sp.dma_start(both[0:1, 1, :], w["br"].unsqueeze(0)).then_inc(loaded, 16)
                sp.dma_start(we[:, :], w["We"]).then_inc(loaded, 16)
                sp.dma_start(g.wl[:, :], w["Wl"]).then_inc(edge_in, 16)
                sp.dma_start(g.wr[:, :], w["Wr"]).then_inc(edge_in, 16)
                sp.dma_start(g.att[:, :], w["att"].rearrange("h d -> (h d)").partition_broadcast(P)).then_inc(edge_in, 16)
                sp.wait_ge(summed, 1)
                for n, (_, of_w) in enumerate(ATT_PARTS):
                    sp.dma_start(g.edge[n * ATT_IN:(n + 1) * ATT_IN, :], we_part[of_w][:, :]).then_inc(spread, 16)
                for i in range(3):
                    row = len(ATT_PARTS) * ATT_IN + i
                    sp.dma_start(g.edge[row:row + 1, :], bias_part[i][0:1, :]).then_inc(spread, 16)
                    sp.dma_start(g.bl_parts[i:i + 1, :], part[i][0:1, :]).then_inc(spread, 16)
                sp.wait_ge(edge_in, 48)
                sp.wait_ge(spread, 16 * (6 + len(ATT_PARTS)))

            @block.vector
            def _(dve):
                link = linked(dve, chain)
                dve.wait_ge(loaded, 48)
                link(dve.tensor_tensor(both[0:1, 2, :], both[0:1, 0, :], both[0:1, 1, :], ALU.add))
                split_bf16(dve, link, both[0:1, 0, :], both[0:1, 1, :], [p[0:1, :] for p in part])
                split_bf16(dve, link, both[0:1, 2, :], both[0:1, 1, :], [p[0:1, :] for p in bias_part])
                split_bf16(dve, link, we[:, :], we_rest[:, :], [p[:, :] for p in we_part])
                dve.sem_inc(summed, 1)
    return g


def gatv2_logits(nc, keep, e, g, x, xt, logits):
    with Phase(nc, "lg", freed="turned") as ph:
        rows = ph.sb("rows", [P, SLOTS, GC, 2, D])
        get_s = ph.sb("get_s", [P, SLOTS, 2, GC], I32)
        att_s = ph.sb("att_s", [P, SLOTS, GC, ATT_IN])
        rest = ph.sb("rest", [P, 2, GC, ATT_IN])
        parts = ph.sb("parts", [P, 2, GC, PARTS_IN], BF16)
        tr = ph.sb("tr", [P, 2, 2, P])
        at = ph.sb("at", [PARTS_IN, 2, P], BF16)
        z = ph.sb("z", [P, 2, HD])
        junk = ph.sb("junk", [P, 2, HD])
        sums = ph.sb("sums", [P, 2, HEADS, GC])
        tr_ps = [ph.ps(f"tr_ps{q}", [P, 4, P]) for q in range(2)]
        at_ps = [ph.ps(f"at_ps{q}", [P, 1024], BF16) for q in range(2)]
        z_ps = [ph.ps(f"z_ps{q}", [P, HD]) for q in range(2)]
        gathered = slot_sems(ph, "gathered", SLOTS)
        turned = slot_sems(ph, "turned", SLOTS)
        staged, go, moved, moved_att = ph.sem("staged"), ph.sem("go"), ph.sem("moved"), ph.sem("moved_att")
        z_low, split_steps, parts_ready = ph.sem("z_low"), ph.sem("split_steps"), ph.sem("parts_ready")
        z_ready, z_out, scored, grouped, stage_go = (ph.sem("z_ready"), ph.sem("z_out"), ph.sem("scored"), ph.sem("grouped"), ph.sem("stage_go"))
        with nc.Block() as block:
            @block.gpsimd
            def _(pool):
                with pool.Fori(0, TURNS) as turn:
                    for s in range(SLOTS):
                        free(pool, turned, turn, s, GC)
                        cols = bass.ds(turn * TURN + s * GC, GC)
                        pool.sem_inc(stage_go, 1)
                        pool.tensor_copy(get_s[:, s, 0, :], e.other_i[:, cols]).then_inc(staged, 1)
                        pool.tensor_copy(get_s[:, s, 1, :], e.key_i[:, cols]).then_inc(staged, 1)
                        pool.tensor_copy(att_s[:, s], e.att[:, cols, :]).then_inc(staged, 1)
                        pool.wait_ge(staged, turn * (3 * SLOTS) + 3 * s + 3)
                        pool.sem_inc(go, 1)
                        for k in range(GC):
                            for i in range(2):
                                pool.indirect_dma_start(out=rows[:, s, k, i, :], out_offset=None, in_=x,
                                                        in_offset=bass.IndirectOffsetOnAxis(ap=get_s[:, s, i, k:k + 1], axis=0))\
                                    .then_inc(gathered[s], 16)

            @block.tensor
            def _(pe):
                def turn_over(turn, c):
                    s, k, q = c // GC, c % GC, c % 2
                    if k == 0:
                        pe.wait_ge(gathered[s], turn * (32 * GC) + 32 * GC)
                        pe.wait_ge(parts_ready, turn * SLOTS + s + 2)
                    after(pe, moved, turn, c, 2, TURN)
                    after(pe, moved_att, turn, c, 2, TURN)
                    for i in range(2):
                        pe.transpose(tr_ps[q][:, i, :], rows[:, s, k, i, :], keep.ident[:, :])
                    pe.transpose(at_ps[q][0:PARTS_IN, 0:P], parts[:, s % 2, k, :], keep.ident_b[:, :]).then_inc(turned[s], 1)

                def product(turn, c):
                    q = c % 2
                    pe.wait_ge(moved, turn * TURN + c + 1)
                    pe.wait_ge(moved_att, turn * TURN + c + 1)
                    after(pe, z_out, turn, c, 2, TURN)
                    pe.matmul(z_ps[q][:, :], tr[:, q, 0, :], g.wl[:, :], start=True, stop=False)
                    pe.matmul(z_ps[q][:, :], tr[:, q, 1, :], g.wr[:, :], start=False, stop=False)
                    pe.matmul(z_ps[q][:, :], at[:, q, :], g.edge[:, :], start=False, stop=True).then_inc(z_ready, 1)

                pipeline(pe, (0, turn_over), (1, product), per_turn=TURN, total=J)

            @block.scalar
            def _(act):
                ph.free_slots(act)
                def move(turn, c):
                    s, k, q = c // GC, c % GC, c % 2
                    act.wait_ge(turned[s], turn * GC + k + 1 + turned.base)
                    after(act, z_ready, turn, c, 2, TURN)
                    act.activation(tr[:, q, :, :], tr_ps[q][:, 0:2, :], ACT.Copy)
                    act.activation(xt[:, bass.ds((turn * TURN + c) * P, P)], tr_ps[q][:, 0, :], ACT.Copy).then_inc(moved, 1)

                def low(turn, c):
                    act.wait_ge(z_ready, turn * TURN + c + 1)
                    after(act, scored, turn, c, 2, TURN)
                    act.activation(z[:, c % 2, :], z_ps[c % 2][:, :], ACT.Copy, scale=SLOPE).then_inc(z_low, 1)

                pipeline(act, (0, move), (1, low), per_turn=TURN, total=J)

            @block.vector
            def _(dve):
                ones = len(ATT_PARTS) * ATT_IN
                dve.memset(parts[:, :, :, ones:PARTS_IN], 1.0).then_inc(parts_ready, 1)

                def split(turn, c):
                    if c % GC:
                        return
                    s = c // GC
                    q, att, st = s % 2, att_s[:, s], Steps(dve, split_steps, turn * SLOTS + s, 4)
                    dve.wait_ge(staged, turn * (3 * SLOTS) + 3 * s + 3)
                    dve.wait_ge(turned[(s - 2) % SLOTS], (turn + (s - 2) // SLOTS + 1) * GC + turned.base)

                    def part(first, count):
                        return parts[:, q, :, first * ATT_IN:(first + count) * ATT_IN].rearrange("p k (n a) -> p k n a", n=count)

                    st(dve.tensor_copy(part(0, 3), att.unsqueeze(2).broadcast_to([P, GC, 3, ATT_IN])))
                    st.wait()
                    st(dve.tensor_tensor(rest[:, q], att, parts[:, q, :, 0:ATT_IN], ALU.subtract))
                    st.wait()
                    st(dve.tensor_copy(part(3, 2), rest[:, q].unsqueeze(2).broadcast_to([P, GC, 2, ATT_IN])))
                    st.wait()
                    st(dve.tensor_tensor(rest[:, q], rest[:, q], parts[:, q, :, 3 * ATT_IN:4 * ATT_IN], ALU.subtract))
                    st.wait()
                    dve.tensor_copy(parts[:, q, :, 5 * ATT_IN:6 * ATT_IN], rest[:, q]).then_inc(parts_ready, 1)

                def move(turn, c):
                    s, k, q = c // GC, c % GC, c % 2
                    dve.wait_ge(turned[s], turn * GC + k + 1 + turned.base)
                    after(dve, z_ready, turn, c, 2, TURN)
                    dve.tensor_copy(at[:, q, :], at_ps[q][0:PARTS_IN, 0:P]).then_inc(moved_att, 1)

                def leaky(turn, c):
                    dve.wait_ge(z_low, turn * TURN + c + 1)
                    dve.tensor_tensor(z[:, c % 2, :], z_ps[c % 2][:, :], z[:, c % 2, :], ALU.max).then_inc(z_out, 1)

                def score(turn, c):
                    s, k, q = c // GC, c % GC, c % 2
                    dve.wait_ge(z_out, turn * TURN + c + 1)
                    if k == 0:
                        after(dve, grouped, turn, s, 2, SLOTS)
                    for h in range(HEADS):
                        part = slice(h * D, (h + 1) * D)
                        ins = dve.tensor_tensor_reduce(junk[:, q, part], z[:, q, part], g.att[:, part], 1.0, 0.0,
                                                       ALU.mult, ALU.add, sums[:, s % 2, h, k:k + 1])
                    ins.then_inc(scored, 1)
                    if k == GC - 1:
                        dve.wait_ge(scored, turn * TURN + c + 1)
                        dve.tensor_copy(logits[:, :, bass.ds(turn * TURN + s * GC, GC)], sums[:, s % 2]).then_inc(grouped, 1)

                pipeline(dve, (0, split), (4, move), (5, leaky), (6, score), per_turn=TURN, total=J)


SLOPE = 0.2


def softmax(nc, keep, e, heads, logits, out, name, make_logits=None, top=None, total=None):
    with Phase(nc, name) as ph:
        mem = reduce_memory(ph, heads)
        red = ph.sb("red", [P, heads, J])
        chain, ready, done = ph.sem("chain"), ph.sem("ready"), ph.sem("done")
        top = top if top is not None else red[:, :, :]
        with nc.Block() as block:
            @block.vector
            def _(dve):
                link = linked(dve, chain)
                if make_logits is not None:
                    make_logits(dve, link)
                key_reduce(dve, link, keep, e, "max", heads, logits, top, *mem, 1)
                link(dve.tensor_tensor(logits, logits, top, ALU.subtract))
                dve.sem_inc(ready, 1)
                dve.wait_ge(done, 1)
                sums = total if total is not None else red[:, :, :]
                key_reduce(dve, link, keep, e, "sum", heads, out, sums, *mem, 2)
                if total is None:
                    link(dve.tensor_scalar(sums, sums, 1e-16, float(heads), ALU.add, ALU.mult))
                    link(dve.reciprocal(sums, sums))
                    link(dve.tensor_tensor(out, out, sums, ALU.mult))

            @block.scalar
            def _(act):
                act.wait_ge(ready, 1)
                act.activation(out, logits, ACT.Exp).then_inc(done, 1)

            @block.tensor
            def _(pe):
                for n in range(2):
                    spread_ends(pe, keep, heads, mem[1], mem[5], mem[6], mem[7], 2 * heads * (n + 1))


def gatv2_edges(nc, keep, e, w, x, agg):
    with ExitStack() as stack:
        g = gatv2_weights(nc, keep, stack, w)
        xt = stack.enter_context(nc.sbuf_tensor("xt_kept", [P, J * P], F32))
        logits = stack.enter_context(nc.sbuf_tensor("logits", [P, HEADS, J], F32))
        alpha = stack.enter_context(nc.sbuf_tensor("alpha", [P, HEADS, J], F32))
        gatv2_logits(nc, keep, e, g, x, xt, logits)
        softmax(nc, keep, e, HEADS, logits[:, :, :], alpha[:, :, :], "sm2")
        edge_sum(nc, keep, "e2", e, agg, PrepareGatv2(keep, xt, g.wl, g.bl_parts, alpha))


def gat_edges(nc, keep, name, e, h, agg):
    with ExitStack() as stack:
        def sb(n, shape):
            return stack.enter_context(nc.sbuf_tensor(f"{name}_{n}", shape, F32))

        rows, a_dst = sb("rows", [P, J, ROW]), sb("a_dst", [P, J, GAT_HEADS])
        logits, weight = sb("logits", [P, GAT_HEADS, J]), sb("weight", [P, GAT_HEADS, J])
        tail = sb("tail", [P, 2 * GAT_HEADS, J])
        pairs = h.rearrange("n (a b) -> (n a) b", b=GAT_HEADS)
        with Phase(nc, name + "g", freed="kept") as ph:
            got, got_a = ph.sb("got", [P, SLOTS, GC, ROW]), ph.sb("got_a", [P, SLOTS, GC, GAT_HEADS])
            a_row = ph.sb("a_row", [P, J], I32)
            get_s = ph.sb("get_s", [P, SLOTS, 2, GC], I32)
            gathered, kept = slot_sems(ph, "gathered", SLOTS), slot_sems(ph, "kept", SLOTS)
            rows_known, staged, go = ph.sem("rows_known"), ph.sem("staged"), ph.sem("go")
            with nc.Block() as block:
                @block.scalar
                def _(act):
                    ph.free_slots(act)

                @block.vector
                def _(dve):
                    dve.tensor_scalar(a_row[:, :], e.key_i[:, :], ROW // GAT_HEADS, ROW // GAT_HEADS - 1, ALU.mult, ALU.add)\
                        .then_inc(rows_known, 1)
                    with dve.Fori(0, TURNS) as turn:
                        for s in range(SLOTS):
                            dve.wait_ge(gathered[s], turn * (32 * GC) + 32 * GC)
                            cols = bass.ds(turn * TURN + s * GC, GC)
                            dve.tensor_copy(rows[:, cols, :], got[:, s]).then_inc(kept[s], 1)
                            dve.tensor_copy(a_dst[:, cols, :], got_a[:, s]).then_inc(kept[s], 1)

                @block.gpsimd
                def _(pool):
                    pool.wait_ge(rows_known, 1)
                    with pool.Fori(0, TURNS) as turn:
                        for s in range(SLOTS):
                            free(pool, kept, turn, s, 2)
                            cols = bass.ds(turn * TURN + s * GC, GC)
                            pool.sem_inc(go, 1)
                            pool.tensor_copy(get_s[:, s, 0, :], e.other_i[:, cols]).then_inc(staged, 1)
                            pool.tensor_copy(get_s[:, s, 1, :], a_row[:, cols]).then_inc(staged, 1)
                            pool.wait_ge(staged, turn * (2 * SLOTS) + 2 * s + 2)
                            pool.sem_inc(go, 1)
                            for k in range(GC):
                                for table, to, i in ((h, got, 0), (pairs, got_a, 1)):
                                    pool.indirect_dma_start(out=to[:, s, k, :], out_offset=None, in_=table,
                                                            in_offset=bass.IndirectOffsetOnAxis(ap=get_s[:, s, i, k:k + 1], axis=0))\
                                        .then_inc(gathered[s], 16)

        def make_logits(dve, link):
            link(dve.tensor_tensor(logits[:, :, :], rows[:, :, D:D + GAT_HEADS].rearrange("p j h -> p h j"),
                                   a_dst[:, :, :].rearrange("p j h -> p h j"), ALU.add))
            link(dve.scalar_tensor_tensor(logits[:, :, :], logits[:, :, :], SLOPE, logits[:, :, :], ALU.mult, ALU.max))

        softmax(nc, keep, e, GAT_HEADS, logits[:, :, :], weight[:, :, :], name + "s", make_logits,
                tail[:, 0:GAT_HEADS, :], tail[:, GAT_HEADS:, :])
        edge_sum(nc, keep, name + "m", e, agg, PrepareAttention(rows, weight, tail))


def wide(v):
    return v.unsqueeze(1).broadcast_to([P, GB, D])


def attention_weights(dve, link, out, w, att_src, att_dst, tmp):
    link(dve.tensor_copy(out[:, 0:D], w))
    for i, att in enumerate((att_src, att_dst)):
        link(dve.tensor_tensor(tmp, w, att, ALU.mult))
        link(dve.tensor_reduce(out[:, D + GAT_HEADS * i:D + GAT_HEADS * (i + 1)],
                               tmp.rearrange("p (h c) -> p h c", h=GAT_HEADS), AX.X, ALU.add))


def node_gatv2(nc, keep, x2, agg, w, gat, x3, h3):
    with Phase(nc, "n2", freed="f_ready h_out h_ready y_ready turned3 x3_out turned1 x3_ready scaled2 sums1") as ph:
        names = ("conv_bias", "g1", "beta1", "b2", "g2", "beta2")
        vec = {n: ph.sb(n, [P, D]) for n in names}
        w1, b1, w2 = ph.sb("w1", [P, 2, D]), ph.sb("b1", [P, 2]), ph.sb("w2", [P, 2, D])
        w1g, b1g, column = ph.sb("w1g", [P, 2, D]), ph.sb("b1g", [P, 2]), ph.sb("column", [P, 2])
        wh, att, waug, tmp = ph.sb("wh", [P, D]), ph.sb("att", [P, 2, D]), ph.sb("waug", [P, ROW]), ph.sb("tmp", [P, D])
        xs, ag = ph.sb("xs", [P, SLOT, GB, D]), ph.sb("ag", [P, SLOT, GB, D])
        r1, r2, x3s = ph.sb("r1", [P, SLOT, GB, D]), ph.sb("r2", [P, SLOT, GB, D]), ph.sb("x3s", [P, SLOT, GB, D])
        xt1, xt3, gt = ph.sb("xt1", [P, SLOT, GB, P]), ph.sb("xt3", [P, SLOT, GB, P]), ph.sb("gt", [P, SLOT, 2, GB, P])
        ho = ph.sb("ho", [P, SLOT, GB, ROW])
        shift = [ph.sb(f"shift{i}", [P, SLOT, GB]) for i in range(3)]
        stats = [ph.sb(f"stats{i}", [P, SLOT, GB, 6]) for i in range(3)]
        mv, rstd = [ph.sb(f"mv{i}", [P, SLOT, GB, 2]) for i in range(3)], [ph.sb(f"rstd{i}", [P, SLOT, GB]) for i in range(3)]
        t1_ps, t3_ps, y_ps = (ph.ps(n, [P, GB, P]) for n in ("t1_ps", "t3_ps", "y_ps"))
        f_ps, h_ps = [ph.ps(f"f_ps{j}", [P, GB, P]) for j in range(2)], [ph.ps(f"h_ps{j}", [P, 2, ROW]) for j in range(2)]
        bias_part, bias_parts = [ph.sb(f"bias_part{i}", [1, D], BF16) for i in range(3)], ph.sb("bias_parts", [3, GB, D], BF16)
        parts_split, parts_in = ph.sem("parts_split"), ph.sem("parts_in")
        weights, chain, w_ready, folded = ph.sem("weights"), ph.sem("chain"), ph.sem("w_ready"), ph.sem("folded")
        x_in, ag_in, x3_out, h_out = (slot_sems(ph, n) for n in ("x_in", "ag_in", "x3_out", "h_out"))
        x_added = slot_sems(ph, "x_added")
        scaled2a = ph.sem("scaled2a")
        added, sums1, rstd1, normed1, scaled1 = (slot_sems(ph, n) for n in ("added", "sums1", "rstd1", "normed1", "scaled1"))
        turned1, moved1, f_ready, gelued, y_ready = (slot_sems(ph, n) for n in ("turned1", "moved1", "f_ready", "gelued", "y_ready"))
        sums2, rstd2, scaled2 = (slot_sems(ph, n) for n in ("sums2", "rstd2", "scaled2"))
        sums3, rstd3, x3_ready = (slot_sems(ph, n) for n in ("sums3", "rstd3", "x3_ready"))
        turned3, moved3, h_ready, h_kept = (slot_sems(ph, n) for n in ("turned3", "moved3", "h_ready", "h_kept"))
        pool_steps = [ph.sem(f"pool_steps{i}") for i in range(3)]
        summed, taken, go = [ph.sem(f"summed{i}") for i in range(2)], [ph.sem(f"taken{i}") for i in range(3)], ph.sem("go")
        n_weights = 16 * (len(names) + 8)
        with nc.Block() as block, nc.allow_non_contiguous_dma(reason="the FFN's first bias, a column for each half"):
            @block.sync
            def _(sp):
                for n in names:
                    sp.dma_start(vec[n][:, :], w[n].partition_broadcast(P)).then_inc(weights, 16)
                sp.dma_start(w1[:, :, :], w["W1"].rearrange("d (j f) -> d j f", j=2)).then_inc(weights, 16)
                sp.dma_start(w2[:, :, :], w["W2"].rearrange("(j f) d -> f j d", j=2)).then_inc(weights, 16)
                sp.dma_start(b1[:, :], w["b1"].rearrange("(j f) -> f j", j=2)).then_inc(weights, 16)
                sp.dma_start(wh[:, :], gat["W"]).then_inc(weights, 16)
                for i, n in enumerate(("g1", "beta1")):
                    sp.dma_start(column[:, i:i + 1], w[n].unsqueeze(1)).then_inc(weights, 16)
                for i, n in enumerate(("att_src", "att_dst")):
                    sp.dma_start(att[:, i, :], gat[n].rearrange("h c -> (h c)").partition_broadcast(P)).then_inc(weights, 16)
                sp.wait_ge(parts_split, 1)
                for i in range(3):
                    for g in range(GB):
                        sp.dma_start(bias_parts[i:i + 1, g, :], bias_part[i][:, :]).then_inc(parts_in, 16)
                with sp.Fori(0, NTURN) as turn:
                    used = sp.snap(turn + 1)
                    for s in range(SLOT):
                        sp.wait_ge(scaled2[s], used)
                        sp.wait_ge(sums1[s], used)
                        sp.dma_start(xs[:, s], block_rows(x2, turn, s)).then_inc(x_in[s], 16)
                        sp.dma_start(ag[:, s], block_rows(agg, turn, s)[:, :, 0:D]).then_inc(ag_in[s], 16)

            @block.gpsimd
            def _(pool):
                pool.wait_ge(w_ready, 1)

                def add(turn, s):
                    done(pool, x_in, turn, s, 16)
                    free(pool, turned1, turn, s)
                    pool.tensor_tensor(r1[:, s], xs[:, s], wide(vec["conv_bias"][:, :]), ALU.add).then_inc(added[s], 1)

                def add_beta(turn, s):
                    done(pool, added, turn, s)
                    pool.tensor_tensor(xs[:, s], xs[:, s], wide(vec["beta2"][:, :]), ALU.add).then_inc(x_added[s], 1)

                def deviation(i, sums, out):
                    def fn(turn, s):
                        done(pool, sums, turn, s)
                        if i == 1:
                            norm_scale(pool, keep, Steps(pool, pool_steps[i], turn * SLOT + s, 1), mv[i][:, s],
                                       rstd[i][:, s, :], out[s])
                        else:
                            norm_shift(pool, keep, Steps(pool, pool_steps[i], turn * SLOT + s, SHIFT_STEPS), mv[i][:, s],
                                       rstd[i][:, s, :], shift[i][:, s, :], out[s])
                    return fn

                pipeline(pool, (1, deviation(0, sums1, rstd1)), (3, deviation(2, sums3, rstd3)), (0, add),
                         (2, deviation(1, sums2, rstd2)), (0, add_beta))

            @block.vector
            def _(dve):
                link = linked(dve, chain)
                dve.wait_ge(weights, n_weights)
                attention_weights(dve, link, waug[:, :], wh[:, :], att[:, 0, :], att[:, 1, :], tmp[:, :])
                link(dve.tensor_scalar(w1g[:, :, :], w1[:, :, :], column[:, 0:1], None, ALU.mult))
                link(dve.tensor_tensor(vec["beta1"][:, :], vec["beta1"][:, :], vec["b2"][:, :], ALU.add))
                split_bf16(dve, link, vec["beta1"][0:1, :], tmp[0:1, :], [p[:, :] for p in bias_part])
                dve.sem_inc(parts_split, 1)
                dve.wait_ge(folded, 1)
                link(dve.tensor_tensor(b1g[:, :], y_ps[:, 0, 0:2], b1[:, :], ALU.add))
                dve.sem_inc(w_ready, 1)

                def count(sem, ins):
                    ins.then_inc(sem, 1)

                def wait(sem, turn, s):
                    dve.wait_ge(sem, turn * SLOT + s + 1)

                def first_add(turn, s):
                    done(dve, added, turn, s)
                    done(dve, ag_in, turn, s, 16)
                    count(summed[0], dve.tensor_tensor(r1[:, s], r1[:, s], ag[:, s], ALU.add))

                def second_add(turn, s):
                    done(dve, y_ready, turn, s)
                    done(dve, scaled1, turn, s)
                    count(summed[1], dve.tensor_tensor(r2[:, s], r2[:, s], y_ps[:, :, :], ALU.add))

                def statistics(i, r):
                    def fn(turn, s):
                        if i == 2:
                            done(dve, scaled2, turn, s)
                        else:
                            wait(summed[i], turn, s)
                        for g in range(GB):
                            ins = dve.bn_stats(stats[i][:, s, g, :], r[:, s, g, :])
                        count(taken[i], ins)
                    return fn

                def together(i, out):
                    def fn(turn, s):
                        wait(taken[i], turn, s)
                        dve.sem_inc(go, 1)
                        for g in range(GB):
                            ins = dve.bn_aggr(mv[i][:, s, g, :], stats[i][:, s, g, :])
                        ins.then_inc(out[s], 1)
                    return fn

                def scale1(turn, s):
                    done(dve, normed1, turn, s)
                    free(dve, x3_ready, turn, s)
                    dve.tensor_tensor(r2[:, s], r1[:, s], wide(vec["g1"][:, :]), ALU.mult).then_inc(scaled1[s], 1)

                def second_norm(turn, s):
                    done(dve, sums2, turn, s)
                    for g in range(GB):
                        ins = dve.scalar_tensor_tensor(r2[:, s, g, :], r2[:, s, g, :], mv[1][:, s, g, 0:1], vec["g2"][:, :],
                                                       ALU.subtract, ALU.mult)
                    count(scaled2a, ins)

                def second_residual(turn, s):
                    done(dve, rstd2, turn, s)
                    done(dve, x_added, turn, s)
                    wait(scaled2a, turn, s)
                    for g in range(GB):
                        ins = dve.scalar_tensor_tensor(r2[:, s, g, :], r2[:, s, g, :], rstd[1][:, s, g:g + 1], xs[:, s, g, :],
                                                       ALU.mult, ALU.add)
                    ins.then_inc(scaled2[s], 1)

                pipeline(dve, (3, statistics(2, r2)), (2, second_add), (3, together(2, sums3)), (1, scale1),
                         (2, statistics(1, r2)), (0, first_add), (2, together(1, sums2)), (0, statistics(0, r1)),
                         (2, second_norm), (0, together(0, sums1)), (2, second_residual))

            @block.tensor
            def _(pe):
                pe.wait_ge(weights, n_weights)
                for j in range(2):
                    ins = pe.matmul(y_ps[:, 0, j:j + 1], w1[:, j, :], column[:, 1:2], start=True, stop=True)
                ins.then_inc(folded, 1)
                pe.wait_ge(w_ready, 1)
                pe.wait_ge(parts_in, 16 * 3 * GB)

                def ffn2(turn, s):
                    done(pe, gelued, turn, s, 2)
                    bank_free(pe, sums2, turn, s)
                    pe.matmul(y_ps[:, :, :], keep.ones_b[0:3, :], bias_parts[:, :, :], start=True, stop=False, skip_group_check=True)
                    for g in range(GB):
                        for j in range(2):
                            ins = pe.matmul(y_ps[:, g, :], gt[:, s, j, g, :], w2[:, j, :], start=False,
                                            stop=(g, j) == (GB - 1, 1), skip_group_check=True)
                    ins.then_inc(y_ready[s], 1)

                def turn3(turn, s):
                    done(pe, x3_ready, turn, s)
                    bank_free(pe, moved3, turn, s)
                    for g in range(GB):
                        ins = pe.transpose(t3_ps[:, g, :], x3s[:, s, g, :], keep.ident[:, :])
                    ins.then_inc(turned3[s], 1)

                def product3(turn, s):
                    done(pe, moved3, turn, s)
                    bank_free(pe, h_kept, turn, s, 2)
                    for g in range(GB):
                        ins = pe.matmul(h_ps[g // 2][:, g % 2, :], xt3[:, s, g, :], waug[:, :], start=True, stop=True)
                    ins.then_inc(h_ready[s], 1)

                def turn1(turn, s):
                    done(pe, normed1, turn, s)
                    bank_free(pe, moved1, turn, s)
                    for g in range(GB):
                        ins = pe.transpose(t1_ps[:, g, :], r1[:, s, g, :], keep.ident[:, :])
                    ins.then_inc(turned1[s], 1)

                def ffn1(turn, s):
                    done(pe, moved1, turn, s)
                    bank_free(pe, gelued, turn, s, 2)
                    for j in range(2):
                        ins = pe.matmul(f_ps[j][:, :, :], w1g[:, j, :], xt1[:, s], start=True, stop=True)
                    ins.then_inc(f_ready[s], 1)

                pipeline(pe, (2, ffn2), (4, turn3), (1, turn1), (4, product3), (1, ffn1))

            @block.scalar
            def _(act):
                ph.free_slots(act)
                def store_h(turn, s):
                    done(act, h_kept, turn, s, 2)
                    act.dma_start(block_rows(h3, turn, s), ho[:, s]).then_inc(h_out[s], 16)

                def store_x3(turn, s):
                    done(act, x3_ready, turn, s)
                    act.dma_start(block_rows(x3, turn, s), x3s[:, s]).then_inc(x3_out[s], 16)

                def first_norm(turn, s):
                    done(act, rstd1, turn, s)
                    norm_act(act, r1[:, s], rstd[0][:, s], shift[0][:, s], r1[:, s]).then_inc(normed1[s], 1)

                def third_norm(turn, s):
                    done(act, rstd3, turn, s)
                    free(act, x3_out, turn, s, 16)
                    free(act, turned3, turn, s)
                    norm_act(act, r2[:, s], rstd[2][:, s], shift[2][:, s], x3s[:, s]).then_inc(x3_ready[s], 1)

                def move3(turn, s):
                    done(act, turned3, turn, s)
                    free(act, h_ready, turn, s)
                    act.activation(xt3[:, s], t3_ps[:, :, :], ACT.Copy).then_inc(moved3[s], 1)

                def keep_h(turn, s):
                    done(act, h_ready, turn, s)
                    free(act, h_out, turn, s, 16)
                    for j in range(2):
                        act.activation(ho[:, s, 2 * j:2 * j + 2, :], h_ps[j][:, :, :], ACT.Copy).then_inc(h_kept[s], 1)

                def move1(turn, s):
                    done(act, turned1, turn, s)
                    free(act, f_ready, turn, s)
                    act.activation(xt1[:, s], t1_ps[:, :, :], ACT.Copy).then_inc(moved1[s], 1)

                def gelu(turn, s):
                    done(act, f_ready, turn, s)
                    free(act, y_ready, turn, s)
                    for j in range(2):
                        act.activation(gt[:, s, j], f_ps[j][:, :, :], ACT.Gelu, bias=b1g[:, j:j + 1]).then_inc(gelued[s], 1)

                pipeline(act, (5, store_h), (1, first_norm), (4, move3), (1, move1), (3, third_norm), (3, store_x3), (1, gelu),
                         (4, keep_h))
                for s in range(SLOT):
                    done(act, x3_out, NTURN - 1, s, 16)
                    done(act, h_out, NTURN - 1, s, 16)


class Attend:
    FIRST_STEPS, LAST_STEPS = 6, 3

    def __init__(self, ph, hs, ag):
        self.hs, self.ag = hs, ag
        self.own, self.top = ph.sb("own", [P, SLOT, GB, GAT_HEADS]), ph.sb("top", [P, SLOT, GB, GAT_HEADS])
        self.most = ph.sb("most", [P, SLOT, GB, GAT_HEADS])
        self.less, self.exps = ph.sb("less", [P, SLOT, 2, GB, GAT_HEADS]), ph.sb("exps", [P, SLOT, 2, GB, GAT_HEADS])
        self.total, self.share = ph.sb("total", [P, SLOT, GB, GAT_HEADS]), ph.sb("share", [P, SLOT, 2, GB, GAT_HEADS])
        self.u = ph.sb("u", [P, SLOT, 2, GB, D])
        self.steps = [ph.sem(f"attend_steps{i}") for i in range(3)]
        self.h_in, self.ag_in = slot_sems(ph, "h_in"), slot_sems(ph, "ag_in")
        self.less_ready, self.exps_ready, self.share_ready = (slot_sems(ph, n) for n in ("less_ready", "exps_ready", "share_ready"))
        self.u_ready = slot_sems(ph, "u_ready")

    def load(self, sp, turn, s, used, h, agg):
        sp.wait_ge(self.u_ready[s], used)
        sp.dma_start(self.hs[:, s], block_rows(h, turn, s)).then_inc(self.h_in[s], 16)
        sp.dma_start(self.ag[:, s], block_rows(agg, turn, s)).then_inc(self.ag_in[s], 16)

    def first(self, dve, turn, s):
        a, h = self, GAT_HEADS
        st = Steps(dve, a.steps[0], turn * SLOT + s, a.FIRST_STEPS)
        done(dve, a.h_in, turn, s, 16)
        done(dve, a.ag_in, turn, s, 16)
        free(dve, a.exps_ready, turn, s)
        st(dve.tensor_tensor(a.own[:, s], a.hs[:, s, :, D:D + h], a.hs[:, s, :, D + h:ROW], ALU.add))
        st(dve.tensor_scalar(a.top[:, s], a.ag[:, s, :, D + h:ROW], 0.0, -BIG, ALU.is_equal, ALU.mult))
        st.wait()
        st(dve.scalar_tensor_tensor(a.own[:, s], a.own[:, s], SLOPE, a.own[:, s], ALU.mult, ALU.max))
        st(dve.tensor_tensor(a.top[:, s], a.top[:, s], a.ag[:, s, :, D:D + h], ALU.add))
        st.wait()
        st(dve.tensor_tensor(a.most[:, s], a.top[:, s], a.own[:, s], ALU.max))
        st.wait()
        st(dve.tensor_tensor(a.less[:, s, 0], a.top[:, s], a.most[:, s], ALU.subtract))
        dve.tensor_tensor(a.less[:, s, 1], a.own[:, s], a.most[:, s], ALU.subtract).then_inc(a.less_ready[s], 1)

    def exp(self, act, turn, s):
        done(act, self.less_ready, turn, s)
        free(act, self.share_ready, turn, s)
        act.activation(self.exps[:, s], self.less[:, s], ACT.Exp).then_inc(self.exps_ready[s], 1)

    def last(self, dve, turn, s):
        a = self
        st = Steps(dve, a.steps[1], turn * SLOT + s, a.LAST_STEPS)
        done(dve, a.exps_ready, turn, s)
        st(dve.tensor_tensor(a.total[:, s], a.ag[:, s, :, D + GAT_HEADS:ROW], a.exps[:, s, 0], ALU.mult))
        st.wait()
        st(dve.scalar_tensor_tensor(a.total[:, s], a.total[:, s], 1e-16, a.exps[:, s, 1], ALU.add, ALU.add))
        st.wait()
        free(dve, a.u_ready, turn, s)
        st(dve.reciprocal(a.total[:, s], a.total[:, s]))
        st.wait()
        dve.tensor_tensor(a.share[:, s], a.exps[:, s], a.total[:, s].unsqueeze(1).broadcast_to([P, 2, GB, GAT_HEADS]),
                          ALU.mult).then_inc(a.share_ready[s], 1)

    def weigh(self, engine, turn, s, which):
        a = self
        done(engine, a.share_ready, turn, s)
        rows = (a.ag, a.hs)[which]
        return engine.tensor_tensor(a.u[:, s, which].rearrange("p g (h c) -> p g h c", h=GAT_HEADS),
                                    rows[:, s, :, 0:D].rearrange("p g (h c) -> p g h c", h=GAT_HEADS),
                                    a.share[:, s, which].unsqueeze(3).broadcast_to([P, GB, GAT_HEADS, GAT_D]), ALU.mult)


def node_gat(nc, keep, x3, h3, agg, one, two, s2, h2):
    with Phase(nc, "n3", freed="h_out product_ready r_ready share_ready exps_ready u_ready s_out turned added") as ph:
        wsk1, wsk2, wh, att = ph.sb("wsk1", [P, D]), ph.sb("wsk2", [P, D]), ph.sb("wh", [P, D]), ph.sb("att", [P, 2, D])
        waug, tmp, b1, b2 = ph.sb("waug", [P, ROW]), ph.sb("tmp", [P, D]), ph.sb("b1", [P, 2]), ph.sb("b2", [P, 2, D])
        bias1, bias2 = ph.sb("bias1", [P, 1]), ph.sb("bias2", [P, D])
        xs, xb, xt, ht = (ph.sb(n, [P, SLOT, GB, D]) for n in ("xs", "xb", "xt", "ht"))
        hs, ag, ho = (ph.sb(n, [P, SLOT, GB, ROW]) for n in ("hs", "ag", "ho"))
        a = Attend(ph, hs, ag)
        t_ps, r_ps, s_ps = (ph.ps(n, [P, GB, P]) for n in ("t_ps", "r_ps", "s_ps"))
        h_ps = [ph.ps(f"h_ps{j}", [P, 2, ROW]) for j in range(2)]
        weights, chain, w_ready = ph.sem("weights"), ph.sem("chain"), ph.sem("w_ready")
        x_in, added, turned, moved, r_ready, relued = (slot_sems(ph, n) for n in ("x_in", "added", "turned", "moved", "r_ready", "relued"))
        weighed = slot_sems(ph, "weighed")
        product_ready, s_ready, h_kept, s_out, h_out = (slot_sems(ph, n) for n in ("product_ready", "s_ready", "h_kept", "s_out", "h_out"))
        n_weights = 16 * 9
        with nc.Block() as block, nc.allow_non_contiguous_dma(reason="two biases, a float on each partition"):
            @block.sync
            def _(sp):
                for to, of in ((wsk1, one["Wsk"]), (wsk2, two["Wsk"]), (wh, two["W"])):
                    sp.dma_start(to[:, :], of).then_inc(weights, 16)
                for i, n in enumerate(("att_src", "att_dst")):
                    sp.dma_start(att[:, i, :], two[n].rearrange("h c -> (h c)").partition_broadcast(P)).then_inc(weights, 16)
                for i, n in enumerate(("b", "bsk")):
                    sp.dma_start(b1[:, i:i + 1], one[n].unsqueeze(1)).then_inc(weights, 16)
                    sp.dma_start(b2[:, i, :], two[n].partition_broadcast(P)).then_inc(weights, 16)
                with sp.Fori(0, NTURN) as turn:
                    used = sp.snap(turn + 1)
                    for s in range(SLOT):
                        sp.wait_ge(turned[s], used)
                        sp.wait_ge(added[s], used)
                        sp.dma_start(xs[:, s], block_rows(x3, turn, s)).then_inc(x_in[s], 16)
                        a.load(sp, turn, s, used, h3, agg)

            @block.gpsimd
            def _(pool):
                pool.wait_ge(w_ready, 1)

                def add(turn, s):
                    done(pool, x_in, turn, s, 16)
                    free(pool, s_out, turn, s, 16)
                    pool.tensor_tensor(xb[:, s], xs[:, s], wide(bias2[:, :]), ALU.add).then_inc(added[s], 1)

                def combine(turn, s):
                    done(pool, weighed, turn, s, 2)
                    pool.tensor_tensor(a.u[:, s, 0], a.u[:, s, 0], a.u[:, s, 1], ALU.add).then_inc(a.u_ready[s], 1)

                pipeline(pool, (1, combine), (0, add))

            @block.vector
            def _(dve):
                link = linked(dve, chain)
                dve.wait_ge(weights, n_weights)
                attention_weights(dve, link, waug[:, :], wh[:, :], att[:, 0, :], att[:, 1, :], tmp[:, :])
                link(dve.tensor_tensor(bias1[:, :], b1[:, 0:1], b1[:, 1:2], ALU.add))
                link(dve.tensor_tensor(bias2[:, :], b2[:, 0, :], b2[:, 1, :], ALU.add))
                dve.sem_inc(w_ready, 1)

                def total(turn, s):
                    done(dve, product_ready, turn, s)
                    done(dve, added, turn, s)
                    dve.tensor_tensor(xb[:, s], xb[:, s], s_ps[:, :, :], ALU.add).then_inc(s_ready[s], 1)

                def weigh(turn, s):
                    a.last(dve, turn, s)
                    free(dve, r_ready, turn, s)
                    for i in range(2):
                        a.weigh(dve, turn, s, i).then_inc(weighed[s], 1)

                pipeline(dve, (0, lambda turn, s: a.first(dve, turn, s)), (1, weigh), (3, total))

            @block.tensor
            def _(pe):
                pe.wait_ge(w_ready, 1)

                def turn_over(turn, s):
                    done(pe, x_in, turn, s, 16)
                    bank_free(pe, moved, turn, s)
                    for g in range(GB):
                        ins = pe.transpose(t_ps[:, g, :], xs[:, s, g, :], keep.ident[:, :])
                    ins.then_inc(turned[s], 1)

                def residual(turn, s):
                    done(pe, moved, turn, s)
                    done(pe, a.u_ready, turn, s)
                    bank_free(pe, relued, turn, s)
                    pe.matmul(r_ps[:, :, :], wsk1[:, :], xt[:, s], start=True, stop=False, skip_group_check=True)
                    for g in range(GB):
                        ins = pe.matmul(r_ps[:, g, :], a.u[:, s, 0, g, :], keep.ident[:, :], start=False, stop=g == GB - 1,
                                        skip_group_check=True)
                    ins.then_inc(r_ready[s], 1)

                def product(turn, s):
                    done(pe, relued, turn, s)
                    bank_free(pe, s_ready, turn, s)
                    bank_free(pe, h_kept, turn, s, 2)
                    for g in range(GB):
                        pe.matmul(s_ps[:, g, :], ht[:, s, g, :], wsk2[:, :], start=True, stop=True)
                    for g in range(GB):
                        ins = pe.matmul(h_ps[g // 2][:, g % 2, :], ht[:, s, g, :], waug[:, :], start=True, stop=True)
                    ins.then_inc(product_ready[s], 1)

                pipeline(pe, (3, product), (2, residual), (0, turn_over))

            @block.scalar
            def _(act):
                ph.free_slots(act)
                act.wait_ge(w_ready, 1)

                def store(turn, s):
                    done(act, s_ready, turn, s)
                    act.dma_start(block_rows(s2, turn, s), xb[:, s]).then_inc(s_out[s], 16)
                    done(act, h_kept, turn, s, 2)
                    act.dma_start(block_rows(h2, turn, s), ho[:, s]).then_inc(h_out[s], 16)

                def keep_h(turn, s):
                    done(act, product_ready, turn, s)
                    free(act, h_out, turn, s, 16)
                    for j in range(2):
                        act.activation(ho[:, s, 2 * j:2 * j + 2, :], h_ps[j][:, :, :], ACT.Copy).then_inc(h_kept[s], 1)

                def move(turn, s):
                    done(act, turned, turn, s)
                    free(act, r_ready, turn, s)
                    act.activation(xt[:, s], t_ps[:, :, :], ACT.Copy).then_inc(moved[s], 1)

                def relu(turn, s):
                    done(act, r_ready, turn, s)
                    free(act, product_ready, turn, s)
                    act.activation(ht[:, s], r_ps[:, :, :], ACT.Relu, bias=bias1[:, 0:1]).then_inc(relued[s], 1)

                pipeline(act, (4, store), (0, lambda turn, s: a.exp(act, turn, s)), (3, keep_h), (2, relu), (0, move))
                for s in range(SLOT):
                    done(act, s_out, NTURN - 1, s, 16)
                    done(act, h_out, NTURN - 1, s, 16)


def node_last(nc, keep, s2, h2, agg, out):
    with Phase(nc, "n4", freed="weighed stored share_ready exps_ready u_ready out_ready sums_ready") as ph:
        ss, os, r = (ph.sb(n, [P, SLOT, GB, D]) for n in ("ss", "os", "r"))
        hs, ag = (ph.sb(n, [P, SLOT, GB, ROW]) for n in ("hs", "ag"))
        a = Attend(ph, hs, ag)
        stats, mv, rstd = ph.sb("stats", [P, SLOT, GB, 6]), ph.sb("mv", [P, SLOT, GB, 2]), ph.sb("rstd", [P, SLOT, GB])
        s_in, sums_ready, rstd_ready, out_ready, stored = (slot_sems(ph, n) for n in ("s_in", "sums_ready", "rstd_ready", "out_ready", "stored"))
        shift, own_steps, weighed = ph.sb("shift", [P, SLOT, GB]), ph.sem("own_steps"), slot_sems(ph, "weighed")
        dve_steps, pool_steps = ph.sem("dve_steps"), ph.sem("pool_steps")
        with nc.Block() as block:
            @block.sync
            def _(sp):
                with sp.Fori(0, NTURN) as turn:
                    used = sp.snap(turn + 1)
                    for s in range(SLOT):
                        sp.wait_ge(weighed[s], used)
                        a.load(sp, turn, s, used, h2, agg)
                        sp.dma_start(ss[:, s], block_rows(s2, turn, s)).then_inc(s_in[s], 16)

            @block.gpsimd
            def _(pool):
                def deviation(turn, s):
                    done(pool, sums_ready, turn, s)
                    norm_shift(pool, keep, Steps(pool, pool_steps, turn * SLOT + s, SHIFT_STEPS), mv[:, s], rstd[:, s, :],
                               shift[:, s, :], rstd_ready[s])

                def own(turn, s):
                    free(pool, sums_ready, turn, s)
                    st = Steps(pool, own_steps, turn * SLOT + s, 1)
                    st(a.weigh(pool, turn, s, 1))
                    st.wait()
                    done(pool, s_in, turn, s, 16)
                    pool.tensor_tensor(a.u[:, s, 1], ss[:, s], a.u[:, s, 1], ALU.add).then_inc(a.u_ready[s], 1)

                pipeline(pool, (3, deviation), (1, own))

            @block.vector
            def _(dve):
                def sums(turn, s):
                    done(dve, a.u_ready, turn, s)
                    done(dve, weighed, turn, s)
                    st = Steps(dve, dve_steps, turn * SLOT + s, NORM_STEPS + 1)
                    free(dve, out_ready, turn, s)
                    st(dve.tensor_tensor(r[:, s], a.u[:, s, 1], a.u[:, s, 0], ALU.add))
                    st.wait()
                    norm_sums(dve, st, r[:, s], stats[:, s], mv[:, s], sums_ready[s])

                def weigh(turn, s):
                    a.last(dve, turn, s)
                    free(dve, sums_ready, turn, s)
                    a.weigh(dve, turn, s, 0).then_inc(weighed[s], 1)

                pipeline(dve, (0, lambda turn, s: a.first(dve, turn, s)), (1, weigh), (2, sums))

            @block.scalar
            def _(act):
                ph.free_slots(act)
                def store(turn, s):
                    done(act, out_ready, turn, s)
                    act.dma_start(block_rows(out, turn, s), os[:, s]).then_inc(stored[s], 16)

                def apply(turn, s):
                    done(act, rstd_ready, turn, s)
                    free(act, stored, turn, s, 16)
                    norm_act(act, r[:, s], rstd[:, s], shift[:, s], os[:, s]).then_inc(out_ready[s], 1)

                pipeline(act, (4, store), (3, apply), (0, lambda turn, s: a.exp(act, turn, s)))
                for s in range(SLOT):
                    done(act, stored, NTURN - 1, s, 16)


def find_descents(nc, keep, dst, descents):
    with Phase(nc, "fd") as ph:
        key, after_i = ph.sb("key", [P, J], I32), ph.sb("after_i", [P, 1], I32)
        flags, count = ph.sb("flags", [P, J]), ph.sb("count", [P, 1])
        total_ps = ph.ps("total_ps", [P, 1])
        loaded, chain, counted, summed, preset = (ph.sem(n) for n in ("loaded", "chain", "counted", "summed", "preset"))
        view = dst.rearrange("(p j) -> p j", p=P)
        with nc.Block() as block, nc.allow_non_contiguous_dma(reason="the first edge of each partition"):
            @block.sync
            def _(sp):
                sp.dma_start(key[:, :], view).then_inc(loaded, 16)
                sp.wait_ge(preset, 1)
                sp.dma_start(after_i[0:P - 1, :], view[1:P, 0:1]).then_inc(loaded, 16)

            @block.vector
            def _(dve):
                link = linked(dve, chain)
                dve.memset(after_i[:, :], NPAD).then_inc(preset, 1)
                dve.wait_ge(loaded, 32)
                dve.tensor_tensor(flags[:, 0:J - 1], key[:, 0:J - 1], key[:, 1:J], ALU.is_gt)
                link(dve.tensor_tensor(flags[:, J - 1:J], key[:, J - 1:J], after_i[:, :], ALU.is_gt))
                dve.tensor_reduce(count[:, :], flags[:, :], AX.X, ALU.add).then_inc(counted, 1)
                dve.wait_ge(summed, 1)
                link(dve.tensor_copy(descents[:, :], total_ps[:, :]))

            @block.tensor
            def _(pe):
                pe.wait_ge(counted, 1)
                pe.matmul(total_ps[:, :], keep.ones[:, :], count[:, :], start=True, stop=True).then_inc(summed, 1)


def lay_out_sorted(nc, src, dst, attr, target):
    with Phase(nc, "lo") as ph:
        pay = ph.sb("pay", [P, J, WD])
        loaded, stored = ph.sem("loaded"), ph.sem("stored")
        with nc.Block() as block:
            n_loads = load_edges(nc, src, dst, attr)(block, ph, pay, loaded)

            @block.scalar
            def _(act):
                act.wait_ge(loaded, n_loads)
                act.dma_start(target.rearrange("(p j) w -> p j w", p=P), pay[:, :, :]).then_inc(stored, 16)
                act.wait_ge(stored, 16)


def gnn(nc, x, src, dst, attr, sage, gcn, gat2, gat, out):
    def dram(name, shape):
        return nc.dram_tensor(name, shape, F32, kind="Internal").ap()

    by_dst, by_src = [dram(f"by_dst{i}", (EPAD, WD)) for i in range(2)], [dram(f"by_src{i}", (EPAD, WS)) for i in range(2)]
    agg_dst, agg_src = dram("agg_dst", (NPAD, ROW)), dram("agg_src", (NPAD, D))
    x1, z1, h3, h4 = (dram(n, (NPAD, ROW)) for n in ("x1", "z1", "h3", "h4"))
    x2, x3, s4 = (dram(n, (NPAD, D)) for n in ("x2", "x3", "s4"))
    with ExitStack() as stack:
        keep = Keep()
        constants(nc, keep, stack)
        descents = stack.enter_context(nc.sbuf_tensor("descents", [P, 1], I32))
        find_descents(nc, keep, dst, descents)
        unsorted = nc.values_load(descents[0:1, 0:1], min_val=0, max_val=EPAD)
        with nc.If(unsorted > 0):
            sort_pass(nc, keep, "d1", WD, LOW, False, load_edges(nc, src, dst, attr), by_dst[0])
            sort_pass(nc, keep, "d2", WD, HIGH, True, load_sorted(by_dst[0]), by_dst[1])
        with nc.Else():
            lay_out_sorted(nc, src, dst, attr, by_dst[1])
        sort_pass(nc, keep, "s1", WS, LOW, False, load_edges(nc, src, dst, None), by_src[0], [agg_dst, agg_src])
        sort_pass(nc, keep, "s2", WS, HIGH, True, load_sorted(by_src[0]), by_src[1])
        to_dst = edge_tables(nc, keep, "d", by_dst[1], WD, stack, True)
        with ExitStack() as src_stack:
            to_src = edge_tables(nc, keep, "s", by_src[1], WS, src_stack, False)
            degrees(nc, keep, to_dst)
            edge_sum(nc, keep, "e0", to_dst, agg_dst, PrepareMean(to_dst), x, D)
            node_sage(nc, keep, x, agg_dst, sage["W"], sage["b"], x1)
            edge_sum(nc, keep, "e1a", to_src, agg_src, PrepareNorm(), x1, ROW)
            node_gcn(nc, keep, "n1a", x1, agg_src, gcn["W1"], GCN_BETA[0], z1)
            edge_sum(nc, keep, "e1b", to_src, agg_src, PrepareNorm(), z1, ROW)
            node_gcn(nc, keep, "n1b", z1, agg_src, gcn["W2"], GCN_BETA[1], x2, x1)
        gatv2_edges(nc, keep, to_dst, gat2, x2, agg_dst)
        node_gatv2(nc, keep, x2, agg_dst, gat2, gat[0], x3, h3)
        gat_edges(nc, keep, "e3", to_dst, h3, agg_dst)
        node_gat(nc, keep, x3, h3, agg_dst, gat[0], gat[1], s4, h4)
        gat_edges(nc, keep, "e4", to_dst, h4, agg_dst)
        node_last(nc, keep, s4, h4, agg_dst, out)


def kernel(**inputs):
    import concourse.bacc as bacc
    from concourse.bass_utils import run_bass_kernel_spmd

    nc = bacc.Bacc("TRN2", target_bir_lowering=False, num_devices=1)
    arrays = {}

    def take(name, a):
        arrays[name] = np.ascontiguousarray(a)
        return nc.dram_tensor(name, arrays[name].shape, mybir.dt.from_np(arrays[name].dtype), kind="ExternalInput").ap()

    def padded(a, rows, fill):
        a = np.asarray(a)
        return np.concatenate([a, np.full((rows - a.shape[0],) + a.shape[1:], fill, a.dtype)])

    def layer(prefix, names, **more):
        w = {n: take(prefix + n, np.asarray(inputs[prefix + n])) for n in names}
        w.update({n: take(prefix + n, np.asarray(inputs[prefix + n]).T) for n in more.get("transposed", ())})
        return w

    x = take("x", padded(inputs["x"], NPAD, 0))
    src, dst = (take(n, padded(inputs[n], EPAD, NPAD - 1)) for n in ("src", "dst"))
    attr = take("edge_attr_16", padded(inputs["edge_attr_16"], EPAD, 0))
    sage = layer("L0_gnn_", ("W_neigh", "b_neigh"))
    gcn = layer("L1_gnn_", ("W1", "W2"))
    gat2 = layer("L2_gnn_", ("bl", "br", "att", "conv_bias", "g1", "beta1", "b1", "b2", "g2", "beta2"),
                 transposed=("Wl", "Wr", "We", "W1", "W2"))
    both = layer("L3_gnn_", [f"{n}{i}" for i in (1, 2) for n in ("W", "att_src", "att_dst", "b", "Wsk", "bsk")])
    gat = [{n: both[f"{n}{i}"] for n in ("W", "att_src", "att_dst", "b", "Wsk", "bsk")} for i in (1, 2)]
    out = nc.dram_tensor("out", (NPAD, D), F32, kind="ExternalOutput").ap()
    gnn(nc, x, src, dst, attr, {"W": sage["W_neigh"], "b": sage["b_neigh"]}, gcn, gat2, gat, out)
    r = run_bass_kernel_spmd(nc, [arrays], core_ids=[0])
    return r.results[0]["out"][:NODES]
```
